# Optimizing a Trainium2 kernel written in Bass

```python
import numpy as np
import jax
import jax.numpy as jnp

def _softmax(x, axis=-1):
    return jax.nn.softmax(x, axis=axis)

def _gelu(x):
    return jax.nn.gelu(x, approximate=True)

def _silu(x):
    return jax.nn.silu(x)

def _sigmoid(x):
    return jax.nn.sigmoid(x)

def _layernorm(x, axis=-1, eps=1e-05):
    m = jnp.mean(x, axis=axis, keepdims=True)
    v = jnp.var(x, axis=axis, keepdims=True)
    return (x - m) / jnp.sqrt(v + eps)

def _scatter_add(tgt, idx, src, axis=0):
    return tgt.at[idx].add(src)

def _segment_sum(src, seg, n):
    return jax.ops.segment_sum(src, seg, n)
kernel_name = 'mk_decoder_preln_d1_seqx_r8_3c7f6a'

def setup_inputs(seed: int=0):
    np.random.seed(seed)
    _w = jnp.asarray

    def _rec_inputs():
        import jax
        import jax.numpy as jnp
        _rk = jax.random.key(seed)
        x = -0.0002928 + 1 * jax.random.normal(jax.random.fold_in(_rk, 1), (64, 128, 128), jnp.float32)
        _lenS = 128 - jax.random.randint(jax.random.fold_in(_rk, 7), (64,), 0, max(1, 128 // 4) + 1, jnp.int32)
        _lenS2 = 77 - jax.random.randint(jax.random.fold_in(_rk, 8), (64,), 0, max(1, 77 // 4) + 1, jnp.int32)
        _ctx_1024P = jax.random.normal(jax.random.fold_in(_rk, 11), (64, 16, 128), jnp.float32)
        _ctx_1024c = jax.random.dirichlet(jax.random.fold_in(_rk, 511), 0.3 * jnp.ones((16,), jnp.float32), (64, 77))
        _ctx_1024t = jnp.einsum('bsk,bkd->bsd', _ctx_1024c, _ctx_1024P)
        _ctx_1024t = _ctx_1024t * jax.lax.rsqrt(jnp.mean(jnp.square(_ctx_1024t)) + 1e-12) * 0.953939
        ctx_1024 = -1.39393e-06 + 0.999914 * (_ctx_1024t + 0.3 * jax.random.normal(jax.random.fold_in(_rk, 611), (64, 77, 128), jnp.float32))
        return (x, ctx_1024)
    x, ctx_1024 = _rec_inputs()

    def _L0_attn_setup():
        import jax, jax.numpy as jnp
        import numpy as np
        NUM_HEADS = 16
        WINDOW = 128

        def apply_rope(x):
            S, Dh = (x.shape[-2], x.shape[-1])
            half = Dh // 2
            inv_freq = 1.0 / 10000.0 ** (jnp.arange(half, dtype=jnp.float32) / half)
            ang = jnp.arange(S, dtype=jnp.float32)[:, None] * inv_freq[None, :]
            cos, sin = (jnp.cos(ang), jnp.sin(ang))
            x1, x2 = (x[..., :half], x[..., half:])
            return jnp.concatenate([x1 * cos - x2 * sin, x1 * sin + x2 * cos], axis=-1).astype(x.dtype)
        key = jax.random.key(seed)
        ks = jax.random.split(key, 5)
        D = 128
        B, S = (2, 256)
        w = 0.02
        return {'x': jax.random.normal(ks[0], (B, S, D), dtype=jnp.float32), 'Wq': jax.random.normal(ks[1], (D, D), dtype=jnp.float32) * w, 'bq': jnp.zeros((D,), dtype=jnp.float32), 'Wk': jax.random.normal(ks[2], (D, D), dtype=jnp.float32) * w, 'bk': jnp.zeros((D,), dtype=jnp.float32), 'Wv': jax.random.normal(ks[3], (D, D), dtype=jnp.float32) * w, 'bv': jnp.zeros((D,), dtype=jnp.float32), 'Wo': jax.random.normal(ks[4], (D, D), dtype=jnp.float32) * w, 'bo': jnp.zeros((D,), dtype=jnp.float32)}
    _L0_attn_all = _L0_attn_setup()
    _L0_attn_in = {k: v for k, v in _L0_attn_all.items() if k in ('Wq', 'bq', 'Wk', 'bk', 'Wv', 'bv', 'Wo', 'bo')}
    del _L0_attn_all

    def _L0_xattn_setup():
        import jax, jax.numpy as jnp
        import numpy as np
        HIDDEN = 128
        NUM_HEADS = 16
        HEAD_DIM = HIDDEN // NUM_HEADS
        key = jax.random.key(seed)
        ks = jax.random.split(key, 10)
        B, T, S = (2, 256, 256)
        sc = 1.0 / np.sqrt(HIDDEN)
        inp = {'tgt': jax.random.normal(ks[0], (B, T, HIDDEN), jnp.float32), 'src': jax.random.normal(ks[1], (B, S, HIDDEN), jnp.float32), 'Wq': jax.random.normal(ks[2], (NUM_HEADS, HIDDEN, HEAD_DIM), jnp.float32) * sc, 'bq': jnp.zeros((NUM_HEADS, HEAD_DIM), jnp.float32), 'Wk': jax.random.normal(ks[3], (NUM_HEADS, HIDDEN, HEAD_DIM), jnp.float32) * sc, 'bk': jnp.zeros((NUM_HEADS, HEAD_DIM), jnp.float32), 'Wv': jax.random.normal(ks[4], (NUM_HEADS, HIDDEN, HEAD_DIM), jnp.float32) * sc, 'bv': jnp.zeros((NUM_HEADS, HEAD_DIM), jnp.float32), 'Wo': jax.random.normal(ks[5], (HIDDEN, HIDDEN), jnp.float32) * sc, 'bo': jnp.zeros((HIDDEN,), jnp.float32)}
        return inp
    _L0_xattn_all = _L0_xattn_setup()
    _L0_xattn_in = {k: v for k, v in _L0_xattn_all.items() if k in ('Wq', 'bq', 'Wk', 'bk', 'Wv', 'bv', 'Wo', 'bo')}
    del _L0_xattn_all

    def _L0_ffn_setup():
        import jax, jax.numpy as jnp
        import numpy as np
        ALPHA = 2.0
        TOP_K = 2
        key = jax.random.key(seed)
        ks = jax.random.split(key, 8)
        B, S, D, H, E = (2, 256, 128, 512, 8)
        Er = E - 1
        s_in = 1.0 / np.sqrt(D)
        s_hid = 1.0 / np.sqrt(H)
        return {'x': jax.random.normal(ks[0], (B, S, D), dtype=jnp.float32), 'router_w': jax.random.normal(ks[1], (D, E), dtype=jnp.float32) * s_in, 'up_w': jax.random.normal(ks[2], (Er, D, H), dtype=jnp.float32) * s_in, 'gate_w': jax.random.normal(ks[3], (Er, D, H), dtype=jnp.float32) * s_in, 'down_w': jax.random.normal(ks[4], (Er, H, D), dtype=jnp.float32) * s_hid * 0.1, 'shared_up_w': jax.random.normal(ks[5], (D, H), dtype=jnp.float32) * s_in, 'shared_gate_w': jax.random.normal(ks[6], (D, H), dtype=jnp.float32) * s_in, 'shared_down_w': jax.random.normal(ks[7], (H, D), dtype=jnp.float32) * s_hid * 0.1}
    _L0_ffn_all = _L0_ffn_setup()
    _L0_ffn_in = {k: v for k, v in _L0_ffn_all.items() if k in ('router_w', 'up_w', 'gate_w', 'down_w', 'shared_up_w', 'shared_gate_w', 'shared_down_w')}
    del _L0_ffn_all
    return {'x': x, 'ctx_1024': ctx_1024, 'L0_attn_Wq': _L0_attn_in['Wq'], 'L0_attn_bq': _L0_attn_in['bq'], 'L0_attn_Wk': _L0_attn_in['Wk'], 'L0_attn_bk': _L0_attn_in['bk'], 'L0_attn_Wv': _L0_attn_in['Wv'], 'L0_attn_bv': _L0_attn_in['bv'], 'L0_attn_Wo': _L0_attn_in['Wo'], 'L0_attn_bo': _L0_attn_in['bo'], 'L0_xattn_Wq': _L0_xattn_in['Wq'], 'L0_xattn_bq': _L0_xattn_in['bq'], 'L0_xattn_Wk': _L0_xattn_in['Wk'], 'L0_xattn_bk': _L0_xattn_in['bk'], 'L0_xattn_Wv': _L0_xattn_in['Wv'], 'L0_xattn_bv': _L0_xattn_in['bv'], 'L0_xattn_Wo': _L0_xattn_in['Wo'], 'L0_xattn_bo': _L0_xattn_in['bo'], 'L0_ffn_router_w': _L0_ffn_in['router_w'], 'L0_ffn_up_w': _L0_ffn_in['up_w'], 'L0_ffn_gate_w': _L0_ffn_in['gate_w'], 'L0_ffn_down_w': _L0_ffn_in['down_w'], 'L0_ffn_shared_up_w': _L0_ffn_in['shared_up_w'], 'L0_ffn_shared_gate_w': _L0_ffn_in['shared_gate_w'], 'L0_ffn_shared_down_w': _L0_ffn_in['shared_down_w']}

def reference(x, ctx_1024, L0_attn_Wq, L0_attn_bq, L0_attn_Wk, L0_attn_bk, L0_attn_Wv, L0_attn_bv, L0_attn_Wo, L0_attn_bo, L0_xattn_Wq, L0_xattn_bq, L0_xattn_Wk, L0_xattn_bk, L0_xattn_Wv, L0_xattn_bv, L0_xattn_Wo, L0_xattn_bo, L0_ffn_router_w, L0_ffn_up_w, L0_ffn_gate_w, L0_ffn_down_w, L0_ffn_shared_up_w, L0_ffn_shared_gate_w, L0_ffn_shared_down_w):
    import jax
    import jax.numpy as jnp

    def _L0_attn_ref(x, Wq, bq, Wk, bk, Wv, bv, Wo, bo):
        import jax, jax.numpy as jnp
        import numpy as np
        NUM_HEADS = 16
        WINDOW = 128

        def apply_rope(x):
            S, Dh = (x.shape[-2], x.shape[-1])
            half = Dh // 2
            inv_freq = 1.0 / 10000.0 ** (jnp.arange(half, dtype=jnp.float32) / half)
            ang = jnp.arange(S, dtype=jnp.float32)[:, None] * inv_freq[None, :]
            cos, sin = (jnp.cos(ang), jnp.sin(ang))
            x1, x2 = (x[..., :half], x[..., half:])
            return jnp.concatenate([x1 * cos - x2 * sin, x1 * sin + x2 * cos], axis=-1).astype(x.dtype)
        B, S, D = x.shape
        H = NUM_HEADS
        Dh = D // H

        def proj(W, b):
            y = jnp.einsum('bsd,ed->bse', x, W) + b
            return y.reshape(B, S, H, Dh).transpose(0, 2, 1, 3)
        q = apply_rope(proj(Wq, bq)) * Dh ** (-0.5)
        k = apply_rope(proj(Wk, bk))
        v = proj(Wv, bv)
        scores = jnp.einsum('bhqd,bhkd->bhqk', q, k)
        idx = jnp.arange(S)
        rel = idx[None, :] - idx[:, None]
        blocked = (rel > 0) | (rel < -WINDOW)
        scores = jnp.where(blocked[None, None], -jnp.inf, scores)
        probs = jax.nn.softmax(scores, axis=-1)
        out = jnp.einsum('bhqk,bhkd->bhqd', probs, v)
        out = out.transpose(0, 2, 1, 3).reshape(B, S, D)
        return jnp.einsum('bsd,ed->bse', out, Wo) + bo

    def _L0_xattn_ref(tgt, src, Wq, bq, Wk, bk, Wv, bv, Wo, bo):
        import jax, jax.numpy as jnp
        import numpy as np
        HIDDEN = 128
        NUM_HEADS = 16
        HEAD_DIM = HIDDEN // NUM_HEADS
        q = jnp.einsum('btd,hdk->bhtk', tgt, Wq) + bq[None, :, None, :]
        k = jnp.einsum('bsd,hdk->bhsk', src, Wk) + bk[None, :, None, :]
        v = jnp.einsum('bsd,hdk->bhsk', src, Wv) + bv[None, :, None, :]
        scale = 1.0 / jnp.sqrt(jnp.asarray(HEAD_DIM, q.dtype))
        scores = jnp.einsum('bhtk,bhsk->bhts', q, k) * scale
        weights = jax.nn.softmax(scores, axis=-1)
        out = jnp.einsum('bhts,bhsk->bhtk', weights, v)
        B, H, T, Dh = out.shape
        h = out.transpose(0, 2, 1, 3).reshape(B, T, H * Dh)
        return h @ Wo + bo

    def _L0_ffn_ref(x, router_w, up_w, gate_w, down_w, shared_up_w, shared_gate_w, shared_down_w):
        import jax, jax.numpy as jnp
        import numpy as np
        ALPHA = 2.0
        TOP_K = 2
        logits = jnp.einsum('bsd,de->bse', x, router_w)
        probs = jax.nn.softmax(logits, axis=-1)
        topk_vals, topk_idx = jax.lax.top_k(probs, TOP_K)
        top1_val = topk_vals[..., 0]
        top1_idx = topk_idx[..., 0]
        hid = jnp.einsum('bsd,edh->ebsh', x, up_w) * jax.nn.silu(jnp.einsum('bsd,edh->ebsh', x, gate_w))
        Er = up_w.shape[0]
        mask = (top1_idx[None, :, :] == jnp.arange(Er)[:, None, None]).astype(x.dtype)
        routed = jnp.einsum('ebsh,ehd,ebs->bsd', hid, down_w, mask)
        shid = jnp.einsum('bsd,dh->bsh', x, shared_up_w) * jax.nn.silu(jnp.einsum('bsd,dh->bsh', x, shared_gate_w))
        shared = jnp.einsum('bsh,hd->bsd', shid, shared_down_w)
        return ALPHA * top1_val[..., None] * routed + shared
    x = x + _L0_attn_ref(_layernorm(x, axis=-1), L0_attn_Wq, L0_attn_bq, L0_attn_Wk, L0_attn_bk, L0_attn_Wv, L0_attn_bv, L0_attn_Wo, L0_attn_bo)
    x = x + _L0_xattn_ref(_layernorm(x, axis=-1), ctx_1024, L0_xattn_Wq, L0_xattn_bq, L0_xattn_Wk, L0_xattn_bk, L0_xattn_Wv, L0_xattn_bv, L0_xattn_Wo, L0_xattn_bo)
    x = x + _L0_ffn_ref(_layernorm(x, axis=-1), L0_ffn_router_w, L0_ffn_up_w, L0_ffn_gate_w, L0_ffn_down_w, L0_ffn_shared_up_w, L0_ffn_shared_gate_w, L0_ffn_shared_down_w)
    return x

_drawn_inputs = setup_inputs


def setup_inputs(seed=0):
    import zlib

    import numpy as np

    out = dict(_drawn_inputs(seed))
    spreads = {'L0_attn_bq': (0.0, 0.8),
     'L0_attn_bk': (0.0, 0.8),
     'L0_attn_bv': (0.0, 0.426),
     'L0_attn_bo': (0.0, 0.1),
     'L0_xattn_bq': (0.0, 0.327),
     'L0_xattn_bk': (0.0, 0.8),
     'L0_xattn_bv': (0.0, 0.1),
     'L0_xattn_bo': (0.0, 0.1)}
    factors = {'L0_attn_Wq': 8.0, 'L0_attn_Wk': 8.0, 'L0_attn_Wv': 5.751}
    for name, (base, spread) in spreads.items():
        noise = np.random.default_rng([zlib.crc32(name.encode()), seed]).standard_normal(out[name].shape)
        drawn = base * np.exp(spread * noise) if base else spread * noise
        out[name] = jnp.asarray(drawn.astype(out[name].dtype))
    for name, factor in factors.items():
        out[name] = (out[name] * factor).astype(out[name].dtype)
    return out
```

```python
import concourse.bass as bass
from concourse import mybir
from contextlib import ExitStack

F32 = mybir.dt.float32
F16 = mybir.dt.float16
BF16 = mybir.dt.bfloat16
I32 = mybir.dt.int32
U32 = mybir.dt.uint32
ALU = mybir.AluOpType
ACT = mybir.ActivationFunctionType
AX = mybir.AxisListType

P = 128
H = 16
HD = P // H
SLOT = 32
HG = H * SLOT // P
K1 = 3 * HD
K2 = K1 + 2
VC = 2 * HD + 1
EPS = 1e-5
LAG = 4
ARENA = 58 * 1024


def decoder_layer(nc, x, ctx_in, sWq, sbq, sWk, sbk, sWv, sbv, sWo, sbo,
                  cWq, cbq, cWk, cbk, cWv, cbv, cWo, cbo,
                  router_w, up_w, gate_w, down_w, sup_w, sgate_w, sdown_w,
                  rope_cos, rope_sin, row_consts, earlier_in, causal_rows, causal_cols, ident32, ident16, identbf,
                  out):
    NB, S, D = x.shape
    C = ctx_in.shape[1]
    CP = C + C % 2
    QSCALE = float(HD) ** -0.5
    E = router_w.shape[1]
    F = up_w.shape[2]
    FC = F // P
    NG = NB // 4
    NT = NB + E - 2
    ALPHA = 2.0
    assert S == P and D == P and NB % 16 == 0 and F == 4 * P and NT % 2 == 0 and NB * E <= 512

    with ExitStack() as stack:
        def sb(name, shape, dt=F32):
            return stack.enter_context(nc.sbuf_tensor(name, shape, dt))

        def ps(name):
            return stack.enter_context(nc.psum_tensor(name, [P, 512], F32))

        def sem(name):
            return stack.enter_context(nc.semaphore(name))

        arena = sb("arena", [P, ARENA], mybir.dt.uint8)
        taken = [0]

        def carve(shape, dt=F32):
            size = mybir.dt.size(dt)
            for n in shape[1:]:
                size *= n
            at = taken[0]
            taken[0] += (size + 31) // 32 * 32
            assert taken[0] <= ARENA
            flat = arena[:, at:at + size].bitcast(dt)
            names = "abcd"[:len(shape) - 1]
            if len(names) == 1:
                return flat
            return flat.rearrange(f"p ({' '.join(names)}) -> p {' '.join(names)}",
                                  **dict(zip(names[1:], shape[2:])))

        resid = sb("resid", [P, NB, D])
        id32 = sb("id32", [P, P])
        id16 = sb("id16", [P, P], F16)
        idbf = sb("idbf", [P, P], BF16)
        mask_qk = sb("mask_qk", [P, 4 * P], BF16)
        mask_kq = sb("mask_kq", [P, 4 * P], BF16)
        cos = sb("cos", [P, 2 * D])
        sin = sb("sin", [P, 2 * D])
        w_qkv = sb("w_qkv", [P, 3 * D])
        w_o = sb("w_o", [P, D])
        wc_q = sb("wc_q", [P, D])
        wc_kv = sb("wc_kv", [P, 2 * D])
        wc_o = sb("wc_o", [P, D])
        rope_bias = sb("rope_bias", [P, 2 * D])
        b_cqs = sb("b_cqs", [P, D])
        b_ck = sb("b_ck", [P, D])
        out_bias = sb("out_bias", [P, 2, D])
        eps = sb("eps", [P, 1])
        neg_half = sb("neg_half", [P, 1])

        bn6 = carve([P, 3, 6])
        mv = carve([P, 3, 2, 2])
        varp = carve([P, 3, 1])
        rstd = carve([P, 3, 2])
        xn = carve([P, 3, 2, D])
        xnT = carve([P, 3, P])
        rot = carve([P, 2, 2 * D])
        rot1 = carve([P, 2 * D])
        roped = carve([P, 2, 2 * D])
        stQ = carve([P, 2, H, SLOT], F16)
        stK = carve([P, 2, H, SLOT], F16)
        qkT = carve([P, 2, 8 * P], F16)
        qmT = carve([P, 4 * P], F16)
        val = carve([P, 2, H, VC], F16)
        nmax = carve([P, 2, H])
        e32 = carve([P, 2, 512])
        pr_hi = carve([P, 2, 512], F16)
        pr_lo = carve([P, 2, 512], F16)
        rsum = carve([P, 2, H])
        oraw = carve([P, 2, D])
        otok = carve([P, 2, 2, D])
        oT = carve([P, 2, P])
        xb = carve([P, 2, 2, D])
        ctx_t = carve([P, 2, D])
        ctxT = carve([P, P])
        q2 = carve([P, D])
        k2 = carve([P, D])
        stQ2 = carve([P, 2, H, SLOT], F16)
        stK2 = carve([P, 2, H, SLOT], F16)
        qkT2 = carve([P, 2, 4 * P + 4 * CP], F16)
        qmT2 = carve([P, 4 * P], F16)
        val2 = carve([P, 2, H, VC], F16)
        nmax2 = carve([P, 2, H])
        e32c = carve([P, 2, 512])
        pr_hic = carve([P, 2, 512], F16)
        pr_loc = carve([P, 2, 512], F16)
        w_load = e32
        b_rope = e32c
        b_qk = rot1
        b_cq = q2
        bv_bc = rot.rearrange("p a (b c) -> p a b c", c=P)[:, :, 0]
        bv_col = mv.rearrange("p a b c -> p (a b c)")[:, 0:2]
        b_o = otok[:, 0]
        xn3T = sb("xn3T", [P, NB, P])

        xn3 = sb("xn3", [P, NB, P])
        logits = sb("logits", [P, NB, E])
        w_router = sb("w_router", [P, E])
        w_gate = sb("w_gate", [P, E - 1, F])
        w_up = sb("w_up", [P, E - 1, F])
        ws_gate = sb("ws_gate", [P, F])
        ws_up = sb("ws_up", [P, F])
        ws_down = sb("ws_down", [P, FC, D])

        attention_end = taken[0]
        taken[0] = 0
        r_shift = carve([P, NB * E])
        r_mark = carve([P, NB * E])
        r_hot = carve([P, NB * E])
        r_run = carve([P, NB * E])
        r_hot16 = carve([P, NB * E], F16)
        r_exp = carve([P, NB * E])
        r_row = carve([P, NB * E])
        owner_cmp = carve([P, NT * (E - 1)])
        top = sb("top", [P, NB])
        gate = sb("gate", [P, NB])
        pos = sb("pos", [P, NB])
        pos_put = sb("pos_put", [P, NB], U32)
        pos_get = sb("pos_get", [P, NB], U32)
        tiles = sb("tiles", [P, E])
        tile_end = sb("tile_end", [P, E])
        tile_start = sb("tile_start", [P, E])
        owner_f = sb("owner_f", [P, NT])
        owner = sb("owner", [P, NT], I32)
        consts = sb("consts", [P, NT + NT + E])
        tile_rows = consts[:, 0:NT]
        tile_ids = consts[:, NT:2 * NT]
        marks = consts[:, 2 * NT:2 * NT + E]
        earlier = sb("earlier", [P, P], F16)
        ones16 = sb("ones16", [P, P], F16)
        ones_f = sb("ones_f", [P, NB])
        zero_t = sb("zero_t", [P, D])

        taken[0] = 0
        w_down = carve([P, E - 1, FC, D])
        y_row = carve([P, 4, D])
        silu_s = carve([P, 2, F])
        hid = carve([P, 2, F])
        hT_tile = carve([P, 2, F])
        hidT = carve([P, 2, FC, 4 * P])
        x_tile = carve([P, 2, D])
        xT_tile = carve([P, 2, D])
        y_tile = carve([P, 2, D])

        xs = nc.dram_tensor("xs", [NT * P + NB * P, D], F32, kind="Internal").ap()
        ys = nc.dram_tensor("ys", [NT * P + P, D], F32, kind="Internal").ap()
        xs_tiles = xs[0:NT * P].rearrange("(k p) d -> k p d", p=P)
        ys_tiles = ys[0:NT * P].rearrange("(k p) d -> k p d", p=P)

        sc = [ps(f"sc{r}") for r in range(4)]
        pj = ps("pj")
        st = ps("st")
        pv = ps("pv")
        ro = ps("ro")
        st16 = st[:, :].bitcast(F16)

        w_in = sem("w_in"); x_head = sem("x_head"); x_tail = sem("x_tail")
        ctx_in_s = [sem("ctx_in0"), sem("ctx_in1")]
        setup_v = sem("setup_v"); setup_pe = sem("setup_pe"); setup_g = sem("setup_g"); setup_a = sem("setup_a")
        ln_stats = [sem(f"ln{n}_stats") for n in (1, 2, 3)]
        ln_mv = [sem(f"ln{n}_mv") for n in (1, 2, 3)]
        ln_var = [sem(f"ln{n}_var") for n in (1, 2, 3)]
        ln_rstd = [sem(f"ln{n}_rstd") for n in (1, 2, 3)]
        xn_ready = [sem(f"xn{n}_ready") for n in (1, 2, 3)]
        xnT_psum = [sem(f"xnT{n}_psum") for n in (1, 2, 3)]
        xnT_ready = [sem(f"xnT{n}_ready") for n in (1, 2, 3)]
        qkv_psum = sem("qkv_psum"); v_hi = sem("v_hi"); qkv_read = sem("qkv_read")
        rot1_ready = sem("rot1_ready"); roped_ready = sem("roped_ready")
        qk_hi = sem("qk_hi"); qk_lo = sem("qk_lo"); qkT_psum = sem("qkT_psum"); qkT_ready = sem("qkT_ready")
        s1_psum = sem("s1_psum"); s1_max = sem("s1_max"); m_hi = sem("m_hi"); m_ready = sem("m_ready")
        qmT_psum = sem("qmT_psum"); qmT_ready = sem("qmT_ready")
        s2_psum = sem("s2_psum"); s2_exp = sem("s2_exp"); s2_lo = sem("s2_lo"); s2_pv = sem("s2_pv")
        o_sum = sem("o_sum"); o_ready = sem("o_ready"); xb_ready = sem("xb_ready")
        oT_psum = sem("oT_psum"); oT_ready = sem("oT_ready"); proj_psum = sem("proj_psum"); resid1 = sem("resid1")
        q2_psum = sem("q2_psum"); q2_ready = sem("q2_ready"); q2_hi = sem("q2_hi"); q2_lo = sem("q2_lo")
        ctxT_psum = sem("ctxT_psum"); ctxT_ready = sem("ctxT_ready"); kv2_psum = sem("kv2_psum")
        v2_hi = sem("v2_hi"); k2_ready = sem("k2_ready"); k2_hi = sem("k2_hi"); k2_lo = sem("k2_lo")
        qkT2_psum = sem("qkT2_psum"); qkT2_ready = sem("qkT2_ready")
        c1_psum = sem("c1_psum"); c1_max = sem("c1_max"); cm_hi = sem("cm_hi"); cm_ready = sem("cm_ready")
        qmT2_psum = sem("qmT2_psum"); qmT2_ready = sem("qmT2_ready")
        c2_psum = sem("c2_psum"); c2_exp = sem("c2_exp"); c2_lo = sem("c2_lo"); c2_pv = sem("c2_pv")
        oc_sum = sem("oc_sum"); oc_ready = sem("oc_ready"); xb2_ready = sem("xb2_ready")
        ocT_psum = sem("ocT_psum"); ocT_ready = sem("ocT_ready"); projc_psum = sem("projc_psum"); resid2 = sem("resid2")
        rot_mid = sem("rot_mid"); kv2_read = sem("kv2_read"); logits_psum = sem("logits_psum")
        logits_ready = sem("logits_ready"); xn3T_kept = sem("xn3T_kept")
        xn3_kept = [sem("xn3_kept0"), sem("xn3_kept1")]
        stored = sem("stored")
        w_ffn = sem("w_ffn"); w_down_in = sem("w_down_in"); zeroed = sem("zeroed"); zero_ready = sem("zero_ready")
        route = sem("route"); shift_ready = sem("shift_ready"); rexp_ready = sem("rexp_ready")
        hot_ready = sem("hot_ready"); counts_psum = sem("counts_psum"); pos_ready = sem("pos_ready")
        route_done = sem("route_done"); scattered = sem("scattered")
        gathered = [sem(f"gathered{n}") for n in range(4)]
        combined = sem("combined")
        sh_gu = sem("sh_gu"); sh_silu = sem("sh_silu"); sh_mul = sem("sh_mul"); sh_y = sem("sh_y"); sh_add = sem("sh_add")
        x_tile_in = [sem("x_tile_in0"), sem("x_tile_in1")]
        y_stored = [sem("y_stored0"), sem("y_stored1")]
        tT_psum = sem("tT_psum"); tT_ready = sem("tT_ready"); t_gu = sem("t_gu"); t_silu = sem("t_silu")
        t_mul = sem("t_mul"); thT_psum = sem("thT_psum"); thT_ready = sem("thT_ready")
        ty_psum = sem("ty_psum"); ty_ready = sem("ty_ready")

        block = stack.enter_context(nc.Block())

        def wait(eng, event, count):
            if not (isinstance(count, int) and count <= 0):
                eng.wait_ge(event, count)

        def run(eng, step):
            for i in range(6):
                step(i, i % 2)
            with eng.Fori(3, NB // 2) as pair:
                step(2 * pair, 0)
                step(2 * pair + 1, 1)
            for i in range(NB, NB + LAG):
                step(i, i % 2)

        def has(i, lag):
            return not isinstance(i, int) or 0 <= i - lag < NB

        def upto(count):
            return min(count, NB) if isinstance(count, int) else count

        def attention_over(eng):
            eng.wait_ge(logits_ready, NB)
            eng.wait_ge(o_ready, NB)
            eng.wait_ge(xb2_ready, NB)
            eng.wait_ge(xn3T_kept, NB)
            eng.wait_ge(qmT2_ready, NB)
            for par in range(2):
                eng.wait_ge(xn3_kept[par], 16 * (NB // 2))

        def run_groups(eng, lo, group):
            hi = lo + NG // 2
            group(lo, 0, True, False)
            group(lo + 1, 1, False, False)
            if hi - lo > 2:
                with eng.Fori(lo // 2 + 1, hi // 2) as pair:
                    group(2 * pair, 0, False, False)
                    group(2 * pair + 1, 1, False, False)
            group(hi, 0, False, True)

        def run_tiles(eng, tile):
            for k in range(4):
                tile(k, k % 2)
            with eng.Fori(2, NT // 2) as pair:
                tile(2 * pair, 0)
                tile(2 * pair + 1, 1)
            for k in range(NT, NT + 4):
                tile(k, k % 2)

        def within(k, lag):
            return not isinstance(k, int) or 0 <= k - lag < NT

        W_FFN = 2 * (E - 1) + 3

        N_LOADS = 26
        W_ALL = 16 * N_LOADS

        @block.sync
        def _(sync):
            sync.dma_start(resid[:, 0:6, :], x[0:6].rearrange("b s d -> s b d")).then_inc(x_head, 16)
            for n, w in enumerate((sWq, sWk, sWv, sWo)):
                sync.dma_start(w_load[:, n // 2, n % 2 * D:n % 2 * D + D], w).then_inc(w_in, 16)
            sync.dma_start(wc_q[:, :].rearrange("p (h k) -> p h k", k=HD), cWq.rearrange("h d k -> d h k")).then_inc(w_in, 16)
            for n, w in enumerate((cWk, cWv)):
                sync.dma_start(wc_kv[:, n * D:(n + 1) * D].rearrange("p (h k) -> p h k", k=HD),
                               w.rearrange("h d k -> d h k")).then_inc(w_in, 16)
            sync.dma_start(wc_o[:, :], cWo).then_inc(w_in, 16)
            sync.dma_start(w_router[:, :], router_w).then_inc(w_in, 16)
            for t, src in ((cos, rope_cos), (sin, rope_sin), (mask_qk, causal_rows.bitcast(BF16)), (mask_kq, causal_cols.bitcast(BF16)),
                           (consts, row_consts), (earlier, earlier_in),
                           (id32, ident32), (id16, ident16), (idbf, identbf.bitcast(BF16))):
                sync.dma_start(t[:, :], src).then_inc(w_in, 16)
            for e in range(E - 1):
                sync.dma_start(w_gate[:, e, :], gate_w[e]).then_inc(w_ffn, 16)
                sync.dma_start(w_up[:, e, :], up_w[e]).then_inc(w_ffn, 16)
            sync.dma_start(ws_gate[:, :], sgate_w).then_inc(w_ffn, 16)
            sync.dma_start(ws_up[:, :], sup_w).then_inc(w_ffn, 16)
            sync.dma_start(ws_down[:, :, :], sdown_w.rearrange("(c p) d -> p c d", p=P)).then_inc(w_ffn, 16)

            def step(i, p):
                if has(i, 0):
                    wait(sync, ctxT_psum, i - 1)
                    sync.dma_start(ctx_t[0:C, p, :], ctx_in[i]).then_inc(ctx_in_s[p], 16)
                if has(i, 4):
                    wait(sync, xn_ready[2], i - 3)
                    sync.dma_start(xn3[:, i - 4, :], xn[:, 2, p, :]).then_inc(xn3_kept[p], 16)
            run(sync, step)

            attention_over(sync)
            sync.wait_ge(route_done, 1)
            for e in range(E - 1):
                sync.dma_start(w_down[:, e, :, :], down_w[e].rearrange("(c p) d -> p c d", p=P)).then_inc(w_down_in, 16)

            sync.wait_ge(scattered, 16 * NB)

            def tile(k, p):
                if within(k, 0):
                    wait(sync, tT_psum, k - 1)
                    sync.dma_start(x_tile[:, p, :], xs_tiles[k]).then_inc(x_tile_in[p], 16)
                if within(k, 4):
                    wait(sync, ty_ready, k - 3)
                    sync.dma_start(ys_tiles[k - 4], y_tile[:, p, :]).then_inc(y_stored[p], 16)
            run_tiles(sync, tile)

            for n in range(NG):
                sync.wait_ge(combined, 4 * n + 4)
                sync.dma_start(out[4 * n:4 * n + 4].rearrange("b s d -> s b d"),
                               resid[:, 4 * n:4 * n + 4, :]).then_inc(stored, 16)
            sync.wait_ge(stored, 16 * NG)

        @block.gpsimd
        def _(pool):
            g = nc.gpsimd
            pool.wait_ge(setup_v, 8)

            def ln_rstd_of(n, b, p):
                wait(pool, ln_mv[n], b + 1)
                g.tensor_tensor(varp[:, n, :], mv[:, n, p, 1:2], eps[:, :], ALU.add).then_inc(ln_var[n], 1)
                wait(pool, ln_var[n], b + 1)
                g.tensor_tensor(rstd[:, n, p:p + 1], varp[:, n, :], neg_half[:, :], ALU.pow).then_inc(ln_rstd[n], 1)

            def prob_lo(done, exped, used, e, hi, lo, b, u, rows):
                wait(pool, exped, 4 * b + u + 1)
                wait(pool, used, 4 * b + u - 1)
                g.tensor_tensor(lo[0:rows, u % 2, :], e[0:rows, u % 2, :], hi[0:rows, u % 2, :],
                                ALU.subtract).then_inc(done, 1)

            def step(i, p):
                q = 1 - p
                if has(i, 0):
                    ln_rstd_of(0, i, p)
                if has(i, 4):
                    prob_lo(c2_lo, c2_exp, c2_pv, e32c, pr_hic, pr_loc, i - 4, 0, C)
                if has(i, 2):
                    ln_rstd_of(1, i - 2, p)
                if has(i, 4):
                    prob_lo(c2_lo, c2_exp, c2_pv, e32c, pr_hic, pr_loc, i - 4, 1, C)
                if has(i, 0):
                    wait(pool, rot1_ready, i + 1)
                    g.tensor_tensor(rot1[:, :], rot[:, 0, :], rope_bias[:, :], ALU.add).then_inc(rot_mid, 1)
                    wait(pool, rot_mid, i + 1)
                    wait(pool, qk_lo, i - 1)
                    g.tensor_tensor(roped[:, p, :], rot1[:, :], rot[:, 1, :], ALU.add).then_inc(roped_ready, 1)
                if has(i, 4):
                    prob_lo(c2_lo, c2_exp, c2_pv, e32c, pr_hic, pr_loc, i - 4, 2, C)
                    prob_lo(c2_lo, c2_exp, c2_pv, e32c, pr_hic, pr_loc, i - 4, 3, C)
                if has(i, 2):
                    b = i - 2
                    wait(pool, q2_hi, b + 1)
                    g.tensor_tensor(stQ2[:, p, :, HD:2 * HD], q2[:, :].rearrange("p (h d) -> p h d", d=HD),
                                    stQ2[:, p, :, 0:HD], ALU.subtract).then_inc(q2_lo, 1)
                if has(i, 0):
                    wait(pool, qk_hi, i + 1)
                    r = roped[:, p, :].rearrange("p (t h d) -> p t h d", t=2, d=HD)
                    g.tensor_tensor(stQ[:, p, :, HD:2 * HD], r[:, 0], stQ[:, p, :, 0:HD], ALU.subtract)
                    g.tensor_tensor(stK[:, p, :, 2 * HD:3 * HD], r[:, 1], stK[:, p, :, 0:HD],
                                    ALU.subtract).then_inc(qk_lo, 1)
                if has(i, 1):
                    b = i - 1
                    wait(pool, resid1, b - 1)
                    g.tensor_tensor(xb[:, 0, q, :], resid[:, b, :], out_bias[:, 0, :], ALU.add).then_inc(xb_ready, 1)
                    for u in range(4):
                        prob_lo(s2_lo, s2_exp, s2_pv, e32, pr_hi, pr_lo, b, u, P)
                        if u == 1 and has(i, 2):
                            wait(pool, k2_hi, i - 1)
                            g.tensor_tensor(stK2[0:C, p, :, 2 * HD:3 * HD],
                                            k2[0:C, :].rearrange("p (h d) -> p h d", d=HD),
                                            stK2[0:C, p, :, 0:HD], ALU.subtract).then_inc(k2_lo, 1)
                elif has(i, 2):
                    wait(pool, k2_hi, i - 1)
                    g.tensor_tensor(stK2[0:C, p, :, 2 * HD:3 * HD],
                                    k2[0:C, :].rearrange("p (h d) -> p h d", d=HD),
                                    stK2[0:C, p, :, 0:HD], ALU.subtract).then_inc(k2_lo, 1)
                if has(i, 4):
                    ln_rstd_of(2, i - 4, p)
                if has(i, 3):
                    b = i - 3
                    wait(pool, resid1, b + 1)
                    wait(pool, resid2, b - 1)
                    g.tensor_tensor(xb[:, 1, q, :], resid[:, b, :], out_bias[:, 1, :], ALU.add).then_inc(xb2_ready, 1)
            run(pool, step)

            pool.wait_ge(zeroed, 32)
            pool.wait_ge(pos_ready, 1)
            for par in range(2):
                pool.wait_ge(xn3_kept[par], 16 * (NB // 2))
            for b in range(NB):
                g.indirect_dma_start(out=xs, out_offset=bass.IndirectOffsetOnAxis(ap=pos_put[:, b:b + 1], axis=0),
                                     in_=xn3[:, b, :], in_offset=None).then_inc(scattered, 16)
            pool.wait_ge(route_done, 1)
            for par in range(2):
                pool.wait_ge(y_stored[par], 16 * (NT // 2))
            for b in range(NB):
                wait(pool, combined, b - 3)
                g.indirect_dma_start(out=y_row[:, b % 4, :], out_offset=None, in_=ys,
                                     in_offset=bass.IndirectOffsetOnAxis(ap=pos_get[:, b:b + 1], axis=0)).then_inc(gathered[b % 4], 16)

        @block.vector
        def _(dve):
            v = nc.vector

            def swapped(t):
                return t.rearrange("p (g t d) -> p g t d", t=2, d=HD // 2)[:, :, ::-1, :]

            def halves(t):
                return t.rearrange("p (g t d) -> p g t d", t=2, d=HD // 2)

            v.memset(zero_t[:, :], 0.0).then_inc(zero_ready, 1)
            v.memset(neg_half[:, :], -0.5)
            v.memset(eps[:, :], EPS)
            v.memset(ones16[:, :], 1.0)
            v.memset(ones_f[:, :], 1.0)
            for t in (stQ, stK, stQ2, stK2):
                v.memset(t[:, :, :, :].rearrange("p a h s -> p (a h s)").bitcast(U32), 0)
            v.memset(val[:, :, :, VC - 1:VC], 1.0)
            v.memset(val2[:, :, :, VC - 1:VC], 1.0).then_inc(setup_v, 1)
            dve.wait_ge(setup_v, 1)
            v.memset(stK[:, :, :, K1:K2], 1.0)
            v.memset(stK2[:, :, :, K1:K2], 1.0).then_inc(setup_v, 1)
            dve.wait_ge(w_in, W_ALL)
            v.tensor_copy(bv_bc[:, 0, :], bv_col[:, 0:1].to_broadcast([P, P]))
            v.tensor_copy(bv_bc[:, 1, :], bv_col[:, 1:2].to_broadcast([P, P]))
            v.tensor_scalar_mul(b_cqs[:, :], b_cq[:, :], QSCALE)
            v.tensor_tensor(b_rope[:, 0, 0:2 * D], b_qk[:, :], cos[:, :], ALU.mult)
            v.tensor_tensor(halves(b_rope[:, 1, 0:2 * D]), swapped(b_qk[:, :]), halves(sin[:, :]),
                            ALU.mult).then_inc(setup_v, 1)
            dve.wait_ge(setup_v, 3)
            v.tensor_tensor(rope_bias[:, :], b_rope[:, 0, 0:2 * D], b_rope[:, 1, 0:2 * D], ALU.add).then_inc(setup_v, 1)
            dve.wait_ge(setup_pe, 1)
            v.tensor_copy(w_qkv[:, :], pj[:, 0:3 * D])
            v.tensor_copy(w_o[:, :], ro[:, 0:D]).then_inc(setup_v, 1)
            dve.wait_ge(setup_pe, 2)
            v.tensor_tensor(out_bias[:, 0, :], ro[:, D:2 * D], b_o[:, 0, :], ALU.add)
            v.tensor_tensor(out_bias[:, 1, :], ro[:, 2 * D:3 * D], b_o[:, 1, :], ALU.add).then_inc(setup_v, 3)
            dve.wait_ge(x_head, 16)

            def ln_sums(n, b):
                v.bn_stats(bn6[:, n, :], resid[:, b, :]).then_inc(ln_stats[n], 1)

            def ln_mean(n, b, p):
                v.bn_aggr(mv[:, n, p, :], bn6[:, n, :]).then_inc(ln_mv[n], 1)

            def ln_out(n, b, p):
                wait(dve, ln_rstd[n], b + 1)
                v.tensor_scalar(xn[:, n, p, :], resid[:, b, :], mv[:, n, p, 0:1], rstd[:, n, p:p + 1],
                                ALU.subtract, ALU.mult).then_inc(xn_ready[n], 1)

            def unit_max(done, scores, t, nm, n, b, u, p, keys):
                wait(dve, scores, 4 * b + u + 1)
                v.tensor_reduce(nm[:, p, :].rearrange("p (g j) -> p g j", j=4)[:, :, u],
                                t[:, 0:4 * keys].rearrange("p (g k) -> p g k", k=keys), axis=AX.X, op=ALU.max,
                                negate=True).then_inc(done, 1)

            def max_parts(done, hi, ready, nm, stk, b, p):
                wait(dve, done, 4 * b + 4)
                v.tensor_copy(stk[:, p, :, K1], nm[:, p, :]).then_inc(hi, 1)
                wait(dve, hi, b + 1)
                v.tensor_tensor(stk[:, p, :, K1 + 1], nm[:, p, :], stk[:, p, :, K1], ALU.subtract).then_inc(ready, 1)

            def norm(n, prods, summed, ready, b, p):
                wait(dve, prods, 4 * b + 4)
                parts = pv[:, 0:H * VC].rearrange("p (h c) -> p h c", c=VC)
                v.reciprocal(rsum[:, n, :], parts[:, :, VC - 1])
                v.tensor_reduce(oraw[:, n, :].rearrange("p (h d) -> p h d", d=HD),
                                parts[:, :, 0:2 * HD].rearrange("p h (t d) -> p h d t", t=2), axis=AX.X,
                                op=ALU.add).then_inc(summed, 1)
                wait(dve, summed, b + 1)
                v.tensor_tensor(otok[:, n, p, :].rearrange("p (h d) -> p h d", d=HD),
                                oraw[:, n, :].rearrange("p (h d) -> p h d", d=HD),
                                rsum[:, n, :].unsqueeze(2).to_broadcast([P, H, HD]), ALU.mult).then_inc(ready, 1)

            def step(i, p):
                q = 1 - p
                if has(i, 0):
                    if isinstance(i, int) and i == 5:
                        dve.wait_ge(x_tail, 16)
                    ln_sums(0, i)
                    wait(dve, ln_stats[0], i + 1)
                if has(i, 1):
                    unit_max(s1_max, s1_psum, sc[0], nmax, 0, i - 1, 0, q, P)
                if has(i, 0):
                    ln_mean(0, i, p)
                    ln_out(0, i, p)
                if has(i, 2):
                    b = i - 2
                    wait(dve, proj_psum, b + 1)
                    wait(dve, xb_ready, b + 1)
                    v.tensor_tensor(resid[:, b, :], xb[:, 0, p, :], ro[:, P:2 * P], ALU.add).then_inc(resid1, 1)
                if has(i, 2):
                    wait(dve, resid1, i - 1)
                if has(i, 1):
                    unit_max(s1_max, s1_psum, sc[2], nmax, 0, i - 1, 1, q, P)
                if has(i, 2):
                    ln_sums(1, i - 2)
                if has(i, 0) and has(i, 2):
                    wait(dve, ln_stats[1], i - 1)
                if has(i, 0):
                    wait(dve, v_hi, i + 1)
                    wait(dve, roped_ready, i)
                    v.tensor_tensor(rot[:, 0, :], pj[:, 0:2 * D], cos[:, :], ALU.mult)
                if has(i, 2):
                    if isinstance(i, int):
                        wait(dve, ln_stats[1], i - 1)
                    ln_mean(1, i - 2, p)
                if has(i, 0):
                    v.tensor_tensor(halves(rot[:, 1, :]), swapped(pj[:, 0:2 * D]), halves(sin[:, :]),
                                    ALU.mult).then_inc(rot1_ready, 1)
                    v.tensor_tensor(val[:, p, :, HD:2 * HD], pj[:, 2 * D:3 * D].rearrange("p (h d) -> p h d", d=HD),
                                    val[:, p, :, 0:HD], ALU.subtract).then_inc(qkv_read, 1)
                if has(i, 1):
                    unit_max(s1_max, s1_psum, sc[0], nmax, 0, i - 1, 2, q, P)
                if has(i, 2):
                    ln_out(1, i - 2, p)
                if has(i, 1):
                    unit_max(s1_max, s1_psum, sc[2], nmax, 0, i - 1, 3, q, P)
                    max_parts(s1_max, m_hi, m_ready, nmax, stQ, i - 1, q)
                if has(i, 2):
                    b = i - 2
                    wait(dve, q2_psum, b + 1)
                    wait(dve, q2_lo, b)
                    v.scalar_tensor_tensor(out=q2[:, :], in0=ro[:, 3 * P:4 * P], scalar=QSCALE, in1=b_cqs[:, :],
                                           op0=ALU.mult, op1=ALU.add).then_inc(q2_ready, 1)
                if has(i, 4):
                    norm(1, c2_pv, oc_sum, oc_ready, i - 4, p)
                if has(i, 3):
                    unit_max(c1_max, c1_psum, sc[1], nmax2, 0, i - 3, 0, q, C)
                if has(i, 2):
                    b = i - 2
                    wait(dve, v2_hi, b + 1)
                    wait(dve, k2_lo, b)
                    v.tensor_tensor(k2[0:C, :], pj[0:C, 0:D], b_ck[0:C, :], ALU.add).then_inc(k2_ready, 1)
                    v.tensor_tensor(val2[0:C, p, :, HD:2 * HD],
                                    pj[0:C, D:2 * D].rearrange("p (h d) -> p h d", d=HD),
                                    val2[0:C, p, :, 0:HD], ALU.subtract).then_inc(kv2_read, 1)
                if has(i, 3):
                    unit_max(c1_max, c1_psum, sc[3], nmax2, 0, i - 3, 1, q, C)
                if has(i, 0):
                    wait(dve, qkT_psum, i + 1)
                    v.tensor_copy(qkT[:, p, :], st16[:, :]).then_inc(qkT_ready, 1)
                if has(i, 3):
                    unit_max(c1_max, c1_psum, sc[1], nmax2, 0, i - 3, 2, q, C)
                if has(i, 4):
                    b = i - 4
                    wait(dve, projc_psum, b + 1)
                    wait(dve, xb2_ready, b + 1)
                    v.tensor_tensor(resid[:, b, :], xb[:, 1, p, :], ro[:, P:2 * P], ALU.add).then_inc(resid2, 1)
                    wait(dve, resid2, b + 1)
                if has(i, 3):
                    unit_max(c1_max, c1_psum, sc[3], nmax2, 0, i - 3, 3, q, C)
                if has(i, 4):
                    ln_sums(2, i - 4)
                    wait(dve, ln_stats[2], i - 3)
                if has(i, 3):
                    max_parts(c1_max, cm_hi, cm_ready, nmax2, stQ2, i - 3, q)
                if has(i, 4):
                    ln_mean(2, i - 4, p)
                    wait(dve, xn3_kept[p], 8 * i - 32 - 8 * p)
                    ln_out(2, i - 4, p)
                if has(i, 1):
                    norm(0, s2_pv, o_sum, o_ready, i - 1, q)
                if has(i, 4):
                    b = i - 4
                    wait(dve, logits_psum, b + 1)
                    v.tensor_copy(logits[:, b, :], ro[:, 3 * P:3 * P + E]).then_inc(logits_ready, 1)
            run(dve, step)

            attention_over(dve)
            links = [0]

            def link(ins):
                links[0] += 1
                ins.then_inc(route, 1)
                dve.wait_ge(route, links[0])

            def by_row(t):
                return t.rearrange("p (b e) -> p b e", e=E)

            def over_experts(t):
                return t.unsqueeze(2).to_broadcast([P, NB, E])

            link(v.tensor_reduce(top[:, :], logits[:, :, :], axis=AX.X, op=ALU.max))
            v.tensor_tensor(by_row(r_shift), logits[:, :, :], over_experts(top[:, :]), ALU.subtract).then_inc(shift_ready, 1)
            dve.wait_ge(shift_ready, 1)
            link(v.scalar_tensor_tensor(out=by_row(r_mark), in0=by_row(r_shift), scalar=0.0,
                                        in1=marks[:, :].unsqueeze(1).to_broadcast([P, NB, E]), op0=ALU.is_equal, op1=ALU.mult))
            link(v.tensor_reduce(top[:, :], by_row(r_mark), axis=AX.X, op=ALU.max))
            link(v.tensor_tensor(by_row(r_hot), by_row(r_mark), over_experts(top[:, :]), ALU.is_equal))
            v.tensor_copy(r_hot16, r_hot).then_inc(hot_ready, 1)
            dve.wait_ge(rexp_ready, 1)
            link(v.tensor_reduce(top[:, :], by_row(r_exp[:, :]), axis=AX.X, op=ALU.add))
            link(v.reciprocal(gate[:, :], top[:, :]))
            link(v.tensor_scalar_mul(gate[:, :], gate[:, :], ALPHA))
            dve.wait_ge(counts_psum, 1)
            tot = by_row(sc[1][:, 0:NB * E])
            before = by_row(sc[0][:, 0:NB * E])
            for e in range(E):
                ins = v.tensor_tensor_scan(by_row(r_run)[:, :, e], ones_f[:, 0:NB], tot[:, :, e], 0.0, ALU.mult, ALU.add)
            link(ins)
            by_expert = by_row(r_mark).rearrange("p b e -> p e b")
            v.tensor_tensor(by_expert, by_row(r_run)[:, NB - 1, :].unsqueeze(2).to_broadcast([P, E, NB]),
                            tile_rows[:, 0:NB].unsqueeze(1).to_broadcast([P, E, NB]), ALU.is_gt)
            link(v.tensor_tensor(by_row(r_row[:, :]), by_row(r_run), tot, ALU.subtract))
            v.tensor_reduce(tiles[:, :], by_expert, axis=AX.X, op=ALU.add)
            link(v.tensor_tensor(by_row(r_run), by_row(r_row[:, :]), before, ALU.add))
            link(v.tensor_tensor_scan(tile_end[:, :], ones_f[:, 0:E], tiles[:, :], 0.0, ALU.mult, ALU.add))
            v.memset(tile_start[:, E - 1:E], float(NT))
            link(v.tensor_tensor(tile_start[:, 0:E - 1], tile_end[:, 0:E - 1], tiles[:, 0:E - 1], ALU.subtract))
            link(v.scalar_tensor_tensor(out=by_row(r_row[:, :]), in0=tile_start[:, :].unsqueeze(1).to_broadcast([P, NB, E]),
                                        scalar=float(P), in1=by_row(r_run), op0=ALU.mult, op1=ALU.add))
            link(v.tensor_tensor(r_shift, r_row[:, :], r_hot, ALU.mult))
            link(v.tensor_reduce(pos[:, :], by_row(r_shift), axis=AX.X, op=ALU.add))
            v.tensor_copy(pos_put[:, :], pos[:, :]).then_inc(pos_ready, 1)
            link(v.scalar_tensor_tensor(out=top[:, :], in0=pos[:, :], scalar=float(NT * P), in1=by_row(r_hot)[:, :, E - 1],
                                        op0=ALU.subtract, op1=ALU.mult))
            v.tensor_tensor(pos_get[:, :], pos[:, :], top[:, :], ALU.subtract)
            owns = owner_cmp[:, :].rearrange("p (t e) -> p t e", e=E - 1)
            link(v.tensor_tensor(owns, tile_ids[:, :].unsqueeze(2).to_broadcast([P, NT, E - 1]),
                                 tile_end[:, 0:E - 1].unsqueeze(1).to_broadcast([P, NT, E - 1]), ALU.is_ge))
            link(v.tensor_reduce(owner_f[:, :], owns, axis=AX.X, op=ALU.add))
            v.tensor_scalar_min(owner[:, :], owner_f[:, :], float(E - 2)).then_inc(route_done, 1)

            def add_shared(n, p):
                wait(dve, sh_y, n + 1)
                rows = resid[:, bass.ds(4 * n, 4), :]
                v.tensor_tensor(rows, rows, (ro if p else pj)[:, :].rearrange("p (b d) -> p b d", d=D), ALU.add).then_inc(sh_add, 1)

            def combine(m, j):
                b = 8 * m + j
                wait(dve, gathered[j % 4], 16 * (2 * m + j // 4 + 1))
                v.scalar_tensor_tensor(out=resid[:, b, :], in0=y_row[:, j % 4, :], scalar=gate[:, bass.ds(b, 1)],
                                       in1=resid[:, b, :], op0=ALU.mult, op1=ALU.add).then_inc(combined, 1)

            def group(n, p, first, last, back=False):
                if not last:
                    for c in range(FC):
                        wait(dve, sh_silu, FC * n + c + 1)
                        wait(dve, sh_y, n - 1)
                        v.tensor_tensor(hidT[:, p, c, :], silu_s[:, c % 2, :], sc[2 + c % 2][:, :], ALU.mult).then_inc(sh_mul, 1)
                        if c == 1 and not first:
                            add_shared(n - 1, 1 - p)
                            if back:
                                wait(dve, sh_add, n)
                        if c >= 2 and back and not first:
                            for j in range(4):
                                combine(n - 1 - NG // 2, 4 * (c - 2) + j)
                else:
                    add_shared(n - 1, 1 - p)
                    if back:
                        wait(dve, sh_add, n)
                        for j in range(8):
                            combine(n - 1 - NG // 2, j)
            run_groups(dve, 0, group)

            def tile(k, p):
                q = 1 - p
                if within(k, 1):
                    wait(dve, t_silu, k)
                    wait(dve, thT_psum, k - 2)
                    v.tensor_tensor(hid[:, q, :], silu_s[:, q, :], sc[2 + q][:, :], ALU.mult).then_inc(t_mul, 1)
                if within(k, 3):
                    wait(dve, ty_psum, k - 2)
                    wait(dve, y_stored[q], 8 * (k - 3) - 8 * q)
                    v.tensor_copy(y_tile[:, q, :], ro[:, 0:D]).then_inc(ty_ready, 1)
            run_tiles(dve, tile)
            run_groups(dve, NG // 2, lambda n, p, first, last: group(n, p, first, last, back=True))

        @block.scalar
        def _(act):
            a = nc.scalar

            def row(v):
                return v.rearrange("(a d) -> a d", a=1).to_broadcast([P, D])
            act.dma_start(b_qk[:, 0:D], row(sbq)).then_inc(w_in, 16)
            act.dma_start(b_qk[:, D:2 * D], row(sbk)).then_inc(w_in, 16)
            act.dma_start(b_cq[:, :], row(cbq.rearrange("h k -> (h k)"))).then_inc(w_in, 16)
            act.dma_start(b_ck[:, :], row(cbk.rearrange("h k -> (h k)"))).then_inc(w_in, 16)
            act.dma_start(b_o[:, 0, :], row(sbo)).then_inc(w_in, 16)
            act.dma_start(b_o[:, 1, :], row(cbo)).then_inc(w_in, 16)
            act.dma_start(bv_col[:, 0:1], sbv.rearrange("(d a) -> d a", a=1)).then_inc(w_in, 16)
            act.dma_start(bv_col[:, 1:2], cbv.rearrange("h k -> (h k)").rearrange("(d a) -> d a", a=1)).then_inc(w_in, 16)
            act.dma_start(resid[:, 6:NB, :], x[6:NB].rearrange("b s d -> s b d")).then_inc(x_tail, 16)
            act.wait_ge(zero_ready, 1)
            act.dma_start(xs[0:NT * P].rearrange("(k p) d -> p k d", p=P),
                          zero_t[:, :].unsqueeze(1).to_broadcast([P, NT, D])).then_inc(zeroed, 16)
            act.dma_start(ys[NT * P:NT * P + P], zero_t[:, :]).then_inc(zeroed, 16)
            act.wait_ge(setup_v, 8)

            def copy(to, of):
                return a.activation(to, of, ACT.Copy)

            def exps(done, scores, lo, prods, t, e, hi, b, u, rows):
                wait(act, scores, 4 * b + u + 1)
                wait(act, lo, 4 * b + u - 1)
                wait(act, prods, 4 * b + u - 1)
                a.activation(e[0:rows, u % 2, :], t[0:rows, :], ACT.Exp)
                a.activation(hi[0:rows, u % 2, :], t[0:rows, :], ACT.Exp).then_inc(done, 1)

            def cexps(i, u):
                if has(i, 4):
                    exps(c2_exp, c2_psum, c2_lo, c2_pv, sc[1 + 2 * (u % 2)], e32c, pr_hic, i - 4, u, C)

            def sexps(i, u):
                if has(i, 1):
                    exps(s2_exp, s2_psum, s2_lo, s2_pv, sc[2 * (u % 2)], e32, pr_hi, i - 1, u, P)

            def twice(t, a0, step):
                return t[:, :, a0:a0 + 2 * step].rearrange("p h (c d) -> p h c d", c=2)[:, :, :, 0:HD]

            def heads2(t):
                return t.rearrange("p (h d) -> p h d", d=HD).unsqueeze(2).to_broadcast([t.shape[0], H, 2, HD])

            def step(i, p):
                q = 1 - p
                if has(i, 2):
                    wait(act, oT_psum, i - 1)
                    copy(oT[:, 0, :], ro[:, 0:P]).then_inc(oT_ready, 1)
                cexps(i, 0)
                if has(i, 0):
                    wait(act, xnT_psum[0], i + 1)
                    copy(xnT[:, 0, :], pj[:, 3 * D:4 * D]).then_inc(xnT_ready[0], 1)
                cexps(i, 1)
                if has(i, 0):
                    wait(act, qkv_psum, i + 1)
                    copy(val[:, p, :, 0:HD], pj[:, 2 * D:3 * D].rearrange("p (h d) -> p h d", d=HD)).then_inc(v_hi, 1)
                cexps(i, 2)
                if has(i, 2):
                    wait(act, xnT_psum[1], i - 1)
                    copy(xnT[:, 1, :], ro[:, 2 * P:3 * P]).then_inc(xnT_ready[1], 1)
                cexps(i, 3)
                if has(i, 0):
                    wait(act, roped_ready, i + 1)
                    copy(twice(stQ[:, p], 0, 2 * HD), heads2(roped[:, p, 0:D]))
                    copy(twice(stK[:, p], 0, HD), heads2(roped[:, p, D:2 * D])).then_inc(qk_hi, 1)
                if has(i, 2):
                    wait(act, q2_ready, i - 1)
                    copy(twice(stQ2[:, p], 0, 2 * HD), heads2(q2[:, :])).then_inc(q2_hi, 1)
                if has(i, 1):
                    wait(act, qmT_psum, i)
                    copy(qmT[:, :], st16[:, 0:4 * P]).then_inc(qmT_ready, 1)
                sexps(i, 0)
                if has(i, 2):
                    wait(act, ctxT_psum, i - 1)
                    copy(ctxT[:, 0:C], pj[:, 3 * D:3 * D + C]).then_inc(ctxT_ready, 1)
                sexps(i, 1)
                if has(i, 2):
                    wait(act, kv2_psum, i - 1)
                    copy(val2[0:C, p, :, 0:HD], pj[0:C, D:2 * D].rearrange("p (h d) -> p h d", d=HD)).then_inc(v2_hi, 1)
                    wait(act, k2_ready, i - 1)
                    copy(twice(stK2[0:C, p], 0, HD), heads2(k2[0:C, :])).then_inc(k2_hi, 1)
                sexps(i, 2)
                if has(i, 4):
                    wait(act, ocT_psum, i - 3)
                    copy(oT[:, 1, :], ro[:, 0:P]).then_inc(ocT_ready, 1)
                if has(i, 2):
                    wait(act, qkT2_psum, i - 1)
                    copy(qkT2[:, p, :], st16[:, 0:4 * P + 4 * CP]).then_inc(qkT2_ready, 1)
                sexps(i, 3)
                if has(i, 4):
                    b = i - 4
                    wait(act, xnT_psum[2], b + 1)
                    wait(act, logits_psum, b)
                    copy(xnT[:, 2, :], ro[:, 2 * P:3 * P]).then_inc(xnT_ready[2], 1)
                    wait(act, xnT_ready[2], b + 1)
                    copy(xn3T[:, b, :], xnT[:, 2, :]).then_inc(xn3T_kept, 1)
                if has(i, 3):
                    wait(act, qmT2_psum, i - 2)
                    copy(qmT2[:, :], st16[:, 0:4 * P]).then_inc(qmT2_ready, 1)
            run(act, step)

            act.wait_ge(shift_ready, 1)
            a.activation(r_exp[:, :], r_shift, ACT.Exp).then_inc(rexp_ready, 1)

            def group(n, p, first, last):
                if not last:
                    for c in range(FC):
                        wait(act, sh_gu, FC * n + c + 1)
                        wait(act, sh_mul, FC * n + c - 1)
                        a.activation(silu_s[:, c % 2, :], sc[c % 2][:, :], ACT.Silu).then_inc(sh_silu, 1)

            def tile(k, p):
                q = 1 - p
                if within(k, 1):
                    wait(act, t_gu, k)
                    wait(act, t_mul, k - 2)
                    a.activation(silu_s[:, q, :], sc[q][:, :], ACT.Silu).then_inc(t_silu, 1)
                if within(k, 0):
                    wait(act, tT_psum, k + 1)
                    copy(xT_tile[:, p, :], st[:, 0:P]).then_inc(tT_ready, 1)
                if within(k, 2):
                    wait(act, thT_psum, k - 1)
                    copy(hT_tile[:, p, :], (pj if p else pv)[:, :]).then_inc(thT_ready, 1)
            run_groups(act, 0, group)
            run_tiles(act, tile)
            run_groups(act, NG // 2, group)

        @block.tensor
        def _(pe):
            t = nc.tensor
            pe.wait_ge(w_in, W_ALL)
            for n in range(3):
                t.transpose(pj[:, n * D:(n + 1) * D], w_load[:, n // 2, n % 2 * D:n % 2 * D + D], id32[:, :])
            t.transpose(ro[:, 0:D], w_load[:, 1, D:2 * D], id32[:, :]).then_inc(setup_pe, 1)
            pe.wait_ge(setup_v, 5)
            t.matmul(ro[:, D:2 * D], bv_bc[:, 0, :], w_o[:, :], start=True, stop=True)
            t.matmul(ro[:, 2 * D:3 * D], bv_bc[:, 1, :], wc_o[:, :], start=True, stop=True).then_inc(setup_pe, 1)
            pe.wait_ge(setup_v, 8)

            def slot(s, j, col, cols, rows):
                return s[SLOT * j:SLOT * j + rows, col:col + cols]

            def masked(bank, mask):
                t.matmul(bank[:, :], idbf[:, :], mask[:, :], start=True, stop=False, skip_group_check=True)

            def sp1(i, u, q):
                if not has(i, 1):
                    return
                b = i - 1
                bank = sc[2 * (u % 2)]
                if u == 0:
                    wait(pe, qkT_ready, b + 1)
                if u < 2:
                    wait(pe, s2_exp, 4 * (b - 1) + 3 + u)
                else:
                    wait(pe, s1_max, 4 * b + u - 1)
                masked(bank, mask_qk)
                for g in range(HG):
                    last = t.matmul(bank[:, g * P:(g + 1) * P], slot(qkT[:, q], u, g * P, P, K1),
                                    slot(qkT[:, q], u, (HG + g) * P, P, K1), start=False, stop=g == HG - 1,
                                    skip_group_check=True)
                last.then_inc(s1_psum, 1)

            def sp2(i, u, q):
                if not has(i, 1):
                    return
                b = i - 1
                bank = sc[2 * (u % 2)]
                if u == 0:
                    wait(pe, qmT_ready, b + 1)
                if u < 2:
                    wait(pe, s1_max, 4 * b + 3 + u)
                else:
                    wait(pe, s2_exp, 4 * b + u - 1)
                masked(bank, mask_kq)
                for g in range(HG):
                    last = t.matmul(bank[:, g * P:(g + 1) * P], slot(qkT[:, q], u, (HG + g) * P, P, K2),
                                    slot(qmT, u, g * P, P, K2), start=False, stop=g == HG - 1,
                                    skip_group_check=True)
                last.then_inc(s2_psum, 1)

            def cp1(i, u, q):
                if not has(i, 3):
                    return
                b = i - 3
                bank = sc[1 + 2 * (u % 2)]
                if u == 0:
                    wait(pe, qkT2_ready, b + 1)
                if u < 2:
                    wait(pe, c2_exp, 4 * (b - 1) + 3 + u)
                else:
                    wait(pe, c1_max, 4 * b + u - 1)
                for g in range(HG):
                    last = t.matmul(bank[:, g * C:(g + 1) * C], slot(qkT2[:, q], u, g * P, P, K1),
                                    slot(qkT2[:, q], u, HG * P + g * CP, C, K1), start=True, stop=True)
                last.then_inc(c1_psum, 1)

            def cp2(i, u, p):
                if not has(i, 4):
                    return
                b = i - 4
                bank = sc[1 + 2 * (u % 2)]
                if u == 0:
                    wait(pe, qmT2_ready, b + 1)
                if u < 2:
                    wait(pe, c1_max, 4 * b + 3 + u)
                else:
                    wait(pe, c2_exp, 4 * b + u - 1)
                for g in range(HG):
                    last = t.matmul(bank[0:C, g * P:(g + 1) * P], slot(qkT2[:, p], u, HG * P + g * CP, C, K2),
                                    slot(qmT2, u, g * P, P, K2), start=True, stop=True)
                last.then_inc(c2_psum, 1)

            def values(lo_ready, done, hi, lo, vals, b, u, rows):
                wait(pe, lo_ready, 4 * b + u + 1)
                for g in range(HG):
                    h = HG * g + u
                    o = pv[:, h * VC:(h + 1) * VC]
                    t.matmul(o, hi[0:rows, u % 2, g * P:(g + 1) * P], vals[0:rows, h, :], start=True, stop=False)
                    last = t.matmul(o, lo[0:rows, u % 2, g * P:(g + 1) * P], vals[0:rows, h, :], start=False, stop=True)
                last.then_inc(done, 1)

            def pvs(i, u, q):
                if has(i, 1):
                    if u == 0:
                        wait(pe, oc_sum, upto(i - 3))
                        wait(pe, qkv_read, i)
                    values(s2_lo, s2_pv, pr_hi, pr_lo, val[:, q], i - 1, u, P)

            def pvc(i, u, p):
                if has(i, 4):
                    if u == 0:
                        wait(pe, o_sum, upto(i - 1))
                        wait(pe, kv2_read, i - 3)
                    values(c2_lo, c2_pv, pr_hic, pr_loc, val2[:, p], i - 4, u, C)

            def project_out(n, psum_o, ready, done, w, b):
                wait(pe, ready, b + 1)
                t.matmul(ro[:, P:2 * P], oT[:, n, :], w[:, :], start=True, stop=True).then_inc(done, 1)

            def stack4(to, stk, p, rows, ident, step, ready=None):
                for g in range(HG):
                    last = t.transpose(st16[:, to + g * step:to + g * step + rows],
                                       stk[0:rows, p, 4 * g:4 * g + 4, :].rearrange("p h s -> p (h s)"),
                                       ident[0:rows, 0:rows])
                return last

            def step(i, p):
                q = 1 - p
                if has(i, 2):
                    b = i - 2
                    wait(pe, o_ready, b + 1)
                    wait(pe, logits_ready, b - 2)
                    t.transpose(ro[:, 0:P], otok[:, 0, p, :], id32[:, :]).then_inc(oT_psum, 1)
                sp1(i, 0, q)
                cp2(i, 0, p)
                if has(i, 0):
                    wait(pe, xn_ready[0], i + 1)
                    wait(pe, kv2_read, i - 2)
                    wait(pe, qkv_read, i)
                    t.transpose(pj[:, 3 * D:4 * D], xn[:, 0, p, :], id32[:, :]).then_inc(xnT_psum[0], 1)
                if has(i, 2):
                    project_out(0, oT_psum, oT_ready, proj_psum, w_o, i - 2)
                sp1(i, 1, q)
                cp2(i, 1, p)
                if has(i, 0):
                    wait(pe, xnT_ready[0], i + 1)
                    t.matmul(pj[:, 0:3 * D], xnT[:, 0, :], w_qkv[:, :], start=True, stop=True).then_inc(qkv_psum, 1)
                pvc(i, 0, p)
                sp1(i, 2, q)
                cp2(i, 2, p)
                if has(i, 2):
                    wait(pe, xn_ready[1], i - 1)
                    t.transpose(ro[:, 2 * P:3 * P], xn[:, 1, p, :], id32[:, :]).then_inc(xnT_psum[1], 1)
                pvc(i, 1, p)
                sp1(i, 3, q)
                cp2(i, 3, p)
                if has(i, 2):
                    wait(pe, xnT_ready[1], i - 1)
                    t.matmul(ro[:, 3 * P:4 * P], xnT[:, 1, :], wc_q[:, :], start=True, stop=True).then_inc(q2_psum, 1)
                pvc(i, 2, p)
                if has(i, 1):
                    wait(pe, m_ready, i)
                    wait(pe, qmT2_ready, i - 3)
                    wait(pe, qkT_ready, i)
                    stack4(0, stQ, q, P, id16, P).then_inc(qmT_psum, 1)
                pvc(i, 3, p)
                sp2(i, 0, q)
                cp1(i, 0, q)
                if has(i, 2):
                    b = i - 2
                    wait(pe, ctx_in_s[p], 8 * b + 16 - 8 * p)
                    wait(pe, qkv_read, upto(b + 3))
                    t.transpose(pj[:, 3 * D:3 * D + C], ctx_t[0:C, p, :], id32[0:C, 0:C]).then_inc(ctxT_psum, 1)
                sp2(i, 1, q)
                cp1(i, 1, q)
                if has(i, 2):
                    wait(pe, ctxT_ready, i - 1)
                    t.matmul(pj[0:C, 0:2 * D], ctxT[:, 0:C], wc_kv[:, :], start=True, stop=True).then_inc(kv2_psum, 1)
                if has(i, 0):
                    wait(pe, qk_lo, i + 1)
                    wait(pe, qmT_ready, i)
                    wait(pe, qkT2_ready, i - 2)
                    stack4(0, stQ, p, P, id16, P)
                    stack4(4 * P, stK, p, P, id16, P).then_inc(qkT_psum, 1)
                pvs(i, 0, q)
                sp2(i, 2, q)
                cp1(i, 2, q)
                if has(i, 4):
                    b = i - 4
                    wait(pe, oc_ready, b + 1)
                    wait(pe, q2_ready, upto(b + 3))
                    t.transpose(ro[:, 0:P], otok[:, 1, p, :], id32[:, :]).then_inc(ocT_psum, 1)
                pvs(i, 1, q)
                sp2(i, 3, q)
                cp1(i, 3, q)
                if has(i, 4):
                    project_out(1, ocT_psum, ocT_ready, projc_psum, wc_o, i - 4)
                if has(i, 2):
                    b = i - 2
                    wait(pe, q2_lo, b + 1)
                    wait(pe, k2_lo, b + 1)
                    wait(pe, qkT_ready, upto(b + 3))
                    stack4(0, stQ2, p, P, id16, P)
                    stack4(4 * P, stK2, p, C, id16, CP).then_inc(qkT2_psum, 1)
                pvs(i, 2, q)
                if has(i, 3):
                    b = i - 3
                    wait(pe, cm_ready, b + 1)
                    wait(pe, qkT2_ready, upto(b + 2))
                    stack4(0, stQ2, q, P, id16, P).then_inc(qmT2_psum, 1)
                if has(i, 4):
                    b = i - 4
                    wait(pe, xn_ready[2], b + 1)
                    t.transpose(ro[:, 2 * P:3 * P], xn[:, 2, p, :], id32[:, :]).then_inc(xnT_psum[2], 1)
                    wait(pe, xnT_ready[2], b + 1)
                    t.matmul(ro[:, 3 * P:3 * P + E], xnT[:, 2, :], w_router[:, :], start=True, stop=True).then_inc(logits_psum, 1)
                pvs(i, 3, q)
            run(pe, step)

            pe.wait_ge(hot_ready, 1)
            t.matmul(sc[0][:, 0:NB * E], earlier[:, :], r_hot16, start=True, stop=True)
            t.matmul(sc[1][:, 0:NB * E], ones16[:, :], r_hot16, start=True, stop=True).then_inc(counts_psum, 1)
            pe.wait_ge(pos_ready, 1)
            pe.wait_ge(w_ffn, 16 * W_FFN)

            def group(n, p, first, last):
                if not last:
                    for c in range(FC):
                        wait(pe, sh_mul, FC * n + c - 1)
                        toks = xn3T[:, bass.ds(4 * n, 4), :].rearrange("p b t -> p (b t)")
                        t.matmul(sc[c % 2][:, :], ws_gate[:, c * P:(c + 1) * P], toks, start=True, stop=True)
                        t.matmul(sc[2 + c % 2][:, :], ws_up[:, c * P:(c + 1) * P], toks, start=True, stop=True).then_inc(sh_gu, 1)
                        if c == 1 and not first:
                            shared_down(n - 1, 1 - p)
                else:
                    shared_down(n - 1, 1 - p)

            def shared_down(n, p):
                wait(pe, sh_mul, FC * n + FC)
                wait(pe, sh_add, n - 1)
                for r in range(4):
                    for c in range(FC):
                        last = t.matmul((ro if p else pj)[:, r * D:(r + 1) * D], hidT[:, p, c, r * P:(r + 1) * P],
                                        ws_down[:, c, :], start=c == 0, stop=c == FC - 1)
                last.then_inc(sh_y, 1)

            def tile(k, p):
                q = 1 - p
                if within(k, 1):
                    e = expert_of(k - 1)
                    wait(pe, tT_ready, k)
                    wait(pe, t_mul, k - 2)
                    t.matmul(sc[q][:, :], xT_tile[:, q, :], w_gate[:, e, :], start=True, stop=True)
                    t.matmul(sc[2 + q][:, :], xT_tile[:, q, :], w_up[:, e, :], start=True, stop=True).then_inc(t_gu, 1)
                if within(k, 0):
                    wait(pe, x_tile_in[p], 8 * k + 16 - 8 * p)
                    wait(pe, tT_ready, k)
                    t.transpose(st[:, 0:P], x_tile[:, p, :], id32[:, :]).then_inc(tT_psum, 1)
                if within(k, 2):
                    wait(pe, t_mul, k - 1)
                    wait(pe, thT_ready, k - 3)
                    for c in range(FC):
                        last = t.transpose((pj if p else pv)[:, c * P:(c + 1) * P], hid[:, p, c * P:(c + 1) * P], id32[:, :])
                    last.then_inc(thT_psum, 1)
                if within(k, 3):
                    e = expert_of(k - 3)
                    wait(pe, thT_ready, k - 2)
                    wait(pe, ty_ready, k - 3)
                    for c in range(FC):
                        last = t.matmul(ro[:, 0:D], hT_tile[:, q, c * P:(c + 1) * P], w_down[:, e, c, :],
                                        start=c == 0, stop=c == FC - 1)
                    last.then_inc(ty_psum, 1)

            def expert_of(k):
                return pe.value_load(owner[0:1, bass.ds(k, 1)], min_val=0, max_val=E - 2)

            run_groups(pe, 0, group)
            pe.wait_ge(route_done, 1)
            pe.wait_ge(w_down_in, 16 * (E - 1))
            pe.wait_ge(sh_add, NG // 2)
            run_tiles(pe, tile)
            pe.wait_ge(ty_ready, NT)
            pe.wait_ge(thT_ready, NT)
            run_groups(pe, NG // 2, group)


def constants(S, NB, E):
    import numpy as np
    half = HD // 2
    freq = (1.0 / np.float32(10000.0) ** (np.arange(half, dtype=np.float32) / np.float32(half))).astype(np.float32)
    ang = np.arange(S, dtype=np.float32)[:, None] * freq[None, :]
    c, s = np.cos(ang), np.sin(ang)
    cos = np.tile(np.concatenate([c, c], 1), (1, H))
    sin = np.tile(np.concatenate([-s, s], 1), (1, H))
    scale = np.float32(float(HD) ** -0.5)
    rows = np.triu(np.full((S, S), -(2.0 ** 100), np.float32), 1)

    def bf16_bits(a):
        return (np.ascontiguousarray(a, np.float32).view(np.uint32) >> 16).astype(np.uint16)

    NT = NB + E - 2
    row = np.concatenate([P * np.arange(NT), np.arange(NT), E - np.arange(E)]).astype(np.float32)
    return {
        "rope_cos": np.concatenate([cos * scale, cos], 1).astype(np.float32),
        "rope_sin": np.concatenate([sin * scale, sin], 1).astype(np.float32),
        "row_consts": np.tile(row, (P, 1)),
        "earlier": np.triu(np.ones((P, P), np.float16), 1),
        "causal_rows": bf16_bits(np.tile(rows, (1, 4))),
        "causal_cols": bf16_bits(np.tile(rows.T, (1, 4))),
        "ident32": np.eye(P, dtype=np.float32),
        "ident16": np.eye(P, dtype=np.float16),
        "identbf": bf16_bits(np.eye(P)),
    }


_INS = (['x', 'ctx_1024']
        + ['L0_attn_' + n for n in ('Wq', 'bq', 'Wk', 'bk', 'Wv', 'bv', 'Wo', 'bo')]
        + ['L0_xattn_' + n for n in ('Wq', 'bq', 'Wk', 'bk', 'Wv', 'bv', 'Wo', 'bo')]
        + ['L0_ffn_' + n for n in ('router_w', 'up_w', 'gate_w', 'down_w',
                                   'shared_up_w', 'shared_gate_w', 'shared_down_w')])


def kernel(**inputs):
    import numpy as _np
    import concourse.bacc as _bacc
    from concourse import mybir as _mybir
    from concourse.bass_utils import run_bass_kernel_spmd as _run

    nc = _bacc.Bacc("TRN2", target_bir_lowering=False, num_devices=1)
    given = {name: _np.ascontiguousarray(inputs[name]) for name in _INS}
    shape = given["x"].shape
    given.update(constants(shape[1], shape[0], given["L0_ffn_router_w"].shape[1]))
    arrays, args = {}, []
    for name, a in given.items():
        arrays[f"in_{name}_dram"] = a
        args.append(nc.dram_tensor(f"in_{name}_dram", a.shape, _mybir.dt.from_np(a.dtype), kind="ExternalInput").ap())
    out = nc.dram_tensor("out_0_dram", shape, _mybir.dt.float32, kind="ExternalOutput").ap()
    decoder_layer(nc, *args, out)
    r = _run(nc, [arrays], core_ids=[0])
    return r.results[0]["out_0_dram"]
```

```python
import concourse.bass as bass
from concourse import mybir
from contextlib import ExitStack

F32 = mybir.dt.float32
F16 = mybir.dt.float16
BF16 = mybir.dt.bfloat16
I32 = mybir.dt.int32
U32 = mybir.dt.uint32
ALU = mybir.AluOpType
ACT = mybir.ActivationFunctionType
AX = mybir.AxisListType

P = 128
H = 16
HD = P // H
SLOT = 32
HG = H * SLOT // P
K1 = 3 * HD
K2 = K1 + 2
VC = 2 * HD + 1
EPS = 1e-5
LAG = 6
LAG_X3 = 5
ARENA = 58 * 1024


def decoder_layer(nc, x, ctx_in, sWq, sbq, sWk, sbk, sWv, sbv, sWo, sbo,
                  cWq, cbq, cWk, cbk, cWv, cbv, cWo, cbo,
                  router_w, up_w, gate_w, down_w, sup_w, sgate_w, sdown_w,
                  rope_cos, rope_sin, row_consts, earlier_in, causal_rows, causal_cols, ident32, ident16, identbf,
                  out):
    NB, S, D = x.shape
    C = ctx_in.shape[1]
    CP = C + C % 2
    QSCALE = float(HD) ** -0.5
    E = router_w.shape[1]
    F = up_w.shape[2]
    FC = F // P
    NG = NB // 4
    NT = NB + E - 2
    ALPHA = 2.0
    assert S == P and D == P and NB % 16 == 0 and F == 4 * P and NT % 2 == 0 and NB * E <= 512

    with ExitStack() as stack:
        def sb(name, shape, dt=F32):
            return stack.enter_context(nc.sbuf_tensor(name, shape, dt))

        def ps(name):
            return stack.enter_context(nc.psum_tensor(name, [P, 512], F32))

        def sem(name):
            return stack.enter_context(nc.semaphore(name))

        arena = sb("arena", [P, ARENA], mybir.dt.uint8)
        taken = [0]

        def carve(shape, dt=F32):
            size = mybir.dt.size(dt)
            for n in shape[1:]:
                size *= n
            at = taken[0]
            taken[0] += (size + 31) // 32 * 32
            assert taken[0] <= ARENA
            flat = arena[:, at:at + size].bitcast(dt)
            names = "abcd"[:len(shape) - 1]
            if len(names) == 1:
                return flat
            return flat.rearrange(f"p ({' '.join(names)}) -> p {' '.join(names)}",
                                  **dict(zip(names[1:], shape[2:])))

        resid = sb("resid", [P, NB, D])
        id32 = sb("id32", [P, P])
        id16 = sb("id16", [P, P], F16)
        idbf = sb("idbf", [P, P], BF16)
        mask_qk = sb("mask_qk", [P, 4 * P], BF16)
        mask_kq = sb("mask_kq", [P, 4 * P], BF16)
        cos = sb("cos", [P, 2 * D])
        sin = sb("sin", [P, 2 * D])
        w_qkv = sb("w_qkv", [P, 3 * D])
        w_o = sb("w_o", [P, D])
        wc_q = sb("wc_q", [P, D])
        wc_kv = sb("wc_kv", [P, 2 * D])
        wc_o = sb("wc_o", [P, D])
        rope_bias = sb("rope_bias", [P, 2 * D])
        b_cqs = sb("b_cqs", [P, D])
        b_ck = sb("b_ck", [P, D])
        out_bias = sb("out_bias", [P, 2, D])
        eps = sb("eps", [P, 1])
        carried = sb("carried", [P, 2])
        neg_half = sb("neg_half", [P, 1])

        bn6 = carve([P, 3, 6])
        mv = carve([P, 3, 2, 2])
        varp = carve([P, 3, 1])
        rstd = carve([P, 3, 2])
        xn = carve([P, 3, 2, D])
        xnT = carve([P, 3, P])
        rot = carve([P, 2, 2 * D])
        rot1 = carve([P, 2 * D])
        roped = carve([P, 2, 2 * D])
        stQ = carve([P, 2, H, SLOT], F16)
        stK = carve([P, 2, H, SLOT], F16)
        qkT = carve([P, 2, 8 * P], F16)
        qmT = carve([P, 4 * P], F16)
        val = carve([P, 2, H, VC], F16)
        nmax = carve([P, 2, H])
        e32 = carve([P, 4, 512])
        pr_hi = carve([P, 4, 512], F16)
        pr_lo = carve([P, 4, 512], F16)
        rsum = carve([P, 2, H])
        oraw = carve([P, 2, D])
        otok = carve([P, 2, 2, D])
        oT = carve([P, 2, P])
        xb = carve([P, 2, 2, D])
        ctx_t = carve([P, 2, D])
        ctxT = carve([P, P])
        q2 = carve([P, D])
        k2 = carve([P, D])
        stQ2 = carve([P, 2, H, SLOT], F16)
        stK2 = carve([P, 2, H, SLOT], F16)
        qkT2 = carve([P, 2, 4 * P + 4 * CP], F16)
        qmT2 = carve([P, 4 * P], F16)
        val2 = carve([P, 2, H, VC], F16)
        nmax2 = carve([P, 2, H])
        w_load = e32
        b_rope = e32[:, 2:4]
        b_qk = rot1
        b_cq = q2
        bv_bc = rot.rearrange("p a (b c) -> p a b c", c=P)[:, :, 0]
        bv_col = mv.rearrange("p a b c -> p (a b c)")[:, 0:2]
        b_o = otok[:, 0]
        xn3T = sb("xn3T", [P, NB, P])

        xn3 = sb("xn3", [P, NB, P])
        logits = sb("logits", [P, NB, E])
        w_router = sb("w_router", [P, E])
        w_gate = sb("w_gate", [P, E - 1, F])
        w_up = sb("w_up", [P, E - 1, F])
        ws_gate = sb("ws_gate", [P, F])
        ws_up = sb("ws_up", [P, F])
        ws_down = sb("ws_down", [P, FC, D])

        attention_end = taken[0]
        taken[0] = 0
        r_shift = carve([P, NB * E])
        r_mark = carve([P, NB * E])
        r_hot = carve([P, NB * E])
        r_run = carve([P, NB * E])
        r_hot16 = carve([P, NB * E], F16)
        r_exp = carve([P, NB * E])
        r_row = carve([P, NB * E])
        owner_cmp = carve([P, NT * (E - 1)])
        top = sb("top", [P, NB])
        gate = sb("gate", [P, NB])
        pos = sb("pos", [P, NB])
        pos_put = sb("pos_put", [P, NB], U32)
        pos_get = sb("pos_get", [P, NB], U32)
        tiles = sb("tiles", [P, E])
        tile_end = sb("tile_end", [P, E])
        tile_start = sb("tile_start", [P, E])
        owner_f = sb("owner_f", [P, NT])
        owner = sb("owner", [P, NT], I32)
        consts = sb("consts", [P, NT + NT + E])
        tile_rows = consts[:, 0:NT]
        tile_ids = consts[:, NT:2 * NT]
        marks = consts[:, 2 * NT:2 * NT + E]
        earlier = sb("earlier", [P, P], F16)
        ones16 = sb("ones16", [P, P], F16)
        ones_f = sb("ones_f", [P, NB])
        zero_t = sb("zero_t", [P, D])

        taken[0] = 0
        w_down = carve([P, E - 1, FC, D])
        y_row = carve([P, 4, D])
        silu_s = carve([P, 2, F])
        hid = carve([P, 2, F])
        hT_tile = carve([P, 2, F])
        hidT = carve([P, 2, FC, 4 * P])
        x_tile = carve([P, 2, D])
        xT_tile = carve([P, 2, D])
        y_tile = carve([P, 2, D])

        xs = nc.dram_tensor("xs", [NT * P + NB * P, D], F32, kind="Internal").ap()
        ys = nc.dram_tensor("ys", [NT * P + P, D], F32, kind="Internal").ap()
        xs_tiles = xs[0:NT * P].rearrange("(k p) d -> k p d", p=P)
        ys_tiles = ys[0:NT * P].rearrange("(k p) d -> k p d", p=P)

        sc = [ps(f"sc{r}") for r in range(4)]
        pj = ps("pj")
        st = ps("st")
        pv = ps("pv")
        ro = ps("ro")
        st16 = st[:, :].bitcast(F16)

        w_in = sem("w_in"); x_head = sem("x_head"); x_tail = sem("x_tail")
        ctx_in_s = [sem("ctx_in0"), sem("ctx_in1")]
        setup_v = sem("setup_v"); setup_pe = sem("setup_pe"); setup_g = sem("setup_g"); setup_a = sem("setup_a")
        ln_stats = [sem(f"ln{n}_stats") for n in (1, 2, 3)]
        ln_mv = [sem(f"ln{n}_mv") for n in (1, 2, 3)]
        ln_var = [sem(f"ln{n}_var") for n in (1, 2, 3)]
        ln_rstd = [sem(f"ln{n}_rstd") for n in (1, 2, 3)]
        xn_ready = [sem(f"xn{n}_ready") for n in (1, 2, 3)]
        xnT_psum = [sem(f"xnT{n}_psum") for n in (1, 2, 3)]
        xnT_ready = [sem(f"xnT{n}_ready") for n in (1, 2, 3)]
        qkv_psum = sem("qkv_psum"); v_hi = sem("v_hi"); qkv_read = sem("qkv_read")
        rot1_ready = sem("rot1_ready"); roped_ready = sem("roped_ready")
        qk_hi = sem("qk_hi"); qk_lo = sem("qk_lo"); qkT_psum = sem("qkT_psum"); qkT_ready = sem("qkT_ready")
        s1_psum = sem("s1_psum"); s1_max = sem("s1_max"); m_hi = sem("m_hi"); m_ready = sem("m_ready")
        qmT_psum = sem("qmT_psum"); qmT_ready = sem("qmT_ready")
        s2_psum = sem("s2_psum"); s2_exp = sem("s2_exp"); s2_lo = sem("s2_lo"); s2_lo_pool = sem("s2_lo_pool"); s2_pv = sem("s2_pv")
        o_sum = sem("o_sum"); o_ready = sem("o_ready"); xb_ready = sem("xb_ready")
        oT_psum = sem("oT_psum"); oT_ready = sem("oT_ready"); proj_psum = sem("proj_psum"); resid1 = sem("resid1")
        q2_psum = sem("q2_psum"); q2_ready = sem("q2_ready"); q2_hi = sem("q2_hi"); q2_lo = sem("q2_lo")
        ctxT_psum = sem("ctxT_psum"); ctxT_ready = sem("ctxT_ready"); kv2_psum = sem("kv2_psum")
        v2_hi = sem("v2_hi"); k2_ready = sem("k2_ready"); k2_hi = sem("k2_hi"); k2_lo = sem("k2_lo")
        qkT2_psum = sem("qkT2_psum"); qkT2_ready = sem("qkT2_ready")
        c1_psum = sem("c1_psum"); c1_max = sem("c1_max"); cm_hi = sem("cm_hi"); cm_ready = sem("cm_ready")
        qmT2_psum = sem("qmT2_psum"); qmT2_ready = sem("qmT2_ready")
        c2_psum = sem("c2_psum"); c2_exp = sem("c2_exp"); c2_lo = sem("c2_lo"); c2_lo_dve = sem("c2_lo_dve"); c2_pv = sem("c2_pv")
        oc_sum = sem("oc_sum"); oc_ready = sem("oc_ready"); xb2_ready = sem("xb2_ready")
        ocT_psum = sem("ocT_psum"); ocT_ready = sem("ocT_ready"); projc_psum = sem("projc_psum"); resid2 = sem("resid2")
        rot_mid = sem("rot_mid"); kv2_read = sem("kv2_read"); logits_psum = sem("logits_psum")
        logits_ready = sem("logits_ready"); xn3T_kept = sem("xn3T_kept")
        xn3_kept = [sem("xn3_kept0"), sem("xn3_kept1")]
        stored = sem("stored")
        w_ffn = sem("w_ffn"); w_down_in = sem("w_down_in"); zeroed = sem("zeroed"); zero_ready = sem("zero_ready")
        route = sem("route"); shift_ready = sem("shift_ready"); rexp_ready = sem("rexp_ready")
        hot_ready = sem("hot_ready"); counts_psum = sem("counts_psum"); pos_ready = sem("pos_ready")
        route_done = sem("route_done"); scattered = sem("scattered")
        gathered = [sem(f"gathered{n}") for n in range(4)]
        combined = sem("combined")
        sh_gu = sem("sh_gu"); sh_silu = sem("sh_silu"); sh_mul = sem("sh_mul"); sh_y = sem("sh_y"); sh_add = sem("sh_add")
        x_tile_in = [sem("x_tile_in0"), sem("x_tile_in1")]
        y_stored = [sem("y_stored0"), sem("y_stored1")]
        tT_psum = sem("tT_psum"); tT_ready = sem("tT_ready"); t_gu = sem("t_gu"); t_silu = sem("t_silu")
        t_mul = sem("t_mul"); thT_psum = sem("thT_psum"); thT_ready = sem("thT_ready")
        ty_psum = sem("ty_psum"); ty_ready = sem("ty_ready")

        block = stack.enter_context(nc.Block())

        def wait(eng, event, count):
            if not (isinstance(count, int) and count <= 0):
                eng.wait_ge(event, count)

        def run(eng, step):
            first = (LAG + 3) // 2
            for i in range(2 * first):
                step(i, i % 2)
            with eng.Fori(first, NB // 2) as pair:
                step(2 * pair, 0)
                step(2 * pair + 1, 1)
            for i in range(NB, NB + LAG):
                step(i, i % 2)

        def has(i, lag):
            return not isinstance(i, int) or 0 <= i - lag < NB

        def at(i, p, lag, piece, *args):
            if has(i, lag):
                piece(i - lag, (p + lag) % 2, *args)

        def turn(eng, b, *users):
            for k, (event, per_row, n) in enumerate(users):
                if isinstance(b, int):
                    wait(eng, event, min(per_row * b + n, per_row * NB))
                elif k == 0:
                    eng.wait_ge(event, per_row * b + n)

        def attention_over(eng):
            eng.wait_ge(logits_ready, NB)
            eng.wait_ge(o_ready, NB)
            eng.wait_ge(xb2_ready, NB)
            eng.wait_ge(xn3T_kept, NB)
            eng.wait_ge(qmT2_ready, NB)
            for par in range(2):
                eng.wait_ge(xn3_kept[par], 16 * (NB // 2))

        def run_groups(eng, lo, group):
            hi = lo + NG // 2
            group(lo, 0, True, False)
            group(lo + 1, 1, False, False)
            if hi - lo > 2:
                with eng.Fori(lo // 2 + 1, hi // 2) as pair:
                    group(2 * pair, 0, False, False)
                    group(2 * pair + 1, 1, False, False)
            group(hi, 0, False, True)

        def run_tiles(eng, tile):
            for k in range(4):
                tile(k, k % 2)
            with eng.Fori(2, NT // 2) as pair:
                tile(2 * pair, 0)
                tile(2 * pair + 1, 1)
            for k in range(NT, NT + 4):
                tile(k, k % 2)

        def within(k, lag):
            return not isinstance(k, int) or 0 <= k - lag < NT

        W_FFN = 2 * (E - 1) + 3
        N_LOADS = 26
        W_ALL = 16 * N_LOADS

        @block.sync
        def _(sync):
            sync.dma_start(resid[:, 0:6, :], x[0:6].rearrange("b s d -> s b d")).then_inc(x_head, 16)
            for n, w in enumerate((sWq, sWk, sWv, sWo)):
                sync.dma_start(w_load[:, n // 2, n % 2 * D:n % 2 * D + D], w).then_inc(w_in, 16)
            sync.dma_start(wc_q[:, :].rearrange("p (h k) -> p h k", k=HD), cWq.rearrange("h d k -> d h k")).then_inc(w_in, 16)
            for n, w in enumerate((cWk, cWv)):
                sync.dma_start(wc_kv[:, n * D:(n + 1) * D].rearrange("p (h k) -> p h k", k=HD),
                               w.rearrange("h d k -> d h k")).then_inc(w_in, 16)
            sync.dma_start(wc_o[:, :], cWo).then_inc(w_in, 16)
            sync.dma_start(w_router[:, :], router_w).then_inc(w_in, 16)
            for t, src in ((cos, rope_cos), (sin, rope_sin), (mask_qk, causal_rows.bitcast(BF16)), (mask_kq, causal_cols.bitcast(BF16)),
                           (consts, row_consts), (earlier, earlier_in),
                           (id32, ident32), (id16, ident16), (idbf, identbf.bitcast(BF16))):
                sync.dma_start(t[:, :], src).then_inc(w_in, 16)
            sync.wait_ge(w_in, W_ALL)
            for e in range(E - 1):
                sync.dma_start(w_gate[:, e, :], gate_w[e]).then_inc(w_ffn, 16)
                sync.dma_start(w_up[:, e, :], up_w[e]).then_inc(w_ffn, 16)
            sync.dma_start(ws_gate[:, :], sgate_w).then_inc(w_ffn, 16)
            sync.dma_start(ws_up[:, :], sup_w).then_inc(w_ffn, 16)
            sync.dma_start(ws_down[:, :, :], sdown_w.rearrange("(c p) d -> p c d", p=P)).then_inc(w_ffn, 16)

            def step(i, p):
                if has(i, 0):
                    wait(sync, ctxT_psum, i - 1)
                    sync.dma_start(ctx_t[0:C, p, :], ctx_in[i]).then_inc(ctx_in_s[p], 16)
                at(i, p, LAG_X3, keep_xn3)

            def keep_xn3(b, p):
                wait(sync, xn_ready[2], b + 1)
                sync.dma_start(xn3[:, b, :], xn[:, 2, p, :]).then_inc(xn3_kept[p], 16)
            run(sync, step)

            attention_over(sync)
            sync.wait_ge(route_done, 1)
            for e in range(E - 1):
                sync.dma_start(w_down[:, e, :, :], down_w[e].rearrange("(c p) d -> p c d", p=P)).then_inc(w_down_in, 16)

            sync.wait_ge(scattered, 16 * NB)

            def tile(k, p):
                if within(k, 0):
                    wait(sync, tT_psum, k - 1)
                    sync.dma_start(x_tile[:, p, :], xs_tiles[k]).then_inc(x_tile_in[p], 16)
                if within(k, 4):
                    wait(sync, ty_ready, k - 3)
                    sync.dma_start(ys_tiles[k - 4], y_tile[:, p, :]).then_inc(y_stored[p], 16)
            run_tiles(sync, tile)

            for n in range(NG):
                sync.wait_ge(combined, 4 * n + 4)
                sync.dma_start(out[4 * n:4 * n + 4].rearrange("b s d -> s b d"),
                               resid[:, 4 * n:4 * n + 4, :]).then_inc(stored, 16)
            sync.wait_ge(stored, 16 * NG)

        @block.gpsimd
        def _(pool):
            g = nc.gpsimd
            pool.wait_ge(setup_v, 8)

            def ln_rstd_of(b, p, n):
                wait(pool, ln_mv[n], b + 1)
                g.tensor_tensor(varp[:, n, :], mv[:, n, p, 1:2], eps[:, :], ALU.add).then_inc(ln_var[n], 1)
                wait(pool, ln_var[n], b + 1)
                g.tensor_tensor(rstd[:, n, p:p + 1], varp[:, n, :], neg_half[:, :], ALU.pow).then_inc(ln_rstd[n], 1)

            def rope_bias_in(b, p):
                wait(pool, rot1_ready, b + 1)
                g.tensor_tensor(rot1[:, :], rot[:, 0, :], rope_bias[:, :], ALU.add).then_inc(rot_mid, 1)

            def rope_sum(b, p):
                wait(pool, rot_mid, b + 1)
                wait(pool, qk_lo, b - 1)
                g.tensor_tensor(roped[:, p, :], rot1[:, :], rot[:, 1, :], ALU.add).then_inc(roped_ready, 1)

            def qk_low(b, p):
                wait(pool, qk_hi, b + 1)
                r = roped[:, p, :].rearrange("p (t h d) -> p t h d", t=2, d=HD)
                g.tensor_tensor(stQ[:, p, :, HD:2 * HD], r[:, 0], stQ[:, p, :, 0:HD], ALU.subtract)
                g.tensor_tensor(stK[:, p, :, 2 * HD:3 * HD], r[:, 1], stK[:, p, :, 0:HD],
                                ALU.subtract).then_inc(qk_lo, 1)

            def q2_low(b, p):
                wait(pool, q2_hi, b + 1)
                g.tensor_tensor(stQ2[:, p, :, HD:2 * HD], q2[:, :].rearrange("p (h d) -> p h d", d=HD),
                                stQ2[:, p, :, 0:HD], ALU.subtract).then_inc(q2_lo, 1)

            def k2_low(b, p):
                wait(pool, k2_hi, b + 1)
                g.tensor_tensor(stK2[0:C, p, :, 2 * HD:3 * HD],
                                k2[0:C, :].rearrange("p (h d) -> p h d", d=HD),
                                stK2[0:C, p, :, 0:HD], ALU.subtract).then_inc(k2_lo, 1)

            def prob_low(b, p, u, exped, done, rows):
                wait(pool, exped, 4 * b + u + 1)
                g.tensor_tensor(pr_lo[0:rows, u, :], e32[0:rows, u, :], pr_hi[0:rows, u, :],
                                ALU.subtract).then_inc(done, 1)

            def add_out_bias(b, p, n):
                if n:
                    wait(pool, resid1, b + 1)
                else:
                    wait(pool, xn_ready[0], b + 1)
                wait(pool, (resid1, resid2)[n], b - 1)
                g.tensor_tensor(xb[:, n, p, :], resid[:, b, :], out_bias[:, n, :],
                                ALU.add).then_inc((xb_ready, xb2_ready)[n], 1)

            def step(i, p):
                at(i, p, 0, ln_rstd_of, 0)
                at(i, p, 4, add_out_bias, 1)
                at(i, p, 0, rope_bias_in)
                at(i, p, 0, rope_sum)
                at(i, p, 1, add_out_bias, 0)
                at(i, p, 0, qk_low)
                at(i, p, 1, prob_low, 3, s2_exp, s2_lo_pool, P)
                at(i, p, 2, q2_low)
                at(i, p, 2, k2_low)
                at(i, p, 3, prob_low, 0, c2_exp, c2_lo, C)
                at(i, p, 3, prob_low, 1, c2_exp, c2_lo, C)
                at(i, p, 3, prob_low, 2, c2_exp, c2_lo, C)
                at(i, p, 4, ln_rstd_of, 2)
                at(i, p, 1, ln_rstd_of, 1)
                at(i, p, 3, prob_low, 3, c2_exp, c2_lo, C)
            run(pool, step)

            pool.wait_ge(zeroed, 32)
            pool.wait_ge(pos_ready, 1)
            for par in range(2):
                pool.wait_ge(xn3_kept[par], 16 * (NB // 2))
            for b in range(NB):
                g.indirect_dma_start(out=xs, out_offset=bass.IndirectOffsetOnAxis(ap=pos_put[:, b:b + 1], axis=0),
                                     in_=xn3[:, b, :], in_offset=None).then_inc(scattered, 16)
            pool.wait_ge(route_done, 1)
            for par in range(2):
                pool.wait_ge(y_stored[par], 16 * (NT // 2))
            for b in range(NB):
                wait(pool, combined, b - 3)
                g.indirect_dma_start(out=y_row[:, b % 4, :], out_offset=None, in_=ys,
                                     in_offset=bass.IndirectOffsetOnAxis(ap=pos_get[:, b:b + 1], axis=0)).then_inc(gathered[b % 4], 16)

        @block.vector
        def _(dve):
            v = nc.vector

            def swapped(t):
                return t.rearrange("p (g t d) -> p g t d", t=2, d=HD // 2)[:, :, ::-1, :]

            def halves(t):
                return t.rearrange("p (g t d) -> p g t d", t=2, d=HD // 2)

            v.memset(zero_t[:, :], 0.0).then_inc(zero_ready, 1)
            v.memset(neg_half[:, :], -0.5)
            v.memset(eps[:, :], EPS)
            v.memset(ones16[:, :], 1.0)
            v.memset(ones_f[:, :], 1.0)
            for t in (stQ, stK, stQ2, stK2):
                v.memset(t[:, :, :, :].rearrange("p a h s -> p (a h s)").bitcast(U32), 0)
            v.memset(val[:, :, :, VC - 1:VC], 1.0)
            v.memset(val2[:, :, :, VC - 1:VC], 1.0).then_inc(setup_v, 1)
            dve.wait_ge(setup_v, 1)
            v.memset(stK[:, :, :, K1:K2], 1.0)
            v.memset(stK2[:, :, :, K1:K2], 1.0).then_inc(setup_v, 1)
            dve.wait_ge(w_in, W_ALL)
            v.tensor_copy(bv_bc[:, 0, :], bv_col[:, 0:1].to_broadcast([P, P]))
            v.tensor_copy(bv_bc[:, 1, :], bv_col[:, 1:2].to_broadcast([P, P]))
            v.tensor_scalar_mul(b_cqs[:, :], b_cq[:, :], QSCALE)
            v.tensor_tensor(b_rope[:, 0, 0:2 * D], b_qk[:, :], cos[:, :], ALU.mult)
            v.tensor_tensor(halves(b_rope[:, 1, 0:2 * D]), swapped(b_qk[:, :]), halves(sin[:, :]),
                            ALU.mult).then_inc(setup_v, 1)
            dve.wait_ge(setup_v, 3)
            v.tensor_tensor(rope_bias[:, :], b_rope[:, 0, 0:2 * D], b_rope[:, 1, 0:2 * D], ALU.add).then_inc(setup_v, 1)
            dve.wait_ge(setup_pe, 1)
            v.tensor_copy(w_qkv[:, :], pj[:, 0:3 * D])
            v.tensor_copy(w_o[:, :], ro[:, 0:D]).then_inc(setup_v, 1)
            dve.wait_ge(setup_pe, 2)
            v.tensor_tensor(out_bias[:, 0, :], ro[:, D:2 * D], b_o[:, 0, :], ALU.add)
            v.tensor_tensor(out_bias[:, 1, :], ro[:, 2 * D:3 * D], b_o[:, 1, :], ALU.add).then_inc(setup_v, 3)
            dve.wait_ge(x_head, 16)

            def carry(n):
                v.tensor_copy(carried[:, n:n + 1], eps[:, :])

            def ln_mean_var(b, p, n):
                if n:
                    wait(dve, (resid1, resid2)[n - 1], b + 1)
                    carry(0)
                v.bn_stats(bn6[:, n, :], resid[:, b, :]).then_inc(ln_stats[n], 1)
                wait(dve, ln_stats[n], b + 1)
                carry(1)
                v.bn_aggr(mv[:, n, p, :], bn6[:, n, :]).then_inc(ln_mv[n], 1)

            def ln_out(b, p, n):
                wait(dve, ln_rstd[n], b + 1)
                wait(dve, xnT_psum[n], b - 1)
                if n == 2:
                    wait(dve, xn3_kept[p], 8 * b - 8 * p)
                v.tensor_scalar(xn[:, n, p, :], resid[:, b, :], mv[:, n, p, 0:1], rstd[:, n, p:p + 1],
                                ALU.subtract, ALU.mult).then_inc(xn_ready[n], 1)

            def rope_products(b, p):
                wait(dve, v_hi, b + 1)
                wait(dve, roped_ready, b)
                v.tensor_tensor(rot[:, 0, :], pj[:, 0:2 * D], cos[:, :], ALU.mult)
                v.tensor_tensor(halves(rot[:, 1, :]), swapped(pj[:, 0:2 * D]), halves(sin[:, :]),
                                ALU.mult).then_inc(rot1_ready, 1)
                v.tensor_tensor(val[:, p, :, HD:2 * HD], pj[:, 2 * D:3 * D].rearrange("p (h d) -> p h d", d=HD),
                                val[:, p, :, 0:HD], ALU.subtract).then_inc(qkv_read, 1)

            def qkT_copy(b, p):
                wait(dve, qkT_psum, b + 1)
                wait(dve, s2_psum, 4 * (b - 1))
                v.tensor_copy(qkT[:, p, :], st16[:, 0:8 * P]).then_inc(qkT_ready, 1)

            def unit_max(b, p, u, bank, scores, done, nm, keys):
                wait(dve, scores, 4 * b + u + 1)
                v.tensor_reduce(nm[:, p, :].rearrange("p (g j) -> p g j", j=4)[:, :, u],
                                bank[:, 0:4 * keys].rearrange("p (g k) -> p g k", k=keys), axis=AX.X, op=ALU.max,
                                negate=True).then_inc(done, 1)

            def max_parts(b, p, done, hi, ready, nm, stk):
                wait(dve, done, 4 * b + 4)
                v.tensor_copy(stk[:, p, :, K1], nm[:, p, :]).then_inc(hi, 1)
                wait(dve, hi, b + 1)
                v.tensor_tensor(stk[:, p, :, K1 + 1], nm[:, p, :], stk[:, p, :, K1], ALU.subtract).then_inc(ready, 1)

            def prob_low(b, p, u, exped, done, rows):
                wait(dve, exped, 4 * b + u + 1)
                v.tensor_tensor(pr_lo[0:rows, u, :], e32[0:rows, u, :], pr_hi[0:rows, u, :],
                                ALU.subtract).then_inc(done, 1)

            def norm(b, p, n, bank):
                prods, summed, ready, moved = ((s2_pv, o_sum, o_ready, oT_psum), (c2_pv, oc_sum, oc_ready, ocT_psum))[n]
                wait(dve, prods, 4 * b + 4)
                parts = bank[:, 0:H * VC].rearrange("p (h c) -> p h c", c=VC)
                v.reciprocal(rsum[:, n, :], parts[:, :, VC - 1])
                v.tensor_reduce(oraw[:, n, :].rearrange("p (h d) -> p h d", d=HD),
                                parts[:, :, 0:2 * HD].rearrange("p h (t d) -> p h d t", t=2), axis=AX.X,
                                op=ALU.add).then_inc(summed, 1)
                wait(dve, summed, b + 1)
                wait(dve, moved, b - 1)
                v.tensor_tensor(otok[:, n, p, :].rearrange("p (h d) -> p h d", d=HD),
                                oraw[:, n, :].rearrange("p (h d) -> p h d", d=HD),
                                rsum[:, n, :].unsqueeze(2).to_broadcast([P, H, HD]), ALU.mult).then_inc(ready, 1)

            def add_residual(b, p, n):
                wait(dve, (proj_psum, projc_psum)[n], b + 1)
                wait(dve, (xb_ready, xb2_ready)[n], b + 1)
                v.tensor_tensor(resid[:, b, :], xb[:, n, p, :], ro[:, P:2 * P],
                                ALU.add).then_inc((resid1, resid2)[n], 1)

            def q2_bias(b, p):
                wait(dve, q2_psum, b + 1)
                wait(dve, q2_lo, b)
                v.scalar_tensor_tensor(out=q2[:, :], in0=ro[:, 3 * P:4 * P], scalar=QSCALE, in1=b_cqs[:, :],
                                       op0=ALU.mult, op1=ALU.add).then_inc(q2_ready, 1)

            def k2_bias(b, p):
                wait(dve, v2_hi, b + 1)
                wait(dve, k2_lo, b)
                v.tensor_tensor(k2[0:C, :], pj[0:C, 0:D], b_ck[0:C, :], ALU.add).then_inc(k2_ready, 1)
                v.tensor_tensor(val2[0:C, p, :, HD:2 * HD], pj[0:C, D:2 * D].rearrange("p (h d) -> p h d", d=HD),
                                val2[0:C, p, :, 0:HD], ALU.subtract).then_inc(kv2_read, 1)

            def logits_copy(b, p):
                wait(dve, logits_psum, b + 1)
                v.tensor_copy(logits[:, b, :], ro[:, 3 * P:3 * P + E]).then_inc(logits_ready, 1)

            def step(i, p):
                if isinstance(i, int) and i == 5:
                    dve.wait_ge(x_tail, 16)
                at(i, p, 0, ln_mean_var, 0)
                at(i, p, 3, unit_max, 2, sc[2], c1_psum, c1_max, nmax2, C)
                at(i, p, 3, unit_max, 3, sc[3], c1_psum, c1_max, nmax2, C)
                at(i, p, 6, logits_copy)
                at(i, p, 0, ln_out, 0)
                at(i, p, 3, max_parts, c1_max, cm_hi, cm_ready, nmax2, stQ2)
                at(i, p, 4, norm, 1, pv)
                at(i, p, 5, ln_out, 2)
                at(i, p, 0, rope_products)
                at(i, p, 1, prob_low, 0, s2_exp, s2_lo, P)
                at(i, p, 1, prob_low, 1, s2_exp, s2_lo, P)
                at(i, p, 1, prob_low, 2, s2_exp, s2_lo, P)
                at(i, p, 2, q2_bias)
                at(i, p, 0, qkT_copy)
                at(i, p, 2, k2_bias)
                at(i, p, 1, norm, 0, pv)
                at(i, p, 4, add_residual, 1)
                at(i, p, 4, ln_mean_var, 2)
                at(i, p, 0, unit_max, 0, sc[0], s1_psum, s1_max, nmax, P)
                at(i, p, 0, unit_max, 1, sc[1], s1_psum, s1_max, nmax, P)
                at(i, p, 0, unit_max, 2, sc[2], s1_psum, s1_max, nmax, P)
                at(i, p, 0, unit_max, 3, sc[0], s1_psum, s1_max, nmax, P)
                at(i, p, 0, max_parts, s1_max, m_hi, m_ready, nmax, stQ)
                at(i, p, 1, add_residual, 0)
                at(i, p, 1, ln_mean_var, 1)
                at(i, p, 2, unit_max, 0, sc[0], c1_psum, c1_max, nmax2, C)
                at(i, p, 2, unit_max, 1, sc[1], c1_psum, c1_max, nmax2, C)
                at(i, p, 1, ln_out, 1)
            run(dve, step)

            attention_over(dve)
            links = [0]

            def link(ins):
                links[0] += 1
                ins.then_inc(route, 1)
                dve.wait_ge(route, links[0])

            def by_row(t):
                return t.rearrange("p (b e) -> p b e", e=E)

            def over_experts(t):
                return t.unsqueeze(2).to_broadcast([P, NB, E])

            link(v.tensor_reduce(top[:, :], logits[:, :, :], axis=AX.X, op=ALU.max))
            v.tensor_tensor(by_row(r_shift), logits[:, :, :], over_experts(top[:, :]), ALU.subtract).then_inc(shift_ready, 1)
            dve.wait_ge(shift_ready, 1)
            link(v.scalar_tensor_tensor(out=by_row(r_mark), in0=by_row(r_shift), scalar=0.0,
                                        in1=marks[:, :].unsqueeze(1).to_broadcast([P, NB, E]), op0=ALU.is_equal, op1=ALU.mult))
            link(v.tensor_reduce(top[:, :], by_row(r_mark), axis=AX.X, op=ALU.max))
            link(v.tensor_tensor(by_row(r_hot), by_row(r_mark), over_experts(top[:, :]), ALU.is_equal))
            v.tensor_copy(r_hot16, r_hot).then_inc(hot_ready, 1)
            dve.wait_ge(rexp_ready, 1)
            link(v.tensor_reduce(top[:, :], by_row(r_exp[:, :]), axis=AX.X, op=ALU.add))
            link(v.reciprocal(gate[:, :], top[:, :]))
            link(v.tensor_scalar_mul(gate[:, :], gate[:, :], ALPHA))
            dve.wait_ge(counts_psum, 1)
            tot = by_row(st[:, 0:NB * E])
            before = by_row(pv[:, 0:NB * E])
            for e in range(E):
                ins = v.tensor_tensor_scan(by_row(r_run)[:, :, e], ones_f[:, 0:NB], tot[:, :, e], 0.0, ALU.mult, ALU.add)
            link(ins)
            by_expert = by_row(r_mark).rearrange("p b e -> p e b")
            v.tensor_tensor(by_expert, by_row(r_run)[:, NB - 1, :].unsqueeze(2).to_broadcast([P, E, NB]),
                            tile_rows[:, 0:NB].unsqueeze(1).to_broadcast([P, E, NB]), ALU.is_gt)
            link(v.tensor_tensor(by_row(r_row[:, :]), by_row(r_run), tot, ALU.subtract))
            v.tensor_reduce(tiles[:, :], by_expert, axis=AX.X, op=ALU.add)
            link(v.tensor_tensor(by_row(r_run), by_row(r_row[:, :]), before, ALU.add))
            link(v.tensor_tensor_scan(tile_end[:, :], ones_f[:, 0:E], tiles[:, :], 0.0, ALU.mult, ALU.add))
            v.memset(tile_start[:, E - 1:E], float(NT))
            link(v.tensor_tensor(tile_start[:, 0:E - 1], tile_end[:, 0:E - 1], tiles[:, 0:E - 1], ALU.subtract))
            link(v.scalar_tensor_tensor(out=by_row(r_row[:, :]), in0=tile_start[:, :].unsqueeze(1).to_broadcast([P, NB, E]),
                                        scalar=float(P), in1=by_row(r_run), op0=ALU.mult, op1=ALU.add))
            link(v.tensor_tensor(r_shift, r_row[:, :], r_hot, ALU.mult))
            link(v.tensor_reduce(pos[:, :], by_row(r_shift), axis=AX.X, op=ALU.add))
            v.tensor_copy(pos_put[:, :], pos[:, :]).then_inc(pos_ready, 1)
            link(v.scalar_tensor_tensor(out=top[:, :], in0=pos[:, :], scalar=float(NT * P), in1=by_row(r_hot)[:, :, E - 1],
                                        op0=ALU.subtract, op1=ALU.mult))
            v.tensor_tensor(pos_get[:, :], pos[:, :], top[:, :], ALU.subtract)
            owns = owner_cmp[:, :].rearrange("p (t e) -> p t e", e=E - 1)
            link(v.tensor_tensor(owns, tile_ids[:, :].unsqueeze(2).to_broadcast([P, NT, E - 1]),
                                 tile_end[:, 0:E - 1].unsqueeze(1).to_broadcast([P, NT, E - 1]), ALU.is_ge))
            link(v.tensor_reduce(owner_f[:, :], owns, axis=AX.X, op=ALU.add))
            v.tensor_scalar_min(owner[:, :], owner_f[:, :], float(E - 2)).then_inc(route_done, 1)

            def add_shared(n, p):
                wait(dve, sh_y, n + 1)
                rows = resid[:, bass.ds(4 * n, 4), :]
                v.tensor_tensor(rows, rows, (ro if p else pj)[:, :].rearrange("p (b d) -> p b d", d=D), ALU.add).then_inc(sh_add, 1)

            def combine(m, j):
                b = 8 * m + j
                wait(dve, gathered[j % 4], 16 * (2 * m + j // 4 + 1))
                v.scalar_tensor_tensor(out=resid[:, b, :], in0=y_row[:, j % 4, :], scalar=gate[:, bass.ds(b, 1)],
                                       in1=resid[:, b, :], op0=ALU.mult, op1=ALU.add).then_inc(combined, 1)

            def group(n, p, first, last, back=False):
                if not last:
                    for c in range(FC):
                        wait(dve, sh_silu, FC * n + c + 1)
                        wait(dve, sh_y, n - 1)
                        v.tensor_tensor(hidT[:, p, c, :], silu_s[:, c % 2, :], sc[2 + c % 2][:, :], ALU.mult).then_inc(sh_mul, 1)
                        if c == 1 and not first:
                            add_shared(n - 1, 1 - p)
                            if back:
                                wait(dve, sh_add, n)
                        if c >= 2 and back and not first:
                            for j in range(4):
                                combine(n - 1 - NG // 2, 4 * (c - 2) + j)
                else:
                    add_shared(n - 1, 1 - p)
                    if back:
                        wait(dve, sh_add, n)
                        for j in range(8):
                            combine(n - 1 - NG // 2, j)
            run_groups(dve, 0, group)

            def tile(k, p):
                q = 1 - p
                if within(k, 1):
                    wait(dve, t_silu, k)
                    wait(dve, thT_psum, k - 2)
                    v.tensor_tensor(hid[:, q, :], silu_s[:, q, :], sc[2 + q][:, :], ALU.mult).then_inc(t_mul, 1)
                if within(k, 3):
                    wait(dve, ty_psum, k - 2)
                    wait(dve, y_stored[q], 8 * (k - 3) - 8 * q)
                    v.tensor_copy(y_tile[:, q, :], ro[:, 0:D]).then_inc(ty_ready, 1)
            run_tiles(dve, tile)
            run_groups(dve, NG // 2, lambda n, p, first, last: group(n, p, first, last, back=True))

        @block.scalar
        def _(act):
            a = nc.scalar

            def row(v):
                return v.rearrange("(a d) -> a d", a=1).to_broadcast([P, D])
            act.dma_start(b_qk[:, 0:D], row(sbq)).then_inc(w_in, 16)
            act.dma_start(b_qk[:, D:2 * D], row(sbk)).then_inc(w_in, 16)
            act.dma_start(b_cq[:, :], row(cbq.rearrange("h k -> (h k)"))).then_inc(w_in, 16)
            act.dma_start(b_ck[:, :], row(cbk.rearrange("h k -> (h k)"))).then_inc(w_in, 16)
            act.dma_start(b_o[:, 0, :], row(sbo)).then_inc(w_in, 16)
            act.dma_start(b_o[:, 1, :], row(cbo)).then_inc(w_in, 16)
            act.dma_start(bv_col[:, 0:1], sbv.rearrange("(d a) -> d a", a=1)).then_inc(w_in, 16)
            act.dma_start(bv_col[:, 1:2], cbv.rearrange("h k -> (h k)").rearrange("(d a) -> d a", a=1)).then_inc(w_in, 16)
            act.wait_ge(w_in, W_ALL)
            act.dma_start(resid[:, 6:NB, :], x[6:NB].rearrange("b s d -> s b d")).then_inc(x_tail, 16)
            act.wait_ge(zero_ready, 1)
            act.dma_start(xs[0:NT * P].rearrange("(k p) d -> p k d", p=P),
                          zero_t[:, :].unsqueeze(1).to_broadcast([P, NT, D])).then_inc(zeroed, 16)
            act.dma_start(ys[NT * P:NT * P + P], zero_t[:, :]).then_inc(zeroed, 16)
            act.wait_ge(setup_v, 8)

            def copy(to, of):
                return a.activation(to, of, ACT.Copy)

            def exps(b, p, u, bank, scores, done, rows, *users):
                wait(act, scores, 4 * b + u + 1)
                turn(act, b, *users)
                a.activation(e32[0:rows, u, :], bank[0:rows, :], ACT.Exp)
                a.activation(pr_hi[0:rows, u, :], bank[0:rows, :], ACT.Exp).then_inc(done, 1)

            def twice(t, a0, step):
                return t[:, :, a0:a0 + 2 * step].rearrange("p h (c d) -> p h c d", c=2)[:, :, :, 0:HD]

            def heads2(t):
                return t.rearrange("p (h d) -> p h d", d=HD).unsqueeze(2).to_broadcast([t.shape[0], H, 2, HD])

            def outT_copy(b, p, n):
                wait(act, (oT_psum, ocT_psum)[n], b + 1)
                copy(oT[:, n, :], ro[:, 0:P]).then_inc((oT_ready, ocT_ready)[n], 1)

            def xnT_copy(b, p, n):
                wait(act, xnT_psum[n], b + 1)
                if n == 2:
                    wait(act, logits_psum, b)
                    wait(act, xn3T_kept, b)
                copy(xnT[:, n, :], (ro[:, 2 * P:3 * P] if n else pj[:, 3 * D:4 * D])).then_inc(xnT_ready[n], 1)

            def keep_xn3T(b, p):
                wait(act, xnT_ready[2], b + 1)
                copy(xn3T[:, b, :], xnT[:, 2, :]).then_inc(xn3T_kept, 1)

            def v_high(b, p):
                wait(act, qkv_psum, b + 1)
                wait(act, s2_pv, 4 * (b - 1))
                copy(val[:, p, :, 0:HD], pj[:, 2 * D:3 * D].rearrange("p (h d) -> p h d", d=HD)).then_inc(v_hi, 1)

            def qk_high(b, p):
                wait(act, roped_ready, b + 1)
                wait(act, qmT_psum, b - 1)
                copy(twice(stQ[:, p], 0, 2 * HD), heads2(roped[:, p, 0:D]))
                copy(twice(stK[:, p], 0, HD), heads2(roped[:, p, D:2 * D])).then_inc(qk_hi, 1)

            def q2_high(b, p):
                wait(act, q2_ready, b + 1)
                wait(act, qmT2_psum, b - 1)
                copy(twice(stQ2[:, p], 0, 2 * HD), heads2(q2[:, :])).then_inc(q2_hi, 1)

            def qmT_copy(b, p):
                wait(act, qmT_psum, b + 1)
                wait(act, s2_psum, 4 * b)
                copy(qmT[:, :], st16[:, 0:4 * P]).then_inc(qmT_ready, 1)

            def ctxT_copy(b, p):
                wait(act, ctxT_psum, b + 1)
                copy(ctxT[:, 0:C], pj[:, 3 * D:3 * D + C]).then_inc(ctxT_ready, 1)

            def v2_high(b, p):
                wait(act, kv2_psum, b + 1)
                wait(act, c2_pv, 4 * (b - 1))
                copy(val2[0:C, p, :, 0:HD], pj[0:C, D:2 * D].rearrange("p (h d) -> p h d", d=HD)).then_inc(v2_hi, 1)

            def k2_high(b, p):
                wait(act, k2_ready, b + 1)
                wait(act, qkT2_psum, b - 1)
                copy(twice(stK2[0:C, p], 0, HD), heads2(k2[0:C, :])).then_inc(k2_hi, 1)

            def qkT2_copy(b, p):
                wait(act, qkT2_psum, b + 1)
                wait(act, c2_psum, 4 * (b - 1))
                copy(qkT2[:, p, :], st16[:, 0:4 * P + 4 * CP]).then_inc(qkT2_ready, 1)

            def qmT2_copy(b, p):
                wait(act, qmT2_psum, b + 1)
                wait(act, c2_psum, 4 * b)
                copy(qmT2[:, :], st16[:, 0:4 * P]).then_inc(qmT2_ready, 1)

            def step(i, p):
                at(i, p, 6, xnT_copy, 2)
                at(i, p, 1, qmT_copy)
                at(i, p, 6, keep_xn3T)
                at(i, p, 0, xnT_copy, 0)
                at(i, p, 1, exps, 0, sc[0], s2_psum, s2_exp, P, (c2_pv, 4, -11), (s2_pv, 4, -3))
                at(i, p, 0, v_high)
                at(i, p, 1, exps, 1, sc[1], s2_psum, s2_exp, P, (c2_pv, 4, -10), (s2_pv, 4, -2))
                at(i, p, 1, exps, 2, sc[2], s2_psum, s2_exp, P, (c2_pv, 4, -9), (s2_pv, 4, -1))
                at(i, p, 2, xnT_copy, 1)
                at(i, p, 2, ctxT_copy)
                at(i, p, 3, qmT2_copy)
                at(i, p, 0, qk_high)
                at(i, p, 1, exps, 3, sc[0], s2_psum, s2_exp, P, (c2_pv, 4, -8), (s2_pv, 4, 0))
                at(i, p, 2, q2_high)
                at(i, p, 2, v2_high)
                at(i, p, 3, exps, 0, sc[1], c2_psum, c2_exp, C, (s2_pv, 4, 9), (c2_pv, 4, -3))
                at(i, p, 4, outT_copy, 1)
                at(i, p, 2, k2_high)
                at(i, p, 3, exps, 1, sc[2], c2_psum, c2_exp, C, (s2_pv, 4, 10), (c2_pv, 4, -2))
                at(i, p, 3, exps, 2, sc[3], c2_psum, c2_exp, C, (s2_pv, 4, 11), (c2_pv, 4, -1))
                at(i, p, 1, outT_copy, 0)
                at(i, p, 2, qkT2_copy)
                at(i, p, 3, exps, 3, pv, c2_psum, c2_exp, C, (s2_pv, 4, 12), (c2_pv, 4, 0))
            run(act, step)

            act.wait_ge(shift_ready, 1)
            a.activation(r_exp[:, :], r_shift, ACT.Exp).then_inc(rexp_ready, 1)

            def group(n, p, first, last):
                if not last:
                    for c in range(FC):
                        wait(act, sh_gu, FC * n + c + 1)
                        wait(act, sh_mul, FC * n + c - 1)
                        a.activation(silu_s[:, c % 2, :], sc[c % 2][:, :], ACT.Silu).then_inc(sh_silu, 1)

            def tile(k, p):
                q = 1 - p
                if within(k, 1):
                    wait(act, t_gu, k)
                    wait(act, t_mul, k - 2)
                    a.activation(silu_s[:, q, :], sc[q][:, :], ACT.Silu).then_inc(t_silu, 1)
                if within(k, 0):
                    wait(act, tT_psum, k + 1)
                    copy(xT_tile[:, p, :], st[:, 0:P]).then_inc(tT_ready, 1)
                if within(k, 2):
                    wait(act, thT_psum, k - 1)
                    copy(hT_tile[:, p, :], (pj if p else pv)[:, :]).then_inc(thT_ready, 1)
            run_groups(act, 0, group)
            run_tiles(act, tile)
            run_groups(act, NG // 2, group)

        @block.tensor
        def _(pe):
            t = nc.tensor
            pe.wait_ge(w_in, W_ALL)
            for n in range(3):
                t.transpose(pj[:, n * D:(n + 1) * D], w_load[:, n // 2, n % 2 * D:n % 2 * D + D], id32[:, :])
            t.transpose(ro[:, 0:D], w_load[:, 1, D:2 * D], id32[:, :]).then_inc(setup_pe, 1)
            pe.wait_ge(setup_v, 5)
            t.matmul(ro[:, D:2 * D], bv_bc[:, 0, :], w_o[:, :], start=True, stop=True)
            t.matmul(ro[:, 2 * D:3 * D], bv_bc[:, 1, :], wc_o[:, :], start=True, stop=True).then_inc(setup_pe, 1)
            pe.wait_ge(setup_v, 8)

            def slot(s, j, col, cols, rows):
                return s[SLOT * j:SLOT * j + rows, col:col + cols]


            def scores_for_max(b, p, u, bank, *users):
                wait(pe, qkT_ready, b + 1)
                turn(pe, b, *users)
                t.matmul(bank[:, :], idbf[:, :], mask_qk[:, :], start=True, stop=False, skip_group_check=True)
                for g in range(HG):
                    last = t.matmul(bank[:, g * P:(g + 1) * P], slot(qkT[:, p], u, g * P, P, K1),
                                    slot(qkT[:, p], u, (HG + g) * P, P, K1), start=False, stop=g == HG - 1,
                                    skip_group_check=True)
                last.then_inc(s1_psum, 1)

            def scores_for_exp(b, p, u, bank, *users):
                wait(pe, qmT_ready, b + 1)
                turn(pe, b, *users)
                t.matmul(bank[:, :], idbf[:, :], mask_kq[:, :], start=True, stop=False, skip_group_check=True)
                for g in range(HG):
                    last = t.matmul(bank[:, g * P:(g + 1) * P], slot(qkT[:, p], u, (HG + g) * P, P, K2),
                                    slot(qmT, u, g * P, P, K2), start=False, stop=g == HG - 1,
                                    skip_group_check=True)
                last.then_inc(s2_psum, 1)

            def cross_for_max(b, p, u, bank, *users):
                wait(pe, qkT2_ready, b + 1)
                turn(pe, b, *users)
                for g in range(HG):
                    last = t.matmul(bank[:, g * C:(g + 1) * C], slot(qkT2[:, p], u, g * P, P, K1),
                                    slot(qkT2[:, p], u, HG * P + g * CP, C, K1), start=True, stop=True)
                last.then_inc(c1_psum, 1)

            def cross_for_exp(b, p, u, bank, *users):
                wait(pe, qmT2_ready, b + 1)
                turn(pe, b, *users)
                for g in range(HG):
                    last = t.matmul(bank[0:C, g * P:(g + 1) * P], slot(qkT2[:, p], u, HG * P + g * CP, C, K2),
                                    slot(qmT2, u, g * P, P, K2), start=True, stop=True)
                last.then_inc(c2_psum, 1)

            def values(b, p, n, u, bank, low_ready, per_row, order, *users):
                vals, rows, done = ((val, P, s2_pv), (val2, C, c2_pv))[n]
                if u == 0:
                    wait(pe, (qkv_read, kv2_read)[n], b + 1)
                    turn(pe, b, *users)
                wait(pe, low_ready, per_row * b + order)
                for g in range(HG):
                    h = HG * g + u
                    o = bank[:, h * VC:(h + 1) * VC]
                    t.matmul(o, pr_hi[0:rows, u, g * P:(g + 1) * P], vals[0:rows, p, h, :], start=True, stop=False)
                    last = t.matmul(o, pr_lo[0:rows, u, g * P:(g + 1) * P], vals[0:rows, p, h, :], start=False, stop=True)
                last.then_inc(done, 1)

            def outT(b, p, n, *users):
                wait(pe, (o_ready, oc_ready)[n], b + 1)
                turn(pe, b, *users)
                t.transpose(ro[:, 0:P], otok[:, n, p, :], id32[:, :]).then_inc((oT_psum, ocT_psum)[n], 1)

            def project_out(b, p, n):
                wait(pe, (oT_ready, ocT_ready)[n], b + 1)
                t.matmul(ro[:, P:2 * P], oT[:, n, :], (w_o, wc_o)[n][:, :], start=True,
                         stop=True).then_inc((proj_psum, projc_psum)[n], 1)

            def xnT_of(b, p, n, *users):
                wait(pe, xn_ready[n], b + 1)
                turn(pe, b, *users)
                t.transpose((ro[:, 2 * P:3 * P] if n else pj[:, 3 * D:4 * D]), xn[:, n, p, :],
                            id32[:, :]).then_inc(xnT_psum[n], 1)

            def project_qkv(b, p):
                wait(pe, xnT_ready[0], b + 1)
                t.matmul(pj[:, 0:3 * D], xnT[:, 0, :], w_qkv[:, :], start=True, stop=True).then_inc(qkv_psum, 1)

            def project_q2(b, p):
                wait(pe, xnT_ready[1], b + 1)
                t.matmul(ro[:, 3 * P:4 * P], xnT[:, 1, :], wc_q[:, :], start=True, stop=True).then_inc(q2_psum, 1)

            def router(b, p):
                wait(pe, xnT_ready[2], b + 1)
                t.matmul(ro[:, 3 * P:3 * P + E], xnT[:, 2, :], w_router[:, :], start=True,
                         stop=True).then_inc(logits_psum, 1)

            def ctxT_of(b, p, *users):
                wait(pe, ctx_in_s[p], 8 * b + 16 - 8 * p)
                turn(pe, b, *users)
                t.transpose(pj[:, 3 * D:3 * D + C], ctx_t[0:C, p, :], id32[0:C, 0:C]).then_inc(ctxT_psum, 1)

            def project_kv2(b, p):
                wait(pe, ctxT_ready, b + 1)
                t.matmul(pj[0:C, 0:2 * D], ctxT[:, 0:C], wc_kv[:, :], start=True, stop=True).then_inc(kv2_psum, 1)

            def stack4(to, stk, p, rows, step):
                for g in range(HG):
                    last = t.transpose(st16[:, to + g * step:to + g * step + rows],
                                       stk[0:rows, p, 4 * g:4 * g + 4, :].rearrange("p h s -> p (h s)"),
                                       id16[0:rows, 0:rows])
                return last

            def stacks(b, p, *users):
                wait(pe, qk_lo, b + 1)
                turn(pe, b, *users)
                stack4(0, stQ, p, P, P)
                stack4(4 * P, stK, p, P, P).then_inc(qkT_psum, 1)

            def stack_max(b, p, *users):
                wait(pe, m_ready, b + 1)
                turn(pe, b, *users)
                stack4(0, stQ, p, P, P).then_inc(qmT_psum, 1)

            def stacks2(b, p, *users):
                wait(pe, q2_lo, b + 1)
                wait(pe, k2_lo, b + 1)
                turn(pe, b, *users)
                stack4(0, stQ2, p, P, P)
                stack4(4 * P, stK2, p, C, CP).then_inc(qkT2_psum, 1)

            def stack_max2(b, p, *users):
                wait(pe, cm_ready, b + 1)
                turn(pe, b, *users)
                stack4(0, stQ2, p, P, P).then_inc(qmT2_psum, 1)

            def step(i, p):
                at(i, p, 1, stack_max, (qkT2_ready, 1, -1), (qkT_ready, 1, 1), (qmT2_ready, 1, -2), (qmT_ready, 1, 0))
                at(i, p, 6, router)
                at(i, p, 4, values, 1, 3, pv, c2_lo, 4, 4)
                at(i, p, 1, scores_for_exp, 0, sc[0], (c1_max, 4, -7), (s1_max, 4, 4), (s2_exp, 4, 0))
                at(i, p, 0, xnT_of, 0, (kv2_read, 1, -2), (qkv_read, 1, 0))
                at(i, p, 1, scores_for_exp, 1, sc[1], (c1_max, 4, -6), (s1_max, 4, 2), (c2_exp, 4, -11), (s2_exp, 4, -2))
                at(i, p, 0, project_qkv)
                at(i, p, 1, scores_for_exp, 2, sc[2], (c1_max, 4, -5), (s1_max, 4, 3), (c2_exp, 4, -10), (s2_exp, 4, -1))
                at(i, p, 1, scores_for_exp, 3, sc[0], (s2_exp, 4, 1), (c1_max, 4, -7), (s1_max, 4, 4))
                at(i, p, 2, xnT_of, 1, (logits_ready, 1, -3), (resid1, 1, 1), (resid2, 1, -2), (q2_ready, 1, 0))
                at(i, p, 3, stack_max2, (qmT_ready, 1, 3), (qkT2_ready, 1, 1), (qkT_ready, 1, 3), (qmT2_ready, 1, 0))
                at(i, p, 2, ctxT_of, (qkv_read, 1, 3), (kv2_read, 1, 0))
                at(i, p, 1, values, 0, 0, pv, s2_lo, 3, 1, (oc_sum, 1, -2), (c2_exp, 4, -8), (o_sum, 1, 0))
                at(i, p, 2, project_q2)
                at(i, p, 1, values, 0, 1, pv, s2_lo, 3, 2)
                at(i, p, 2, project_kv2)
                at(i, p, 1, values, 0, 2, pv, s2_lo, 3, 3)
                at(i, p, 3, cross_for_exp, 0, sc[1], (s2_exp, 4, 10), (c1_max, 4, 2), (s1_max, 4, 10), (c2_exp, 4, -3))
                at(i, p, 3, cross_for_exp, 1, sc[2], (s2_exp, 4, 11), (c1_max, 4, 3), (s1_max, 4, 11), (c2_exp, 4, -2))
                at(i, p, 3, cross_for_exp, 2, sc[3], (c1_max, 4, 4), (c2_exp, 4, -1))
                at(i, p, 4, outT, 1, (q2_ready, 1, 3), (logits_ready, 1, -1), (resid1, 1, 3), (resid2, 1, 0))
                at(i, p, 0, stacks, (qmT2_ready, 1, -2), (qmT_ready, 1, 0), (qkT2_ready, 1, -2), (qkT_ready, 1, 0))
                at(i, p, 1, values, 0, 3, pv, s2_lo_pool, 1, 1)
                at(i, p, 4, project_out, 1)
                at(i, p, 0, scores_for_max, 0, sc[0], (s2_exp, 4, 0), (c1_max, 4, -11), (s1_max, 4, 0))
                at(i, p, 0, scores_for_max, 1, sc[1], (c2_exp, 4, -11), (s2_exp, 4, -2), (c1_max, 4, -10), (s1_max, 4, -2))
                at(i, p, 0, scores_for_max, 2, sc[2], (c2_exp, 4, -10), (s2_exp, 4, -1), (c1_max, 4, -9), (s1_max, 4, -1))
                at(i, p, 0, scores_for_max, 3, sc[0], (s1_max, 4, 1), (s2_exp, 4, 0), (c1_max, 4, -11))
                at(i, p, 1, outT, 0, (resid2, 1, -2), (q2_ready, 1, 0), (logits_ready, 1, -4), (resid1, 1, 0))
                at(i, p, 2, stacks2, (qkT_ready, 1, 3), (qmT2_ready, 1, 0), (qmT_ready, 1, 2), (qkT2_ready, 1, 0))
                at(i, p, 1, project_out, 0)
                at(i, p, 3, cross_for_exp, 3, pv, (o_sum, 1, 3), (oc_sum, 1, 0), (c2_exp, 4, 0))
                at(i, p, 2, cross_for_max, 0, sc[0], (s1_max, 4, 12), (s2_exp, 4, 8), (c1_max, 4, -3))
                at(i, p, 2, cross_for_max, 1, sc[1], (s1_max, 4, 10), (c2_exp, 4, -3), (s2_exp, 4, 6), (c1_max, 4, -2))
                at(i, p, 2, cross_for_max, 2, sc[2], (s1_max, 4, 11), (c2_exp, 4, -2), (s2_exp, 4, 7), (c1_max, 4, -1))
                at(i, p, 2, cross_for_max, 3, sc[3], (c2_exp, 4, -1), (c1_max, 4, 0))
                at(i, p, 3, values, 1, 0, pv, c2_lo, 4, 1, (c2_exp, 4, 4), (o_sum, 1, 3), (oc_sum, 1, 0))
                at(i, p, 3, values, 1, 1, pv, c2_lo, 4, 2)
                at(i, p, 3, values, 1, 2, pv, c2_lo, 4, 3)
                at(i, p, 5, xnT_of, 2, (resid1, 1, 5), (resid2, 1, 2), (q2_ready, 1, 4), (logits_ready, 1, 0))
            run(pe, step)

            pe.wait_ge(hot_ready, 1)
            t.matmul(pv[:, 0:NB * E], earlier[:, :], r_hot16, start=True, stop=True)
            t.matmul(st[:, 0:NB * E], ones16[:, :], r_hot16, start=True, stop=True).then_inc(counts_psum, 1)
            pe.wait_ge(w_ffn, 16 * W_FFN)

            def group(n, p, first, last):
                if not last:
                    for c in range(FC):
                        wait(pe, sh_mul, FC * n + c - 1)
                        toks = xn3T[:, bass.ds(4 * n, 4), :].rearrange("p b t -> p (b t)")
                        t.matmul(sc[c % 2][:, :], ws_gate[:, c * P:(c + 1) * P], toks, start=True, stop=True)
                        t.matmul(sc[2 + c % 2][:, :], ws_up[:, c * P:(c + 1) * P], toks, start=True, stop=True).then_inc(sh_gu, 1)
                        if c == 1 and not first:
                            shared_down(n - 1, 1 - p)
                else:
                    shared_down(n - 1, 1 - p)

            def shared_down(n, p):
                wait(pe, sh_mul, FC * n + FC)
                wait(pe, sh_add, n - 1)
                for r in range(4):
                    for c in range(FC):
                        last = t.matmul((ro if p else pj)[:, r * D:(r + 1) * D], hidT[:, p, c, r * P:(r + 1) * P],
                                        ws_down[:, c, :], start=c == 0, stop=c == FC - 1)
                last.then_inc(sh_y, 1)

            def tile(k, p):
                q = 1 - p
                if within(k, 1):
                    e = expert_of(k - 1)
                    wait(pe, tT_ready, k)
                    wait(pe, t_mul, k - 2)
                    t.matmul(sc[q][:, :], xT_tile[:, q, :], w_gate[:, e, :], start=True, stop=True)
                    t.matmul(sc[2 + q][:, :], xT_tile[:, q, :], w_up[:, e, :], start=True, stop=True).then_inc(t_gu, 1)
                if within(k, 0):
                    wait(pe, x_tile_in[p], 8 * k + 16 - 8 * p)
                    wait(pe, tT_ready, k)
                    t.transpose(st[:, 0:P], x_tile[:, p, :], id32[:, :]).then_inc(tT_psum, 1)
                if within(k, 2):
                    wait(pe, t_mul, k - 1)
                    wait(pe, thT_ready, k - 3)
                    for c in range(FC):
                        last = t.transpose((pj if p else pv)[:, c * P:(c + 1) * P], hid[:, p, c * P:(c + 1) * P], id32[:, :])
                    last.then_inc(thT_psum, 1)
                if within(k, 3):
                    e = expert_of(k - 3)
                    wait(pe, thT_ready, k - 2)
                    wait(pe, ty_ready, k - 3)
                    for c in range(FC):
                        last = t.matmul(ro[:, 0:D], hT_tile[:, q, c * P:(c + 1) * P], w_down[:, e, c, :],
                                        start=c == 0, stop=c == FC - 1)
                    last.then_inc(ty_psum, 1)

            def expert_of(k):
                return pe.value_load(owner[0:1, bass.ds(k, 1)], min_val=0, max_val=E - 2)

            run_groups(pe, 0, group)
            pe.wait_ge(route_done, 1)
            pe.wait_ge(w_down_in, 16 * (E - 1))
            pe.wait_ge(sh_add, NG // 2)
            run_tiles(pe, tile)
            pe.wait_ge(ty_ready, NT)
            pe.wait_ge(thT_ready, NT)
            run_groups(pe, NG // 2, group)


def constants(S, NB, E):
    import numpy as np
    half = HD // 2
    freq = (1.0 / np.float32(10000.0) ** (np.arange(half, dtype=np.float32) / np.float32(half))).astype(np.float32)
    ang = np.arange(S, dtype=np.float32)[:, None] * freq[None, :]
    c, s = np.cos(ang), np.sin(ang)
    cos = np.tile(np.concatenate([c, c], 1), (1, H))
    sin = np.tile(np.concatenate([-s, s], 1), (1, H))
    scale = np.float32(float(HD) ** -0.5)
    rows = np.triu(np.full((S, S), -(2.0 ** 100), np.float32), 1)

    def bf16_bits(a):
        return (np.ascontiguousarray(a, np.float32).view(np.uint32) >> 16).astype(np.uint16)

    NT = NB + E - 2
    row = np.concatenate([P * np.arange(NT), np.arange(NT), E - np.arange(E)]).astype(np.float32)
    return {
        "rope_cos": np.concatenate([cos * scale, cos], 1).astype(np.float32),
        "rope_sin": np.concatenate([sin * scale, sin], 1).astype(np.float32),
        "row_consts": np.tile(row, (P, 1)),
        "earlier": np.triu(np.ones((P, P), np.float16), 1),
        "causal_rows": bf16_bits(np.tile(rows, (1, 4))),
        "causal_cols": bf16_bits(np.tile(rows.T, (1, 4))),
        "ident32": np.eye(P, dtype=np.float32),
        "ident16": np.eye(P, dtype=np.float16),
        "identbf": bf16_bits(np.eye(P)),
    }


_INS = (['x', 'ctx_1024']
        + ['L0_attn_' + n for n in ('Wq', 'bq', 'Wk', 'bk', 'Wv', 'bv', 'Wo', 'bo')]
        + ['L0_xattn_' + n for n in ('Wq', 'bq', 'Wk', 'bk', 'Wv', 'bv', 'Wo', 'bo')]
        + ['L0_ffn_' + n for n in ('router_w', 'up_w', 'gate_w', 'down_w',
                                   'shared_up_w', 'shared_gate_w', 'shared_down_w')])


def kernel(**inputs):
    import numpy as _np
    import concourse.bacc as _bacc
    from concourse import mybir as _mybir
    from concourse.bass_utils import run_bass_kernel_spmd as _run

    nc = _bacc.Bacc("TRN2", target_bir_lowering=False, num_devices=1)
    given = {name: _np.ascontiguousarray(inputs[name]) for name in _INS}
    shape = given["x"].shape
    given.update(constants(shape[1], shape[0], given["L0_ffn_router_w"].shape[1]))
    arrays, args = {}, []
    for name, a in given.items():
        arrays[f"in_{name}_dram"] = a
        args.append(nc.dram_tensor(f"in_{name}_dram", a.shape, _mybir.dt.from_np(a.dtype), kind="ExternalInput").ap())
    out = nc.dram_tensor("out_0_dram", shape, _mybir.dt.float32, kind="ExternalOutput").ap()
    decoder_layer(nc, *args, out)
    r = _run(nc, [arrays], core_ids=[0])
    return r.results[0]["out_0_dram"]
```

```python
import concourse.bass as bass
from concourse import mybir
from contextlib import ExitStack

F32 = mybir.dt.float32
F16 = mybir.dt.float16
BF16 = mybir.dt.bfloat16
I32 = mybir.dt.int32
U32 = mybir.dt.uint32
ALU = mybir.AluOpType
ACT = mybir.ActivationFunctionType
AX = mybir.AxisListType

P = 128
H = 16
HD = P // H
SLOT = 32
HG = H * SLOT // P
K1 = 3 * HD
K2 = K1 + 2
VC = 2 * HD + 1
EPS = 1e-5
LAG = 8
LAG_X3 = 7
ARENA = 58 * 1024


def decoder_layer(nc, x, ctx_in, sWq, sbq, sWk, sbk, sWv, sbv, sWo, sbo,
                  cWq, cbq, cWk, cbk, cWv, cbv, cWo, cbo,
                  router_w, up_w, gate_w, down_w, sup_w, sgate_w, sdown_w,
                  rope_cos, rope_sin, row_consts, earlier_in, causal_rows, causal_cols, ident32, ident16, identbf,
                  out):
    NB, S, D = x.shape
    C = ctx_in.shape[1]
    CP = C + C % 2
    QSCALE = float(HD) ** -0.5
    E = router_w.shape[1]
    F = up_w.shape[2]
    FC = F // P
    NG = NB // 4
    NT = NB + E - 2
    ALPHA = 2.0
    assert S == P and D == P and NB % 16 == 0 and F == 4 * P and NT % 2 == 0 and NB * E <= 512

    with ExitStack() as stack:
        def sb(name, shape, dt=F32):
            return stack.enter_context(nc.sbuf_tensor(name, shape, dt))

        def ps(name):
            return stack.enter_context(nc.psum_tensor(name, [P, 512], F32))

        def sem(name):
            return stack.enter_context(nc.semaphore(name))

        arena = sb("arena", [P, ARENA], mybir.dt.uint8)
        taken = [0]

        def carve(shape, dt=F32):
            size = mybir.dt.size(dt)
            for n in shape[1:]:
                size *= n
            at = taken[0]
            taken[0] += (size + 31) // 32 * 32
            assert taken[0] <= ARENA
            flat = arena[:, at:at + size].bitcast(dt)
            names = "abcd"[:len(shape) - 1]
            if len(names) == 1:
                return flat
            return flat.rearrange(f"p ({' '.join(names)}) -> p {' '.join(names)}",
                                  **dict(zip(names[1:], shape[2:])))

        resid = sb("resid", [P, NB, D])
        id32 = sb("id32", [P, P])
        id16 = sb("id16", [P, P], F16)
        idbf = sb("idbf", [P, P], BF16)
        mask_qk = sb("mask_qk", [P, 4 * P], BF16)
        mask_kq = sb("mask_kq", [P, 4 * P], BF16)
        cos = sb("cos", [P, 2 * D])
        sin = sb("sin", [P, 2 * D])
        w_qkv = sb("w_qkv", [P, 3 * D])
        w_o = sb("w_o", [P, D])
        wc_q = sb("wc_q", [P, D])
        wc_kv = sb("wc_kv", [P, 2 * D])
        wc_o = sb("wc_o", [P, D])
        rope_bias = sb("rope_bias", [P, 2 * D])
        b_cqs = sb("b_cqs", [P, D])
        b_ck = sb("b_ck", [P, D])
        out_bias = sb("out_bias", [P, 2, D])
        eps = sb("eps", [P, 1])
        carried = sb("carried", [P, 2])
        neg_half = sb("neg_half", [P, 1])

        bn6 = carve([P, 3, 2, 6])
        mv = carve([P, 3, 2, 2])
        varp = carve([P, 3, 1])
        rstd = carve([P, 3, 2])
        xn = carve([P, 3, 2, D])
        xnT = carve([P, 3, P])
        rot = carve([P, 2, 2 * D])
        rot1 = carve([P, 2 * D])
        roped = carve([P, 2, 2 * D])
        stQ = carve([P, 2, H, SLOT], F16)
        stK = carve([P, 2, H, SLOT], F16)
        qkT = carve([P, 2, 8 * P], F16)
        qmT = carve([P, 4 * P], F16)
        val = carve([P, 2, H, VC], F16)
        nmax = carve([P, 2, H])
        e32 = carve([P, 4, 512])
        pr_hi = carve([P, 4, 512], F16)
        pr_lo = carve([P, 4, 512], F16)
        rsum = carve([P, 2, H])
        oraw = carve([P, 2, D])
        otok = carve([P, 2, 2, D])
        oT = carve([P, 2, P])
        xb = carve([P, 2, 2, D])
        ctx_t = carve([P, 2, D])
        ctxT = carve([P, P])
        q2 = carve([P, D])
        k2 = carve([P, D])
        stQ2 = carve([P, 2, H, SLOT], F16)
        stK2 = carve([P, 2, H, SLOT], F16)
        qkT2 = carve([P, 2, 4 * P + 4 * CP], F16)
        qmT2 = carve([P, 4 * P], F16)
        val2 = carve([P, 2, H, VC], F16)
        nmax2 = carve([P, 2, H])
        w_load = e32
        b_rope = e32[:, 2:4]
        b_qk = rot1
        b_cq = q2
        bv_bc = rot.rearrange("p a (b c) -> p a b c", c=P)[:, :, 0]
        bv_col = mv.rearrange("p a b c -> p (a b c)")[:, 0:2]
        b_o = otok[:, 0]
        xn3T = sb("xn3T", [P, NB, P])

        xn3 = sb("xn3", [P, NB, P])
        logits = sb("logits", [P, NB, E])
        w_router = sb("w_router", [P, E])
        w_gate = sb("w_gate", [P, E - 1, F])
        w_up = sb("w_up", [P, E - 1, F])
        ws_gate = sb("ws_gate", [P, F])
        ws_up = sb("ws_up", [P, F])
        ws_down = sb("ws_down", [P, FC, D])

        attention_end = taken[0]
        taken[0] = 0
        r_shift = carve([P, NB * E])
        r_mark = carve([P, NB * E])
        r_hot = carve([P, NB * E])
        r_run = carve([P, NB * E])
        r_hot16 = carve([P, NB * E], F16)
        r_exp = carve([P, NB * E])
        r_row = carve([P, NB * E])
        owner_cmp = carve([P, NT * (E - 1)])
        top = sb("top", [P, NB])
        gate = sb("gate", [P, NB])
        pos = sb("pos", [P, NB])
        pos_put = sb("pos_put", [P, NB], U32)
        pos_get = sb("pos_get", [P, NB], U32)
        tiles = sb("tiles", [P, E])
        tile_end = sb("tile_end", [P, E])
        tile_start = sb("tile_start", [P, E])
        owner_f = sb("owner_f", [P, NT])
        owner = sb("owner", [P, NT], I32)
        consts = sb("consts", [P, NT + NT + E])
        tile_rows = consts[:, 0:NT]
        tile_ids = consts[:, NT:2 * NT]
        marks = consts[:, 2 * NT:2 * NT + E]
        earlier = sb("earlier", [P, P], F16)
        ones16 = sb("ones16", [P, P], F16)
        ones_f = sb("ones_f", [P, NB])
        zero_t = sb("zero_t", [P, D])

        taken[0] = 0
        w_down = carve([P, E - 1, FC, D])
        y_row = carve([P, 4, D])
        silu_s = carve([P, 2, F])
        hid = carve([P, 2, F])
        hT_tile = carve([P, 2, F])
        hidT = carve([P, 2, FC, 4 * P])
        x_tile = carve([P, 2, D])
        xT_tile = carve([P, 2, D])
        y_tile = carve([P, 2, D])

        xs = nc.dram_tensor("xs", [NT * P + NB * P, D], F32, kind="Internal").ap()
        ys = nc.dram_tensor("ys", [NT * P + P, D], F32, kind="Internal").ap()
        xs_tiles = xs[0:NT * P].rearrange("(k p) d -> k p d", p=P)
        ys_tiles = ys[0:NT * P].rearrange("(k p) d -> k p d", p=P)

        sc = [ps(f"sc{r}") for r in range(4)]
        pj = ps("pj")
        st = ps("st")
        pv = ps("pv")
        ro = ps("ro")
        st16 = st[:, :].bitcast(F16)

        w_in = sem("w_in"); x_head = sem("x_head"); x_tail = sem("x_tail")
        ctx_in_s = [sem("ctx_in0"), sem("ctx_in1")]
        setup_v = sem("setup_v"); setup_pe = sem("setup_pe"); setup_g = sem("setup_g"); setup_a = sem("setup_a")
        ln_stats = [sem(f"ln{n}_stats") for n in (1, 2, 3)]
        ln_mv = [sem(f"ln{n}_mv") for n in (1, 2, 3)]
        ln_var = [sem(f"ln{n}_var") for n in (1, 2, 3)]
        ln_rstd = [sem(f"ln{n}_rstd") for n in (1, 2, 3)]
        xn_ready = [sem(f"xn{n}_ready") for n in (1, 2, 3)]
        xnT_psum = [sem(f"xnT{n}_psum") for n in (1, 2, 3)]
        xnT_ready = [sem(f"xnT{n}_ready") for n in (1, 2, 3)]
        qkv_psum = sem("qkv_psum"); v_hi = sem("v_hi"); qkv_read = sem("qkv_read")
        rot1_ready = sem("rot1_ready"); roped_ready = sem("roped_ready")
        qk_hi = sem("qk_hi"); qk_lo = sem("qk_lo"); qkT_psum = sem("qkT_psum"); qkT_ready = sem("qkT_ready")
        s1_psum = sem("s1_psum"); s1_max = sem("s1_max"); m_hi = sem("m_hi"); m_ready = sem("m_ready")
        qmT_psum = sem("qmT_psum"); qmT_ready = sem("qmT_ready")
        s2_psum = sem("s2_psum"); s2_exp = sem("s2_exp"); s2_lo = sem("s2_lo"); s2_lo_pool = sem("s2_lo_pool"); s2_pv = sem("s2_pv")
        o_sum = sem("o_sum"); o_ready = sem("o_ready"); xb_ready = sem("xb_ready")
        oT_psum = sem("oT_psum"); oT_ready = sem("oT_ready"); proj_psum = sem("proj_psum"); resid1 = sem("resid1")
        q2_psum = sem("q2_psum"); q2_ready = sem("q2_ready"); q2_hi = sem("q2_hi"); q2_lo = sem("q2_lo")
        ctxT_psum = sem("ctxT_psum"); ctxT_ready = sem("ctxT_ready"); kv2_psum = sem("kv2_psum")
        v2_hi = sem("v2_hi"); k2_ready = sem("k2_ready"); k2_hi = sem("k2_hi"); k2_lo = sem("k2_lo")
        qkT2_psum = sem("qkT2_psum"); qkT2_ready = sem("qkT2_ready")
        c1_psum = sem("c1_psum"); c1_max = sem("c1_max"); cm_hi = sem("cm_hi"); cm_ready = sem("cm_ready")
        qmT2_psum = sem("qmT2_psum"); qmT2_ready = sem("qmT2_ready")
        c2_psum = sem("c2_psum"); c2_exp = sem("c2_exp"); c2_lo = sem("c2_lo"); c2_lo_dve = sem("c2_lo_dve"); c2_pv = sem("c2_pv")
        oc_sum = sem("oc_sum"); oc_ready = sem("oc_ready"); xb2_ready = sem("xb2_ready")
        ocT_psum = sem("ocT_psum"); ocT_ready = sem("ocT_ready"); projc_psum = sem("projc_psum"); resid2 = sem("resid2")
        rot_mid = sem("rot_mid"); kv2_read = sem("kv2_read"); logits_psum = sem("logits_psum")
        logits_ready = sem("logits_ready"); xn3T_kept = sem("xn3T_kept")
        xn3_kept = [sem("xn3_kept0"), sem("xn3_kept1")]
        stored = sem("stored")
        w_ffn = sem("w_ffn"); w_down_in = sem("w_down_in"); zeroed = sem("zeroed"); zero_ready = sem("zero_ready")
        route = sem("route"); shift_ready = sem("shift_ready"); rexp_ready = sem("rexp_ready")
        hot_ready = sem("hot_ready"); counts_psum = sem("counts_psum"); pos_ready = sem("pos_ready")
        route_done = sem("route_done"); scattered = sem("scattered")
        gathered = [sem(f"gathered{n}") for n in range(4)]
        combined = sem("combined")
        sh_gu = sem("sh_gu"); sh_silu = sem("sh_silu"); sh_mul = sem("sh_mul"); sh_y = sem("sh_y"); sh_add = sem("sh_add")
        x_tile_in = [sem("x_tile_in0"), sem("x_tile_in1")]
        y_stored = [sem("y_stored0"), sem("y_stored1")]
        tT_psum = sem("tT_psum"); tT_ready = sem("tT_ready"); t_gu = sem("t_gu"); t_silu = sem("t_silu")
        t_mul = sem("t_mul"); thT_psum = sem("thT_psum"); thT_ready = sem("thT_ready")
        ty_psum = sem("ty_psum"); ty_ready = sem("ty_ready")

        block = stack.enter_context(nc.Block())

        def wait(eng, event, count):
            if not (isinstance(count, int) and count <= 0):
                eng.wait_ge(event, count)

        def run(eng, step):
            first = (LAG + 3) // 2
            for i in range(2 * first):
                step(i, i % 2)
            with eng.Fori(first, NB // 2) as pair:
                step(2 * pair, 0)
                step(2 * pair + 1, 1)
            for i in range(NB, NB + LAG):
                step(i, i % 2)

        def has(i, lag):
            return not isinstance(i, int) or 0 <= i - lag < NB

        def at(i, p, lag, piece, *args):
            if has(i, lag):
                piece(i - lag, (p + lag) % 2, *args)

        def turn(eng, b, *users):
            for k, (event, per_row, n) in enumerate(users):
                if isinstance(b, int):
                    wait(eng, event, min(per_row * b + n, per_row * NB))
                elif k == 0:
                    eng.wait_ge(event, per_row * b + n)

        def attention_over(eng):
            eng.wait_ge(logits_ready, NB)
            eng.wait_ge(o_ready, NB)
            eng.wait_ge(xb2_ready, NB)
            eng.wait_ge(xn3T_kept, NB)
            eng.wait_ge(qmT2_ready, NB)
            for par in range(2):
                eng.wait_ge(xn3_kept[par], 16 * (NB // 2))

        def run_groups(eng, lo, group):
            hi = lo + NG // 2
            group(lo, 0, True, False)
            group(lo + 1, 1, False, False)
            if hi - lo > 2:
                with eng.Fori(lo // 2 + 1, hi // 2) as pair:
                    group(2 * pair, 0, False, False)
                    group(2 * pair + 1, 1, False, False)
            group(hi, 0, False, True)

        def run_tiles(eng, tile):
            for k in range(4):
                tile(k, k % 2)
            with eng.Fori(2, NT // 2) as pair:
                tile(2 * pair, 0)
                tile(2 * pair + 1, 1)
            for k in range(NT, NT + 4):
                tile(k, k % 2)

        def within(k, lag):
            return not isinstance(k, int) or 0 <= k - lag < NT

        W_FFN = 2 * (E - 1) + 3
        N_LOADS = 26
        W_ALL = 16 * N_LOADS

        @block.sync
        def _(sync):
            sync.dma_start(resid[:, 0:6, :], x[0:6].rearrange("b s d -> s b d")).then_inc(x_head, 16)
            for n, w in enumerate((sWq, sWk, sWv, sWo)):
                sync.dma_start(w_load[:, n // 2, n % 2 * D:n % 2 * D + D], w).then_inc(w_in, 16)
            sync.dma_start(wc_q[:, :].rearrange("p (h k) -> p h k", k=HD), cWq.rearrange("h d k -> d h k")).then_inc(w_in, 16)
            for n, w in enumerate((cWk, cWv)):
                sync.dma_start(wc_kv[:, n * D:(n + 1) * D].rearrange("p (h k) -> p h k", k=HD),
                               w.rearrange("h d k -> d h k")).then_inc(w_in, 16)
            sync.dma_start(wc_o[:, :], cWo).then_inc(w_in, 16)
            sync.dma_start(w_router[:, :], router_w).then_inc(w_in, 16)
            for t, src in ((cos, rope_cos), (sin, rope_sin), (mask_qk, causal_rows.bitcast(BF16)), (mask_kq, causal_cols.bitcast(BF16)),
                           (consts, row_consts), (earlier, earlier_in),
                           (id32, ident32), (id16, ident16), (idbf, identbf.bitcast(BF16))):
                sync.dma_start(t[:, :], src).then_inc(w_in, 16)
            sync.wait_ge(w_in, W_ALL)
            for e in range(E - 1):
                sync.dma_start(w_gate[:, e, :], gate_w[e]).then_inc(w_ffn, 16)
                sync.dma_start(w_up[:, e, :], up_w[e]).then_inc(w_ffn, 16)
            sync.dma_start(ws_gate[:, :], sgate_w).then_inc(w_ffn, 16)
            sync.dma_start(ws_up[:, :], sup_w).then_inc(w_ffn, 16)
            sync.dma_start(ws_down[:, :, :], sdown_w.rearrange("(c p) d -> p c d", p=P)).then_inc(w_ffn, 16)

            def step(i, p):
                if has(i, 0):
                    wait(sync, ctxT_psum, i - 1)
                    sync.dma_start(ctx_t[0:C, p, :], ctx_in[i]).then_inc(ctx_in_s[p], 16)
                at(i, p, LAG_X3, keep_xn3)

            def keep_xn3(b, p):
                wait(sync, xn_ready[2], b + 1)
                sync.dma_start(xn3[:, b, :], xn[:, 2, p, :]).then_inc(xn3_kept[p], 16)
            run(sync, step)

            attention_over(sync)
            sync.wait_ge(route_done, 1)
            for e in range(E - 1):
                sync.dma_start(w_down[:, e, :, :], down_w[e].rearrange("(c p) d -> p c d", p=P)).then_inc(w_down_in, 16)

            sync.wait_ge(scattered, 16 * NB)

            def tile(k, p):
                if within(k, 0):
                    wait(sync, tT_psum, k - 1)
                    sync.dma_start(x_tile[:, p, :], xs_tiles[k]).then_inc(x_tile_in[p], 16)
                if within(k, 4):
                    wait(sync, ty_ready, k - 3)
                    sync.dma_start(ys_tiles[k - 4], y_tile[:, p, :]).then_inc(y_stored[p], 16)
            run_tiles(sync, tile)

            for n in range(NG):
                sync.wait_ge(combined, 4 * n + 4)
                sync.dma_start(out[4 * n:4 * n + 4].rearrange("b s d -> s b d"),
                               resid[:, 4 * n:4 * n + 4, :]).then_inc(stored, 16)
            sync.wait_ge(stored, 16 * NG)

        @block.gpsimd
        def _(pool):
            g = nc.gpsimd
            pool.wait_ge(setup_v, 8)

            def ln_rstd_of(b, p, n):
                wait(pool, ln_mv[n], b + 1)
                wait(pool, ln_rstd[n], b)
                g.tensor_tensor(varp[:, n, :], mv[:, n, p, 1:2], eps[:, :], ALU.add).then_inc(ln_var[n], 1)
                wait(pool, ln_var[n], b + 1)
                g.tensor_tensor(rstd[:, n, p:p + 1], varp[:, n, :], neg_half[:, :], ALU.pow).then_inc(ln_rstd[n], 1)

            def rope_bias_in(b, p):
                wait(pool, rot1_ready, b + 1)
                g.tensor_tensor(rot1[:, :], rot[:, 0, :], rope_bias[:, :], ALU.add).then_inc(rot_mid, 1)

            def rope_sum(b, p):
                wait(pool, rot_mid, b + 1)
                wait(pool, qk_lo, b - 1)
                g.tensor_tensor(roped[:, p, :], rot1[:, :], rot[:, 1, :], ALU.add).then_inc(roped_ready, 1)

            def qk_low(b, p):
                wait(pool, qk_hi, b + 1)
                r = roped[:, p, :].rearrange("p (t h d) -> p t h d", t=2, d=HD)
                g.tensor_tensor(stQ[:, p, :, HD:2 * HD], r[:, 0], stQ[:, p, :, 0:HD], ALU.subtract)
                g.tensor_tensor(stK[:, p, :, 2 * HD:3 * HD], r[:, 1], stK[:, p, :, 0:HD],
                                ALU.subtract).then_inc(qk_lo, 1)

            def q2_low(b, p):
                wait(pool, q2_hi, b + 1)
                g.tensor_tensor(stQ2[:, p, :, HD:2 * HD], q2[:, :].rearrange("p (h d) -> p h d", d=HD),
                                stQ2[:, p, :, 0:HD], ALU.subtract).then_inc(q2_lo, 1)

            def k2_low(b, p):
                wait(pool, k2_hi, b + 1)
                g.tensor_tensor(stK2[0:C, p, :, 2 * HD:3 * HD],
                                k2[0:C, :].rearrange("p (h d) -> p h d", d=HD),
                                stK2[0:C, p, :, 0:HD], ALU.subtract).then_inc(k2_lo, 1)

            def prob_low(b, p, u, exped, done, rows):
                wait(pool, exped, 4 * b + u + 1)
                g.tensor_tensor(pr_lo[0:rows, u, :], e32[0:rows, u, :], pr_hi[0:rows, u, :],
                                ALU.subtract).then_inc(done, 1)

            def add_out_bias(b, p, n):
                if n:
                    wait(pool, resid1, b + 1)
                else:
                    wait(pool, xn_ready[0], b + 1)
                wait(pool, (resid1, resid2)[n], b - 1)
                g.tensor_tensor(xb[:, n, p, :], resid[:, b, :], out_bias[:, n, :],
                                ALU.add).then_inc((xb_ready, xb2_ready)[n], 1)

            def step(i, p):
                at(i, p, 6, prob_low, 0, c2_exp, c2_lo, C)
                at(i, p, 5, k2_low)
                at(i, p, 0, ln_rstd_of, 0)
                at(i, p, 5, q2_low)
                at(i, p, 7, ln_rstd_of, 2)
                at(i, p, 6, prob_low, 1, c2_exp, c2_lo, C)
                at(i, p, 6, prob_low, 2, c2_exp, c2_lo, C)
                at(i, p, 4, ln_rstd_of, 1)
                at(i, p, 2, rope_bias_in)
                at(i, p, 6, prob_low, 3, c2_exp, c2_lo, C)
                at(i, p, 2, rope_sum)
                at(i, p, 2, add_out_bias, 0)
                at(i, p, 2, qk_low)
                at(i, p, 5, add_out_bias, 1)
                at(i, p, 3, prob_low, 3, s2_exp, s2_lo_pool, P)
            run(pool, step)

            pool.wait_ge(zeroed, 32)
            pool.wait_ge(pos_ready, 1)
            for par in range(2):
                pool.wait_ge(xn3_kept[par], 16 * (NB // 2))
            for b in range(NB):
                g.indirect_dma_start(out=xs, out_offset=bass.IndirectOffsetOnAxis(ap=pos_put[:, b:b + 1], axis=0),
                                     in_=xn3[:, b, :], in_offset=None).then_inc(scattered, 16)
            pool.wait_ge(route_done, 1)
            for par in range(2):
                pool.wait_ge(y_stored[par], 16 * (NT // 2))
            for b in range(NB):
                wait(pool, combined, b - 3)
                g.indirect_dma_start(out=y_row[:, b % 4, :], out_offset=None, in_=ys,
                                     in_offset=bass.IndirectOffsetOnAxis(ap=pos_get[:, b:b + 1], axis=0)).then_inc(gathered[b % 4], 16)

        @block.vector
        def _(dve):
            v = nc.vector

            def swapped(t):
                return t.rearrange("p (g t d) -> p g t d", t=2, d=HD // 2)[:, :, ::-1, :]

            def halves(t):
                return t.rearrange("p (g t d) -> p g t d", t=2, d=HD // 2)

            v.memset(zero_t[:, :], 0.0).then_inc(zero_ready, 1)
            v.memset(neg_half[:, :], -0.5)
            v.memset(eps[:, :], EPS)
            v.memset(ones16[:, :], 1.0)
            v.memset(ones_f[:, :], 1.0)
            for t in (stQ, stK, stQ2, stK2):
                v.memset(t[:, :, :, :].rearrange("p a h s -> p (a h s)").bitcast(U32), 0)
            v.memset(val[:, :, :, VC - 1:VC], 1.0)
            v.memset(val2[:, :, :, VC - 1:VC], 1.0).then_inc(setup_v, 1)
            dve.wait_ge(setup_v, 1)
            v.memset(stK[:, :, :, K1:K2], 1.0)
            v.memset(stK2[:, :, :, K1:K2], 1.0).then_inc(setup_v, 1)
            dve.wait_ge(w_in, W_ALL)
            v.tensor_copy(bv_bc[:, 0, :], bv_col[:, 0:1].to_broadcast([P, P]))
            v.tensor_copy(bv_bc[:, 1, :], bv_col[:, 1:2].to_broadcast([P, P]))
            v.tensor_scalar_mul(b_cqs[:, :], b_cq[:, :], QSCALE)
            v.tensor_tensor(b_rope[:, 0, 0:2 * D], b_qk[:, :], cos[:, :], ALU.mult)
            v.tensor_tensor(halves(b_rope[:, 1, 0:2 * D]), swapped(b_qk[:, :]), halves(sin[:, :]),
                            ALU.mult).then_inc(setup_v, 1)
            dve.wait_ge(setup_v, 3)
            v.tensor_tensor(rope_bias[:, :], b_rope[:, 0, 0:2 * D], b_rope[:, 1, 0:2 * D], ALU.add).then_inc(setup_v, 1)
            dve.wait_ge(setup_pe, 1)
            v.tensor_copy(w_qkv[:, :], pj[:, 0:3 * D])
            v.tensor_copy(w_o[:, :], ro[:, 0:D]).then_inc(setup_v, 1)
            dve.wait_ge(setup_pe, 2)
            v.tensor_tensor(out_bias[:, 0, :], ro[:, D:2 * D], b_o[:, 0, :], ALU.add)
            v.tensor_tensor(out_bias[:, 1, :], ro[:, 2 * D:3 * D], b_o[:, 1, :], ALU.add).then_inc(setup_v, 3)
            dve.wait_ge(x_head, 16)

            def carry(n):
                v.tensor_copy(carried[:, n:n + 1], eps[:, :])

            def ln_mean_var(b, p, n):
                if n:
                    wait(dve, (resid1, resid2)[n - 1], b + 1)
                    carry(0)
                v.bn_stats(bn6[:, n, p, :], resid[:, b, :]).then_inc(ln_stats[n], 1)
                wait(dve, ln_stats[n], b + 1)
                carry(1)
                v.bn_aggr(mv[:, n, p, :], bn6[:, n, p, :]).then_inc(ln_mv[n], 1)

            def ln_out(b, p, n):
                wait(dve, ln_rstd[n], b + 1)
                wait(dve, xnT_psum[n], b - 1)
                if n == 2:
                    wait(dve, xn3_kept[p], 8 * b - 8 * p)
                v.tensor_scalar(xn[:, n, p, :], resid[:, b, :], mv[:, n, p, 0:1], rstd[:, n, p:p + 1],
                                ALU.subtract, ALU.mult).then_inc(xn_ready[n], 1)

            def rope_products(b, p):
                wait(dve, v_hi, b + 1)
                wait(dve, roped_ready, b)
                v.tensor_tensor(rot[:, 0, :], pj[:, 0:2 * D], cos[:, :], ALU.mult)
                v.tensor_tensor(halves(rot[:, 1, :]), swapped(pj[:, 0:2 * D]), halves(sin[:, :]),
                                ALU.mult).then_inc(rot1_ready, 1)
                v.tensor_tensor(val[:, p, :, HD:2 * HD], pj[:, 2 * D:3 * D].rearrange("p (h d) -> p h d", d=HD),
                                val[:, p, :, 0:HD], ALU.subtract).then_inc(qkv_read, 1)

            def qkT_copy(b, p):
                wait(dve, qkT_psum, b + 1)
                wait(dve, s2_psum, 4 * (b - 1))
                v.tensor_copy(qkT[:, p, :], st16[:, 0:8 * P]).then_inc(qkT_ready, 1)

            def unit_max(b, p, u, bank, scores, done, nm, keys):
                wait(dve, scores, 4 * b + u + 1)
                v.tensor_reduce(nm[:, p, :].rearrange("p (g j) -> p g j", j=4)[:, :, u],
                                bank[:, 0:4 * keys].rearrange("p (g k) -> p g k", k=keys), axis=AX.X, op=ALU.max,
                                negate=True).then_inc(done, 1)

            def max_parts(b, p, done, hi, ready, nm, stk):
                wait(dve, done, 4 * b + 4)
                v.tensor_copy(stk[:, p, :, K1], nm[:, p, :]).then_inc(hi, 1)
                wait(dve, hi, b + 1)
                v.tensor_tensor(stk[:, p, :, K1 + 1], nm[:, p, :], stk[:, p, :, K1], ALU.subtract).then_inc(ready, 1)

            def prob_low(b, p, u, exped, done, rows):
                wait(dve, exped, 4 * b + u + 1)
                v.tensor_tensor(pr_lo[0:rows, u, :], e32[0:rows, u, :], pr_hi[0:rows, u, :],
                                ALU.subtract).then_inc(done, 1)

            def norm(b, p, n, bank):
                prods, summed, ready, moved = ((s2_pv, o_sum, o_ready, oT_psum), (c2_pv, oc_sum, oc_ready, ocT_psum))[n]
                wait(dve, prods, 4 * b + 4)
                parts = bank[:, 0:H * VC].rearrange("p (h c) -> p h c", c=VC)
                v.reciprocal(rsum[:, n, :], parts[:, :, VC - 1])
                v.tensor_reduce(oraw[:, n, :].rearrange("p (h d) -> p h d", d=HD),
                                parts[:, :, 0:2 * HD].rearrange("p h (t d) -> p h d t", t=2), axis=AX.X,
                                op=ALU.add).then_inc(summed, 1)
                wait(dve, summed, b + 1)
                wait(dve, moved, b - 1)
                v.tensor_tensor(otok[:, n, p, :].rearrange("p (h d) -> p h d", d=HD),
                                oraw[:, n, :].rearrange("p (h d) -> p h d", d=HD),
                                rsum[:, n, :].unsqueeze(2).to_broadcast([P, H, HD]), ALU.mult).then_inc(ready, 1)

            def add_residual(b, p, n):
                wait(dve, (proj_psum, projc_psum)[n], b + 1)
                wait(dve, (xb_ready, xb2_ready)[n], b + 1)
                v.tensor_tensor(resid[:, b, :], xb[:, n, p, :], ro[:, P:2 * P],
                                ALU.add).then_inc((resid1, resid2)[n], 1)

            def q2_bias(b, p):
                wait(dve, q2_psum, b + 1)
                wait(dve, q2_lo, b)
                v.scalar_tensor_tensor(out=q2[:, :], in0=ro[:, 3 * P:4 * P], scalar=QSCALE, in1=b_cqs[:, :],
                                       op0=ALU.mult, op1=ALU.add).then_inc(q2_ready, 1)

            def k2_bias(b, p):
                wait(dve, v2_hi, b + 1)
                wait(dve, k2_lo, b)
                v.tensor_tensor(k2[0:C, :], pj[0:C, 0:D], b_ck[0:C, :], ALU.add).then_inc(k2_ready, 1)
                v.tensor_tensor(val2[0:C, p, :, HD:2 * HD], pj[0:C, D:2 * D].rearrange("p (h d) -> p h d", d=HD),
                                val2[0:C, p, :, 0:HD], ALU.subtract).then_inc(kv2_read, 1)

            def logits_copy(b, p):
                wait(dve, logits_psum, b + 1)
                v.tensor_copy(logits[:, b, :], ro[:, 3 * P:3 * P + E]).then_inc(logits_ready, 1)

            def step(i, p):
                if isinstance(i, int) and i == 5:
                    dve.wait_ge(x_tail, 16)
                at(i, p, 0, ln_mean_var, 0)
                at(i, p, 7, add_residual, 1)
                at(i, p, 7, ln_mean_var, 2)
                at(i, p, 3, unit_max, 0, sc[3], s1_psum, s1_max, nmax, P)
                at(i, p, 4, norm, 0, pv)
                at(i, p, 3, unit_max, 1, sc[1], s1_psum, s1_max, nmax, P)
                at(i, p, 0, ln_out, 0)
                at(i, p, 3, unit_max, 2, sc[3], s1_psum, s1_max, nmax, P)
                at(i, p, 3, unit_max, 3, sc[0], s1_psum, s1_max, nmax, P)
                at(i, p, 4, add_residual, 0)
                at(i, p, 3, max_parts, s1_max, m_hi, m_ready, nmax, stQ)
                at(i, p, 4, ln_mean_var, 1)
                at(i, p, 2, rope_products)
                at(i, p, 5, unit_max, 0, sc[3], c1_psum, c1_max, nmax2, C)
                at(i, p, 4, ln_out, 1)
                at(i, p, 5, unit_max, 1, sc[2], c1_psum, c1_max, nmax2, C)
                at(i, p, 5, unit_max, 2, sc[3], c1_psum, c1_max, nmax2, C)
                at(i, p, 8, logits_copy)
                at(i, p, 5, unit_max, 3, sc[0], c1_psum, c1_max, nmax2, C)
                at(i, p, 5, max_parts, c1_max, cm_hi, cm_ready, nmax2, stQ2)
                at(i, p, 6, norm, 1, pv)
                at(i, p, 3, prob_low, 0, s2_exp, s2_lo, P)
                at(i, p, 4, q2_bias)
                at(i, p, 7, ln_out, 2)
                at(i, p, 3, prob_low, 1, s2_exp, s2_lo, P)
                at(i, p, 3, prob_low, 2, s2_exp, s2_lo, P)
                at(i, p, 2, qkT_copy)
                at(i, p, 4, k2_bias)
            run(dve, step)

            attention_over(dve)
            links = [0]

            def link(ins):
                links[0] += 1
                ins.then_inc(route, 1)
                dve.wait_ge(route, links[0])

            def by_row(t):
                return t.rearrange("p (b e) -> p b e", e=E)

            def over_experts(t):
                return t.unsqueeze(2).to_broadcast([P, NB, E])

            link(v.tensor_reduce(top[:, :], logits[:, :, :], axis=AX.X, op=ALU.max))
            v.tensor_tensor(by_row(r_shift), logits[:, :, :], over_experts(top[:, :]), ALU.subtract).then_inc(shift_ready, 1)
            dve.wait_ge(shift_ready, 1)
            link(v.scalar_tensor_tensor(out=by_row(r_mark), in0=by_row(r_shift), scalar=0.0,
                                        in1=marks[:, :].unsqueeze(1).to_broadcast([P, NB, E]), op0=ALU.is_equal, op1=ALU.mult))
            link(v.tensor_reduce(top[:, :], by_row(r_mark), axis=AX.X, op=ALU.max))
            link(v.tensor_tensor(by_row(r_hot), by_row(r_mark), over_experts(top[:, :]), ALU.is_equal))
            v.tensor_copy(r_hot16, r_hot).then_inc(hot_ready, 1)
            dve.wait_ge(rexp_ready, 1)
            link(v.tensor_reduce(top[:, :], by_row(r_exp[:, :]), axis=AX.X, op=ALU.add))
            link(v.reciprocal(gate[:, :], top[:, :]))
            link(v.tensor_scalar_mul(gate[:, :], gate[:, :], ALPHA))
            dve.wait_ge(counts_psum, 1)
            tot = by_row(st[:, 0:NB * E])
            before = by_row(pv[:, 0:NB * E])
            for e in range(E):
                ins = v.tensor_tensor_scan(by_row(r_run)[:, :, e], ones_f[:, 0:NB], tot[:, :, e], 0.0, ALU.mult, ALU.add)
            link(ins)
            by_expert = by_row(r_mark).rearrange("p b e -> p e b")
            v.tensor_tensor(by_expert, by_row(r_run)[:, NB - 1, :].unsqueeze(2).to_broadcast([P, E, NB]),
                            tile_rows[:, 0:NB].unsqueeze(1).to_broadcast([P, E, NB]), ALU.is_gt)
            link(v.tensor_tensor(by_row(r_row[:, :]), by_row(r_run), tot, ALU.subtract))
            v.tensor_reduce(tiles[:, :], by_expert, axis=AX.X, op=ALU.add)
            link(v.tensor_tensor(by_row(r_run), by_row(r_row[:, :]), before, ALU.add))
            link(v.tensor_tensor_scan(tile_end[:, :], ones_f[:, 0:E], tiles[:, :], 0.0, ALU.mult, ALU.add))
            v.memset(tile_start[:, E - 1:E], float(NT))
            link(v.tensor_tensor(tile_start[:, 0:E - 1], tile_end[:, 0:E - 1], tiles[:, 0:E - 1], ALU.subtract))
            link(v.scalar_tensor_tensor(out=by_row(r_row[:, :]), in0=tile_start[:, :].unsqueeze(1).to_broadcast([P, NB, E]),
                                        scalar=float(P), in1=by_row(r_run), op0=ALU.mult, op1=ALU.add))
            link(v.tensor_tensor(r_shift, r_row[:, :], r_hot, ALU.mult))
            link(v.tensor_reduce(pos[:, :], by_row(r_shift), axis=AX.X, op=ALU.add))
            v.tensor_copy(pos_put[:, :], pos[:, :]).then_inc(pos_ready, 1)
            link(v.scalar_tensor_tensor(out=top[:, :], in0=pos[:, :], scalar=float(NT * P), in1=by_row(r_hot)[:, :, E - 1],
                                        op0=ALU.subtract, op1=ALU.mult))
            v.tensor_tensor(pos_get[:, :], pos[:, :], top[:, :], ALU.subtract)
            owns = owner_cmp[:, :].rearrange("p (t e) -> p t e", e=E - 1)
            link(v.tensor_tensor(owns, tile_ids[:, :].unsqueeze(2).to_broadcast([P, NT, E - 1]),
                                 tile_end[:, 0:E - 1].unsqueeze(1).to_broadcast([P, NT, E - 1]), ALU.is_ge))
            link(v.tensor_reduce(owner_f[:, :], owns, axis=AX.X, op=ALU.add))
            v.tensor_scalar_min(owner[:, :], owner_f[:, :], float(E - 2)).then_inc(route_done, 1)

            def add_shared(n, p):
                wait(dve, sh_y, n + 1)
                rows = resid[:, bass.ds(4 * n, 4), :]
                v.tensor_tensor(rows, rows, (ro if p else pj)[:, :].rearrange("p (b d) -> p b d", d=D), ALU.add).then_inc(sh_add, 1)

            def combine(m, j):
                b = 8 * m + j
                wait(dve, gathered[j % 4], 16 * (2 * m + j // 4 + 1))
                v.scalar_tensor_tensor(out=resid[:, b, :], in0=y_row[:, j % 4, :], scalar=gate[:, bass.ds(b, 1)],
                                       in1=resid[:, b, :], op0=ALU.mult, op1=ALU.add).then_inc(combined, 1)

            def group(n, p, first, last, back=False):
                if not last:
                    for c in range(FC):
                        wait(dve, sh_silu, FC * n + c + 1)
                        wait(dve, sh_y, n - 1)
                        v.tensor_tensor(hidT[:, p, c, :], silu_s[:, c % 2, :], sc[2 + c % 2][:, :], ALU.mult).then_inc(sh_mul, 1)
                        if c == 1 and not first:
                            add_shared(n - 1, 1 - p)
                            if back:
                                wait(dve, sh_add, n)
                        if c >= 2 and back and not first:
                            for j in range(4):
                                combine(n - 1 - NG // 2, 4 * (c - 2) + j)
                else:
                    add_shared(n - 1, 1 - p)
                    if back:
                        wait(dve, sh_add, n)
                        for j in range(8):
                            combine(n - 1 - NG // 2, j)
            run_groups(dve, 0, group)

            def tile(k, p):
                q = 1 - p
                if within(k, 1):
                    wait(dve, t_silu, k)
                    wait(dve, thT_psum, k - 2)
                    v.tensor_tensor(hid[:, q, :], silu_s[:, q, :], sc[2 + q][:, :], ALU.mult).then_inc(t_mul, 1)
                if within(k, 3):
                    wait(dve, ty_psum, k - 2)
                    wait(dve, y_stored[q], 8 * (k - 3) - 8 * q)
                    v.tensor_copy(y_tile[:, q, :], ro[:, 0:D]).then_inc(ty_ready, 1)
            run_tiles(dve, tile)
            run_groups(dve, NG // 2, lambda n, p, first, last: group(n, p, first, last, back=True))

        @block.scalar
        def _(act):
            a = nc.scalar

            def row(v):
                return v.rearrange("(a d) -> a d", a=1).to_broadcast([P, D])
            act.dma_start(b_qk[:, 0:D], row(sbq)).then_inc(w_in, 16)
            act.dma_start(b_qk[:, D:2 * D], row(sbk)).then_inc(w_in, 16)
            act.dma_start(b_cq[:, :], row(cbq.rearrange("h k -> (h k)"))).then_inc(w_in, 16)
            act.dma_start(b_ck[:, :], row(cbk.rearrange("h k -> (h k)"))).then_inc(w_in, 16)
            act.dma_start(b_o[:, 0, :], row(sbo)).then_inc(w_in, 16)
            act.dma_start(b_o[:, 1, :], row(cbo)).then_inc(w_in, 16)
            act.dma_start(bv_col[:, 0:1], sbv.rearrange("(d a) -> d a", a=1)).then_inc(w_in, 16)
            act.dma_start(bv_col[:, 1:2], cbv.rearrange("h k -> (h k)").rearrange("(d a) -> d a", a=1)).then_inc(w_in, 16)
            act.wait_ge(w_in, W_ALL)
            act.dma_start(resid[:, 6:NB, :], x[6:NB].rearrange("b s d -> s b d")).then_inc(x_tail, 16)
            act.wait_ge(zero_ready, 1)
            act.dma_start(xs[0:NT * P].rearrange("(k p) d -> p k d", p=P),
                          zero_t[:, :].unsqueeze(1).to_broadcast([P, NT, D])).then_inc(zeroed, 16)
            act.dma_start(ys[NT * P:NT * P + P], zero_t[:, :]).then_inc(zeroed, 16)
            act.wait_ge(setup_v, 8)

            def copy(to, of):
                return a.activation(to, of, ACT.Copy)

            def exps(b, p, u, bank, scores, done, rows, *users):
                wait(act, scores, 4 * b + u + 1)
                turn(act, b, *users)
                a.activation(e32[0:rows, u, :], bank[0:rows, :], ACT.Exp)
                a.activation(pr_hi[0:rows, u, :], bank[0:rows, :], ACT.Exp).then_inc(done, 1)

            def twice(t, a0, step):
                return t[:, :, a0:a0 + 2 * step].rearrange("p h (c d) -> p h c d", c=2)[:, :, :, 0:HD]

            def heads2(t):
                return t.rearrange("p (h d) -> p h d", d=HD).unsqueeze(2).to_broadcast([t.shape[0], H, 2, HD])

            def outT_copy(b, p, n):
                wait(act, (oT_psum, ocT_psum)[n], b + 1)
                copy(oT[:, n, :], ro[:, 0:P]).then_inc((oT_ready, ocT_ready)[n], 1)

            def xnT_copy(b, p, n):
                wait(act, xnT_psum[n], b + 1)
                if n == 2:
                    wait(act, logits_psum, b)
                    wait(act, xn3T_kept, b)
                copy(xnT[:, n, :], (ro[:, 2 * P:3 * P] if n else pj[:, 3 * D:4 * D])).then_inc(xnT_ready[n], 1)

            def keep_xn3T(b, p):
                wait(act, xnT_ready[2], b + 1)
                copy(xn3T[:, b, :], xnT[:, 2, :]).then_inc(xn3T_kept, 1)

            def v_high(b, p):
                wait(act, qkv_psum, b + 1)
                wait(act, s2_pv, 4 * (b - 1))
                copy(val[:, p, :, 0:HD], pj[:, 2 * D:3 * D].rearrange("p (h d) -> p h d", d=HD)).then_inc(v_hi, 1)

            def qk_high(b, p):
                wait(act, roped_ready, b + 1)
                wait(act, qmT_psum, b - 1)
                copy(twice(stQ[:, p], 0, 2 * HD), heads2(roped[:, p, 0:D]))
                copy(twice(stK[:, p], 0, HD), heads2(roped[:, p, D:2 * D])).then_inc(qk_hi, 1)

            def q2_high(b, p):
                wait(act, q2_ready, b + 1)
                wait(act, qmT2_psum, b - 1)
                copy(twice(stQ2[:, p], 0, 2 * HD), heads2(q2[:, :])).then_inc(q2_hi, 1)

            def qmT_copy(b, p):
                wait(act, qmT_psum, b + 1)
                wait(act, s2_psum, 4 * b)
                copy(qmT[:, :], st16[:, 0:4 * P]).then_inc(qmT_ready, 1)

            def ctxT_copy(b, p):
                wait(act, ctxT_psum, b + 1)
                copy(ctxT[:, 0:C], pj[:, 3 * D:3 * D + C]).then_inc(ctxT_ready, 1)

            def v2_high(b, p):
                wait(act, kv2_psum, b + 1)
                wait(act, c2_pv, 4 * (b - 1))
                copy(val2[0:C, p, :, 0:HD], pj[0:C, D:2 * D].rearrange("p (h d) -> p h d", d=HD)).then_inc(v2_hi, 1)

            def k2_high(b, p):
                wait(act, k2_ready, b + 1)
                wait(act, qkT2_psum, b - 1)
                copy(twice(stK2[0:C, p], 0, HD), heads2(k2[0:C, :])).then_inc(k2_hi, 1)

            def qkT2_copy(b, p):
                wait(act, qkT2_psum, b + 1)
                wait(act, c2_psum, 4 * (b - 1))
                copy(qkT2[:, p, :], st16[:, 0:4 * P + 4 * CP]).then_inc(qkT2_ready, 1)

            def qmT2_copy(b, p):
                wait(act, qmT2_psum, b + 1)
                wait(act, c2_psum, 4 * b)
                copy(qmT2[:, :], st16[:, 0:4 * P]).then_inc(qmT2_ready, 1)

            def step(i, p):
                at(i, p, 5, k2_high)
                at(i, p, 5, q2_high)
                at(i, p, 6, exps, 1, sc[0], c2_psum, c2_exp, C, (s2_pv, 4, 10), (c2_pv, 4, -2))
                at(i, p, 2, xnT_copy, 0)
                at(i, p, 6, exps, 2, sc[2], c2_psum, c2_exp, C, (s2_pv, 4, 11), (c2_pv, 4, -1))
                at(i, p, 4, outT_copy, 0)
                at(i, p, 5, qkT2_copy)
                at(i, p, 2, v_high)
                at(i, p, 3, qmT_copy)
                at(i, p, 8, xnT_copy, 2)
                at(i, p, 6, exps, 3, sc[0], c2_psum, c2_exp, C, (s2_pv, 4, 12), (c2_pv, 4, 0))
                at(i, p, 8, keep_xn3T)
                at(i, p, 3, exps, 0, sc[1], s2_psum, s2_exp, P, (c2_pv, 4, -11), (s2_pv, 4, -3))
                at(i, p, 4, xnT_copy, 1)
                at(i, p, 2, qk_high)
                at(i, p, 3, exps, 1, sc[2], s2_psum, s2_exp, P, (c2_pv, 4, -10), (s2_pv, 4, -2))
                at(i, p, 4, ctxT_copy)
                at(i, p, 5, qmT2_copy)
                at(i, p, 3, exps, 2, sc[3], s2_psum, s2_exp, P, (c2_pv, 4, -9), (s2_pv, 4, -1))
                at(i, p, 3, exps, 3, sc[1], s2_psum, s2_exp, P, (c2_pv, 4, -8), (s2_pv, 4, 0))
                at(i, p, 6, outT_copy, 1)
                at(i, p, 4, v2_high)
                at(i, p, 5, exps, 0, sc[0], c2_psum, c2_exp, C, (s2_pv, 4, 9), (c2_pv, 4, -3))
            run(act, step)

            act.wait_ge(shift_ready, 1)
            a.activation(r_exp[:, :], r_shift, ACT.Exp).then_inc(rexp_ready, 1)

            def group(n, p, first, last):
                if not last:
                    for c in range(FC):
                        wait(act, sh_gu, FC * n + c + 1)
                        wait(act, sh_mul, FC * n + c - 1)
                        a.activation(silu_s[:, c % 2, :], sc[c % 2][:, :], ACT.Silu).then_inc(sh_silu, 1)

            def tile(k, p):
                q = 1 - p
                if within(k, 1):
                    wait(act, t_gu, k)
                    wait(act, t_mul, k - 2)
                    a.activation(silu_s[:, q, :], sc[q][:, :], ACT.Silu).then_inc(t_silu, 1)
                if within(k, 0):
                    wait(act, tT_psum, k + 1)
                    copy(xT_tile[:, p, :], st[:, 0:P]).then_inc(tT_ready, 1)
                if within(k, 2):
                    wait(act, thT_psum, k - 1)
                    copy(hT_tile[:, p, :], (pj if p else pv)[:, :]).then_inc(thT_ready, 1)
            run_groups(act, 0, group)
            run_tiles(act, tile)
            run_groups(act, NG // 2, group)

        @block.tensor
        def _(pe):
            t = nc.tensor
            pe.wait_ge(w_in, W_ALL)
            for n in range(3):
                t.transpose(pj[:, n * D:(n + 1) * D], w_load[:, n // 2, n % 2 * D:n % 2 * D + D], id32[:, :])
            t.transpose(ro[:, 0:D], w_load[:, 1, D:2 * D], id32[:, :]).then_inc(setup_pe, 1)
            pe.wait_ge(setup_v, 5)
            t.matmul(ro[:, D:2 * D], bv_bc[:, 0, :], w_o[:, :], start=True, stop=True)
            t.matmul(ro[:, 2 * D:3 * D], bv_bc[:, 1, :], wc_o[:, :], start=True, stop=True).then_inc(setup_pe, 1)
            pe.wait_ge(setup_v, 8)

            def slot(s, j, col, cols, rows):
                return s[SLOT * j:SLOT * j + rows, col:col + cols]


            def scores_for_max(b, p, u, bank, *users):
                wait(pe, qkT_ready, b + 1)
                turn(pe, b, *users)
                t.matmul(bank[:, :], idbf[:, :], mask_qk[:, :], start=True, stop=False, skip_group_check=True)
                for g in range(HG):
                    last = t.matmul(bank[:, g * P:(g + 1) * P], slot(qkT[:, p], u, g * P, P, K1),
                                    slot(qkT[:, p], u, (HG + g) * P, P, K1), start=False, stop=g == HG - 1,
                                    skip_group_check=True)
                last.then_inc(s1_psum, 1)

            def scores_for_exp(b, p, u, bank, *users):
                wait(pe, qmT_ready, b + 1)
                turn(pe, b, *users)
                t.matmul(bank[:, :], idbf[:, :], mask_kq[:, :], start=True, stop=False, skip_group_check=True)
                for g in range(HG):
                    last = t.matmul(bank[:, g * P:(g + 1) * P], slot(qkT[:, p], u, (HG + g) * P, P, K2),
                                    slot(qmT, u, g * P, P, K2), start=False, stop=g == HG - 1,
                                    skip_group_check=True)
                last.then_inc(s2_psum, 1)

            def cross_for_max(b, p, u, bank, *users):
                wait(pe, qkT2_ready, b + 1)
                turn(pe, b, *users)
                for g in range(HG):
                    last = t.matmul(bank[:, g * C:(g + 1) * C], slot(qkT2[:, p], u, g * P, P, K1),
                                    slot(qkT2[:, p], u, HG * P + g * CP, C, K1), start=True, stop=True)
                last.then_inc(c1_psum, 1)

            def cross_for_exp(b, p, u, bank, *users):
                wait(pe, qmT2_ready, b + 1)
                turn(pe, b, *users)
                for g in range(HG):
                    last = t.matmul(bank[0:C, g * P:(g + 1) * P], slot(qkT2[:, p], u, HG * P + g * CP, C, K2),
                                    slot(qmT2, u, g * P, P, K2), start=True, stop=True)
                last.then_inc(c2_psum, 1)

            def values(b, p, n, u, bank, low_ready, per_row, order, *users):
                vals, rows, done = ((val, P, s2_pv), (val2, C, c2_pv))[n]
                if u == 0:
                    wait(pe, (qkv_read, kv2_read)[n], b + 1)
                    turn(pe, b, *users)
                wait(pe, low_ready, per_row * b + order)
                for g in range(HG):
                    h = HG * g + u
                    o = bank[:, h * VC:(h + 1) * VC]
                    t.matmul(o, pr_hi[0:rows, u, g * P:(g + 1) * P], vals[0:rows, p, h, :], start=True, stop=False)
                    last = t.matmul(o, pr_lo[0:rows, u, g * P:(g + 1) * P], vals[0:rows, p, h, :], start=False, stop=True)
                last.then_inc(done, 1)

            def outT(b, p, n, *users):
                wait(pe, (o_ready, oc_ready)[n], b + 1)
                turn(pe, b, *users)
                t.transpose(ro[:, 0:P], otok[:, n, p, :], id32[:, :]).then_inc((oT_psum, ocT_psum)[n], 1)

            def project_out(b, p, n):
                wait(pe, (oT_ready, ocT_ready)[n], b + 1)
                t.matmul(ro[:, P:2 * P], oT[:, n, :], (w_o, wc_o)[n][:, :], start=True,
                         stop=True).then_inc((proj_psum, projc_psum)[n], 1)

            def xnT_of(b, p, n, *users):
                wait(pe, xn_ready[n], b + 1)
                turn(pe, b, *users)
                t.transpose((ro[:, 2 * P:3 * P] if n else pj[:, 3 * D:4 * D]), xn[:, n, p, :],
                            id32[:, :]).then_inc(xnT_psum[n], 1)

            def project_qkv(b, p):
                wait(pe, xnT_ready[0], b + 1)
                t.matmul(pj[:, 0:3 * D], xnT[:, 0, :], w_qkv[:, :], start=True, stop=True).then_inc(qkv_psum, 1)

            def project_q2(b, p):
                wait(pe, xnT_ready[1], b + 1)
                t.matmul(ro[:, 3 * P:4 * P], xnT[:, 1, :], wc_q[:, :], start=True, stop=True).then_inc(q2_psum, 1)

            def router(b, p):
                wait(pe, xnT_ready[2], b + 1)
                t.matmul(ro[:, 3 * P:3 * P + E], xnT[:, 2, :], w_router[:, :], start=True,
                         stop=True).then_inc(logits_psum, 1)

            def ctxT_of(b, p, *users):
                wait(pe, ctx_in_s[p], 8 * b + 16 - 8 * p)
                turn(pe, b, *users)
                t.transpose(pj[:, 3 * D:3 * D + C], ctx_t[0:C, p, :], id32[0:C, 0:C]).then_inc(ctxT_psum, 1)

            def project_kv2(b, p):
                wait(pe, ctxT_ready, b + 1)
                t.matmul(pj[0:C, 0:2 * D], ctxT[:, 0:C], wc_kv[:, :], start=True, stop=True).then_inc(kv2_psum, 1)

            def stack4(to, stk, p, rows, step):
                for g in range(HG):
                    last = t.transpose(st16[:, to + g * step:to + g * step + rows],
                                       stk[0:rows, p, 4 * g:4 * g + 4, :].rearrange("p h s -> p (h s)"),
                                       id16[0:rows, 0:rows])
                return last

            def stacks(b, p, *users):
                wait(pe, qk_lo, b + 1)
                turn(pe, b, *users)
                stack4(0, stQ, p, P, P)
                stack4(4 * P, stK, p, P, P).then_inc(qkT_psum, 1)

            def stack_max(b, p, *users):
                wait(pe, m_ready, b + 1)
                turn(pe, b, *users)
                stack4(0, stQ, p, P, P).then_inc(qmT_psum, 1)

            def stacks2(b, p, *users):
                wait(pe, q2_lo, b + 1)
                wait(pe, k2_lo, b + 1)
                turn(pe, b, *users)
                stack4(0, stQ2, p, P, P)
                stack4(4 * P, stK2, p, C, CP).then_inc(qkT2_psum, 1)

            def stack_max2(b, p, *users):
                wait(pe, cm_ready, b + 1)
                turn(pe, b, *users)
                stack4(0, stQ2, p, P, P).then_inc(qmT2_psum, 1)

            def step(i, p):
                at(i, p, 3, scores_for_max, 0, sc[3], (s2_exp, 4, -1), (c1_max, 4, -9), (s1_max, 4, -1))
                at(i, p, 2, xnT_of, 0, (kv2_read, 1, -2), (qkv_read, 1, 0))
                at(i, p, 6, cross_for_exp, 1, sc[0], (c2_exp, 4, 1), (c1_max, 4, 4), (s1_max, 4, 12))
                at(i, p, 4, values, 0, 3, pv, s2_lo_pool, 1, 1)
                at(i, p, 3, scores_for_max, 1, sc[1], (s2_exp, 4, 0), (s1_max, 4, -2))
                at(i, p, 6, cross_for_exp, 2, sc[2], (s2_exp, 4, 10), (c1_max, 4, 2), (c2_exp, 4, -1))
                at(i, p, 3, scores_for_max, 2, sc[3], (s1_max, 4, 1), (s2_exp, 4, -1), (c1_max, 4, -9))
                at(i, p, 3, scores_for_max, 3, sc[0], (c2_exp, 4, -10), (c1_max, 4, -8), (s1_max, 4, 0))
                at(i, p, 4, outT, 0, (resid2, 1, -2), (q2_ready, 1, 0), (logits_ready, 1, -4), (resid1, 1, 0))
                at(i, p, 5, stacks2, (qkT_ready, 1, 3), (qmT2_ready, 1, 0), (qmT_ready, 1, 2), (qkT2_ready, 1, 0))
                at(i, p, 4, project_out, 0)
                at(i, p, 2, project_qkv)
                at(i, p, 3, stack_max, (qkT2_ready, 1, -1), (qkT_ready, 1, 1), (qmT2_ready, 1, -2), (qmT_ready, 1, 0))
                at(i, p, 6, cross_for_exp, 3, sc[0], (s1_max, 4, 16), (c2_exp, 4, 2), (c1_max, 4, 4))
                at(i, p, 5, cross_for_max, 0, sc[3], (s1_max, 4, 11), (s2_exp, 4, 7), (c1_max, 4, -1))
                at(i, p, 8, xnT_of, 2, (resid1, 1, 5), (resid2, 1, 2), (q2_ready, 1, 4), (logits_ready, 1, 0))
                at(i, p, 6, values, 1, 0, pv, c2_lo, 4, 1, (o_sum, 1, 3), (oc_sum, 1, 0))
                at(i, p, 5, cross_for_max, 1, sc[2], (c2_exp, 4, -1), (s2_exp, 4, 6), (c1_max, 4, -2))
                at(i, p, 3, scores_for_exp, 0, sc[1], (s1_max, 4, 2), (s2_exp, 4, 0))
                at(i, p, 6, values, 1, 1, pv, c2_lo, 4, 2)
                at(i, p, 4, ctxT_of, (qkv_read, 1, 3), (kv2_read, 1, 0))
                at(i, p, 5, cross_for_max, 2, sc[3], (c1_max, 4, 1), (s1_max, 4, 11), (s2_exp, 4, 7))
                at(i, p, 8, router)
                at(i, p, 6, values, 1, 2, pv, c2_lo, 4, 3)
                at(i, p, 5, cross_for_max, 3, sc[0], (c2_exp, 4, 0), (s1_max, 4, 12), (c1_max, 4, 0))
                at(i, p, 4, xnT_of, 1, (logits_ready, 1, -3), (resid1, 1, 1), (resid2, 1, -2), (q2_ready, 1, 0))
                at(i, p, 6, values, 1, 3, pv, c2_lo, 4, 4)
                at(i, p, 3, scores_for_exp, 1, sc[2], (c1_max, 4, -6), (c2_exp, 4, -9), (s2_exp, 4, -2))
                at(i, p, 4, project_q2)
                at(i, p, 3, scores_for_exp, 2, sc[3], (c1_max, 4, -5), (s1_max, 4, 3), (s2_exp, 4, -1))
                at(i, p, 5, stack_max2, (qmT_ready, 1, 3), (qkT2_ready, 1, 1), (qkT_ready, 1, 3), (qmT2_ready, 1, 0))
                at(i, p, 3, values, 0, 0, pv, s2_lo, 3, 1, (oc_sum, 1, -2), (o_sum, 1, 0))
                at(i, p, 3, scores_for_exp, 3, sc[1], (s2_exp, 4, 1), (s1_max, 4, 2))
                at(i, p, 6, outT, 1, (q2_ready, 1, 3), (logits_ready, 1, -1), (resid1, 1, 3), (resid2, 1, 0))
                at(i, p, 2, stacks, (qmT2_ready, 1, -2), (qmT_ready, 1, 0), (qkT2_ready, 1, -2), (qkT_ready, 1, 0))
                at(i, p, 4, project_kv2)
                at(i, p, 5, cross_for_exp, 0, sc[0], (c1_max, 4, 4), (c2_exp, 4, 0), (s1_max, 4, 12))
                at(i, p, 3, values, 0, 1, pv, s2_lo, 3, 2)
                at(i, p, 6, project_out, 1)
                at(i, p, 3, values, 0, 2, pv, s2_lo, 3, 3)
            run(pe, step)

            pe.wait_ge(hot_ready, 1)
            t.matmul(pv[:, 0:NB * E], earlier[:, :], r_hot16, start=True, stop=True)
            t.matmul(st[:, 0:NB * E], ones16[:, :], r_hot16, start=True, stop=True).then_inc(counts_psum, 1)
            pe.wait_ge(w_ffn, 16 * W_FFN)

            def group(n, p, first, last):
                if not last:
                    for c in range(FC):
                        wait(pe, sh_mul, FC * n + c - 1)
                        toks = xn3T[:, bass.ds(4 * n, 4), :].rearrange("p b t -> p (b t)")
                        t.matmul(sc[c % 2][:, :], ws_gate[:, c * P:(c + 1) * P], toks, start=True, stop=True)
                        t.matmul(sc[2 + c % 2][:, :], ws_up[:, c * P:(c + 1) * P], toks, start=True, stop=True).then_inc(sh_gu, 1)
                        if c == 1 and not first:
                            shared_down(n - 1, 1 - p)
                else:
                    shared_down(n - 1, 1 - p)

            def shared_down(n, p):
                wait(pe, sh_mul, FC * n + FC)
                wait(pe, sh_add, n - 1)
                for r in range(4):
                    for c in range(FC):
                        last = t.matmul((ro if p else pj)[:, r * D:(r + 1) * D], hidT[:, p, c, r * P:(r + 1) * P],
                                        ws_down[:, c, :], start=c == 0, stop=c == FC - 1)
                last.then_inc(sh_y, 1)

            def tile(k, p):
                q = 1 - p
                if within(k, 1):
                    e = expert_of(k - 1)
                    wait(pe, tT_ready, k)
                    wait(pe, t_mul, k - 2)
                    t.matmul(sc[q][:, :], xT_tile[:, q, :], w_gate[:, e, :], start=True, stop=True)
                    t.matmul(sc[2 + q][:, :], xT_tile[:, q, :], w_up[:, e, :], start=True, stop=True).then_inc(t_gu, 1)
                if within(k, 0):
                    wait(pe, x_tile_in[p], 8 * k + 16 - 8 * p)
                    wait(pe, tT_ready, k)
                    t.transpose(st[:, 0:P], x_tile[:, p, :], id32[:, :]).then_inc(tT_psum, 1)
                if within(k, 2):
                    wait(pe, t_mul, k - 1)
                    wait(pe, thT_ready, k - 3)
                    for c in range(FC):
                        last = t.transpose((pj if p else pv)[:, c * P:(c + 1) * P], hid[:, p, c * P:(c + 1) * P], id32[:, :])
                    last.then_inc(thT_psum, 1)
                if within(k, 3):
                    e = expert_of(k - 3)
                    wait(pe, thT_ready, k - 2)
                    wait(pe, ty_ready, k - 3)
                    for c in range(FC):
                        last = t.matmul(ro[:, 0:D], hT_tile[:, q, c * P:(c + 1) * P], w_down[:, e, c, :],
                                        start=c == 0, stop=c == FC - 1)
                    last.then_inc(ty_psum, 1)

            def expert_of(k):
                return pe.value_load(owner[0:1, bass.ds(k, 1)], min_val=0, max_val=E - 2)

            run_groups(pe, 0, group)
            pe.wait_ge(route_done, 1)
            pe.wait_ge(w_down_in, 16 * (E - 1))
            pe.wait_ge(sh_add, NG // 2)
            run_tiles(pe, tile)
            pe.wait_ge(ty_ready, NT)
            pe.wait_ge(thT_ready, NT)
            run_groups(pe, NG // 2, group)


def constants(S, NB, E):
    import numpy as np
    half = HD // 2
    freq = (1.0 / np.float32(10000.0) ** (np.arange(half, dtype=np.float32) / np.float32(half))).astype(np.float32)
    ang = np.arange(S, dtype=np.float32)[:, None] * freq[None, :]
    c, s = np.cos(ang), np.sin(ang)
    cos = np.tile(np.concatenate([c, c], 1), (1, H))
    sin = np.tile(np.concatenate([-s, s], 1), (1, H))
    scale = np.float32(float(HD) ** -0.5)
    rows = np.triu(np.full((S, S), -(2.0 ** 100), np.float32), 1)

    def bf16_bits(a):
        return (np.ascontiguousarray(a, np.float32).view(np.uint32) >> 16).astype(np.uint16)

    NT = NB + E - 2
    row = np.concatenate([P * np.arange(NT), np.arange(NT), E - np.arange(E)]).astype(np.float32)
    return {
        "rope_cos": np.concatenate([cos * scale, cos], 1).astype(np.float32),
        "rope_sin": np.concatenate([sin * scale, sin], 1).astype(np.float32),
        "row_consts": np.tile(row, (P, 1)),
        "earlier": np.triu(np.ones((P, P), np.float16), 1),
        "causal_rows": bf16_bits(np.tile(rows, (1, 4))),
        "causal_cols": bf16_bits(np.tile(rows.T, (1, 4))),
        "ident32": np.eye(P, dtype=np.float32),
        "ident16": np.eye(P, dtype=np.float16),
        "identbf": bf16_bits(np.eye(P)),
    }


_INS = (['x', 'ctx_1024']
        + ['L0_attn_' + n for n in ('Wq', 'bq', 'Wk', 'bk', 'Wv', 'bv', 'Wo', 'bo')]
        + ['L0_xattn_' + n for n in ('Wq', 'bq', 'Wk', 'bk', 'Wv', 'bv', 'Wo', 'bo')]
        + ['L0_ffn_' + n for n in ('router_w', 'up_w', 'gate_w', 'down_w',
                                   'shared_up_w', 'shared_gate_w', 'shared_down_w')])


def kernel(**inputs):
    import numpy as _np
    import concourse.bacc as _bacc
    from concourse import mybir as _mybir
    from concourse.bass_utils import run_bass_kernel_spmd as _run

    nc = _bacc.Bacc("TRN2", target_bir_lowering=False, num_devices=1)
    given = {name: _np.ascontiguousarray(inputs[name]) for name in _INS}
    shape = given["x"].shape
    given.update(constants(shape[1], shape[0], given["L0_ffn_router_w"].shape[1]))
    arrays, args = {}, []
    for name, a in given.items():
        arrays[f"in_{name}_dram"] = a
        args.append(nc.dram_tensor(f"in_{name}_dram", a.shape, _mybir.dt.from_np(a.dtype), kind="ExternalInput").ap())
    out = nc.dram_tensor("out_0_dram", shape, _mybir.dt.float32, kind="ExternalOutput").ap()
    decoder_layer(nc, *args, out)
    r = _run(nc, [arrays], core_ids=[0])
    return r.results[0]["out_0_dram"]
```
